# Optimizing a Trainium2 kernel written in Bass

```python
import numpy as np
import jax
import jax.numpy as jnp

def _softmax(x, axis=-1):
    return jax.nn.softmax(x, axis=axis)

def _gelu(x):
    return jax.nn.gelu(x, approximate=True)

def _silu(x):
    return jax.nn.silu(x)

def _sigmoid(x):
    return jax.nn.sigmoid(x)

def _layernorm(x, axis=-1, eps=1e-05):
    m = jnp.mean(x, axis=axis, keepdims=True)
    v = jnp.var(x, axis=axis, keepdims=True)
    return (x - m) / jnp.sqrt(v + eps)

def _scatter_add(tgt, idx, src, axis=0):
    return tgt.at[idx].add(src)

def _segment_sum(src, seg, n):
    return jax.ops.segment_sum(src, seg, n)
kernel_name = 'mk_gnn_ffn_d2_gnn_r8_ae6ecd'

def setup_inputs(seed: int=0):
    np.random.seed(seed)
    _w = jnp.asarray

    def _rec_inputs():
        import jax
        import jax.numpy as jnp
        _gk = jax.random.key(seed)
        x = -0.0002928 + 1 * jax.random.normal(jax.random.fold_in(_gk, 1), (1024, 512), jnp.float32)
        src = jax.random.randint(jax.random.fold_in(_gk, 2), (16384,), 0, 1024, jnp.int32)
        dst = jax.random.randint(jax.random.fold_in(_gk, 3), (16384,), 0, 1024, jnp.int32)
        _o = jnp.argsort(dst, stable=True)
        src = src[_o]
        dst = dst[_o]
        return (x, src, dst)
    x, src, dst = _rec_inputs()

    def _L0_gnn_setup():
        import jax, jax.numpy as jnp
        import numpy as np
        N = 1024
        D = 512
        E = 32768
        STEPS = 3
        key = jax.random.key(seed)
        k1, k2, k3 = jax.random.split(key, 3)
        x = jax.random.normal(k1, (N, D), dtype=jnp.float32)
        edge_index = jax.random.randint(k2, (2, E), 0, N, dtype=jnp.int32)
        W = jax.random.normal(k3, (D, D), dtype=jnp.float32) / np.sqrt(D)
        b = jnp.zeros((D,), dtype=jnp.float32)
        diffusion_weights = jnp.ones((STEPS + 1,), dtype=jnp.float32) / (STEPS + 1)
        return {'x': x, 'edge_index': edge_index, 'W': W, 'b': b, 'diffusion_weights': diffusion_weights}
    _L0_gnn_all = _L0_gnn_setup()
    _L0_gnn_in = {k: v for k, v in _L0_gnn_all.items() if k in ('W', 'b', 'diffusion_weights')}
    del _L0_gnn_all

    def _L0_ffn_setup():
        import jax, jax.numpy as jnp
        import numpy as np
        TOP_K = 6
        CAP_FACTOR = 2.0
        key = jax.random.key(seed)
        ks = jax.random.split(key, 9)
        B, S, D, F, E, SH = (4, 256, 512, 256, 64, 2)
        return {'x': jax.random.normal(ks[0], (B, S, D), jnp.float32), 'router_w': jax.random.normal(ks[1], (E, D), jnp.float32) * 0.02, 'bias': jnp.zeros((E,), jnp.float32), 'shared_w_gate': jax.random.normal(ks[2], (SH, F, D), jnp.float32) * 0.02, 'shared_w_up': jax.random.normal(ks[3], (SH, F, D), jnp.float32) * 0.02, 'shared_w_down': jax.random.normal(ks[4], (SH, D, F), jnp.float32) * 0.02, 'w_gate': jax.random.normal(ks[5], (E, F, D), jnp.float32) * 0.02, 'w_up': jax.random.normal(ks[6], (E, F, D), jnp.float32) * 0.02, 'w_down': jax.random.normal(ks[7], (E, D, F), jnp.float32) * 0.02}
    _L0_ffn_all = _L0_ffn_setup()
    _L0_ffn_in = {k: v for k, v in _L0_ffn_all.items() if k in ('router_w', 'bias', 'shared_w_gate', 'shared_w_up', 'shared_w_down', 'w_gate', 'w_up', 'w_down')}
    del _L0_ffn_all

    def _L1_gnn_setup():
        import jax, jax.numpy as jnp
        import numpy as np
        N = 6250
        IN_CH = 512
        OUT_CH = 512
        DEG = 32
        E = N * DEG
        key = jax.random.key(seed)
        kx, kwc, kwn, kb, ke = jax.random.split(key, 5)
        x = jax.random.normal(kx, (N, IN_CH), dtype=jnp.float32)
        bound = 1.0 / np.sqrt(IN_CH)
        wc = jax.random.uniform(kwc, (IN_CH, OUT_CH), minval=-bound, maxval=bound, dtype=jnp.float32)
        wn = jax.random.uniform(kwn, (IN_CH, OUT_CH), minval=-bound, maxval=bound, dtype=jnp.float32)
        bias = jax.random.uniform(kb, (OUT_CH,), minval=-bound, maxval=bound, dtype=jnp.float32)
        src = jnp.repeat(jnp.arange(N, dtype=jnp.int64), DEG)
        dst = jax.random.randint(ke, (E,), 0, N, dtype=jnp.int64)
        edge_index = jnp.stack([src, dst], axis=0)
        return {'x': x, 'wc': wc, 'wn': wn, 'bias': bias, 'edge_index': edge_index}
    _L1_gnn_all = _L1_gnn_setup()
    _L1_gnn_in = {k: v for k, v in _L1_gnn_all.items() if k in ('wc', 'wn', 'bias')}
    del _L1_gnn_all

    def _L1_ffn_setup():
        import jax, jax.numpy as jnp
        import numpy as np
        E = 8
        K = 1
        D = 512
        I = 256
        B, T = (2, 256)
        key = jax.random.key(seed)
        ks = jax.random.split(key, 7)
        s = 0.02
        x = jax.random.normal(ks[0], (B, T, D), jnp.float32)
        gate_w = jax.random.normal(ks[1], (E, D), jnp.float32) * s
        w1 = jax.random.normal(ks[2], (E, I, D), jnp.float32) * s
        w2 = jax.random.normal(ks[3], (E, D, I), jnp.float32) * s
        w3 = jax.random.normal(ks[4], (E, I, D), jnp.float32) * s
        sw1 = jax.random.normal(ks[5], (I, D), jnp.float32) * s
        sw2 = jax.random.normal(ks[6], (D, I), jnp.float32) * s
        return {'x': x, 'gate_w': gate_w, 'w1': w1, 'w2': w2, 'w3': w3, 'sw1': sw1, 'sw2': sw2}
    _L1_ffn_all = _L1_ffn_setup()
    _L1_ffn_in = {k: v for k, v in _L1_ffn_all.items() if k in ('gate_w', 'w1', 'w2', 'w3', 'sw1', 'sw2')}
    del _L1_ffn_all
    return {'x': x, 'src': src, 'dst': dst, 'L0_gnn_W': _L0_gnn_in['W'], 'L0_gnn_b': _L0_gnn_in['b'], 'L0_gnn_diffusion_weights': _L0_gnn_in['diffusion_weights'], 'L0_ffn_router_w': _L0_ffn_in['router_w'], 'L0_ffn_bias': _L0_ffn_in['bias'], 'L0_ffn_shared_w_gate': _L0_ffn_in['shared_w_gate'], 'L0_ffn_shared_w_up': _L0_ffn_in['shared_w_up'], 'L0_ffn_shared_w_down': _L0_ffn_in['shared_w_down'], 'L0_ffn_w_gate': _L0_ffn_in['w_gate'], 'L0_ffn_w_up': _L0_ffn_in['w_up'], 'L0_ffn_w_down': _L0_ffn_in['w_down'], 'L1_gnn_wc': _L1_gnn_in['wc'], 'L1_gnn_wn': _L1_gnn_in['wn'], 'L1_gnn_bias': _L1_gnn_in['bias'], 'L1_ffn_gate_w': _L1_ffn_in['gate_w'], 'L1_ffn_w1': _L1_ffn_in['w1'], 'L1_ffn_w2': _L1_ffn_in['w2'], 'L1_ffn_w3': _L1_ffn_in['w3'], 'L1_ffn_sw1': _L1_ffn_in['sw1'], 'L1_ffn_sw2': _L1_ffn_in['sw2']}

def reference(x, src, dst, L0_gnn_W, L0_gnn_b, L0_gnn_diffusion_weights, L0_ffn_router_w, L0_ffn_bias, L0_ffn_shared_w_gate, L0_ffn_shared_w_up, L0_ffn_shared_w_down, L0_ffn_w_gate, L0_ffn_w_up, L0_ffn_w_down, L1_gnn_wc, L1_gnn_wn, L1_gnn_bias, L1_ffn_gate_w, L1_ffn_w1, L1_ffn_w2, L1_ffn_w3, L1_ffn_sw1, L1_ffn_sw2):
    import jax
    import jax.numpy as jnp

    def _L0_gnn_ref(x, edge_index, W, b, diffusion_weights):
        import jax, jax.numpy as jnp
        import numpy as np
        N = 1024
        D = 512
        E = 32768
        STEPS = 3
        h = x @ W + b
        row, col = (edge_index[0], edge_index[1])
        adj = jnp.zeros((N, N), dtype=h.dtype)
        adj = adj.at[row, col].set(1.0)
        adj = adj.at[col, row].set(1.0)
        adj = adj + jnp.eye(N, dtype=h.dtype)
        row_sum = adj.sum(axis=1, keepdims=True)
        adj = adj / jnp.maximum(row_sum, 1.0)
        out = diffusion_weights[0] * h
        cur = h
        for i in range(STEPS):
            cur = adj @ cur
            out = out + diffusion_weights[i + 1] * cur
        return jax.nn.relu(out)

    def _L0_ffn_ref(x, router_w, bias, shared_w_gate, shared_w_up, shared_w_down, w_gate, w_up, w_down):
        import jax, jax.numpy as jnp
        import numpy as np
        TOP_K = 6
        CAP_FACTOR = 2.0
        B, S, D = x.shape
        E = router_w.shape[0]
        K = TOP_K
        N = B * S
        C = max(1, int(N * K * CAP_FACTOR / E))
        router_logits = jnp.einsum('bsd,ed->bse', x, router_w) + bias
        hg = jnp.einsum('bsd,efd->bsef', x, shared_w_gate)
        hu = jnp.einsum('bsd,efd->bsef', x, shared_w_up)
        shared_out = jnp.einsum('bsef,edf->bsd', jax.nn.silu(hg) * hu, shared_w_down)
        shared_out = shared_out / shared_w_gate.shape[0]
        router_probs = jax.nn.softmax(router_logits, axis=-1)
        topk_p, topk_i = jax.lax.top_k(router_probs, K)
        topk_p = topk_p / (jnp.sum(topk_p, axis=-1, keepdims=True) + 1e-09)
        x_flat = x.reshape(N, D)
        flat_e = topk_i.reshape(-1)
        flat_g = topk_p.reshape(-1)
        token_ids = jnp.repeat(jnp.arange(N), K)
        order = jnp.argsort(flat_e)
        se = flat_e[order]
        st = token_ids[order]
        sg = flat_g[order]
        M = se.shape[0]
        pos = jnp.arange(M)
        is_first = jnp.concatenate([jnp.ones((1,), bool), se[1:] != se[:-1]])
        group_starts = jax.lax.cummax(pos * is_first.astype(pos.dtype))
        slot = pos - group_starts
        valid = slot < C
        safe_slot = jnp.where(valid, slot, C)
        expert_in = jnp.zeros((E, C + 1, D), x.dtype).at[se, safe_slot].set(x_flat[st])
        expert_gate = jnp.zeros((E, C + 1), x.dtype).at[se, safe_slot].set(sg)
        expert_tok = jnp.full((E, C + 1), N, jnp.int32).at[se, safe_slot].set(st.astype(jnp.int32))
        expert_mask = jnp.zeros((E, C + 1), bool).at[se, safe_slot].set(valid)
        expert_in = expert_in[:, :C]
        expert_gate = expert_gate[:, :C]
        expert_tok = expert_tok[:, :C]
        expert_mask = expert_mask[:, :C]
        hg = jnp.einsum('ecd,efd->ecf', expert_in, w_gate)
        hu = jnp.einsum('ecd,efd->ecf', expert_in, w_up)
        expert_out = jnp.einsum('ecf,edf->ecd', jax.nn.silu(hg) * hu, w_down)
        fm = expert_mask.reshape(-1)
        dst = jnp.where(fm, expert_tok.reshape(-1), N)
        fg = jnp.where(fm, expert_gate.reshape(-1), jnp.zeros((), x.dtype))
        sparse = jax.ops.segment_sum(fg[:, None] * expert_out.reshape(-1, D), dst, num_segments=N + 1)[:N]
        return shared_out + sparse.reshape(B, S, D)

    def _L1_gnn_ref(x, wc, wn, bias, edge_index):
        import jax, jax.numpy as jnp
        import numpy as np
        N = 6250
        IN_CH = 512
        OUT_CH = 512
        DEG = 32
        E = N * DEG
        alpha = x @ wc
        beta = x @ wn
        src, dst = (edge_index[0], edge_index[1])
        sums = jax.ops.segment_sum(beta[dst], src, num_segments=x.shape[0])
        counts = jax.ops.segment_sum(jnp.ones_like(src, dtype=beta.dtype), src, num_segments=x.shape[0])
        gamma = sums / counts[:, None]
        return alpha + gamma + bias

    def _L1_ffn_ref(x, gate_w, w1, w2, w3, sw1, sw2):
        import jax, jax.numpy as jnp
        import numpy as np
        E = 8
        K = 1
        D = 512
        I = 256
        B, T = (2, 256)
        xf = x.reshape(-1, D)
        logits = xf @ gate_w.T
        wts, idx = jax.lax.top_k(logits, K)
        wts = jax.nn.softmax(wts, axis=-1)
        comb = jnp.einsum('nke,nk->ne', jax.nn.one_hot(idx, E, dtype=xf.dtype), wts)
        h = jax.nn.silu(jnp.einsum('nd,eid->nei', xf, w1)) * jnp.einsum('nd,eid->nei', xf, w3)
        y = jnp.einsum('nei,edi->nd', h * comb[:, :, None], w2)
        y = y + jax.nn.gelu(xf @ sw1.T, approximate=False) @ sw2.T
        return y.reshape(x.shape)
    edge_index = jnp.stack([src, dst])
    x = x + _L0_gnn_ref(_layernorm(x, axis=-1), edge_index, L0_gnn_W, L0_gnn_b, L0_gnn_diffusion_weights)
    x = x + _L0_ffn_ref(_layernorm(x, axis=-1)[None], L0_ffn_router_w, L0_ffn_bias, L0_ffn_shared_w_gate, L0_ffn_shared_w_up, L0_ffn_shared_w_down, L0_ffn_w_gate, L0_ffn_w_up, L0_ffn_w_down)[0]
    x = x + _L1_gnn_ref(_layernorm(x, axis=-1), L1_gnn_wc, L1_gnn_wn, L1_gnn_bias, edge_index)
    x = x + _L1_ffn_ref(_layernorm(x, axis=-1)[None], L1_ffn_gate_w, L1_ffn_w1, L1_ffn_w2, L1_ffn_w3, L1_ffn_sw1, L1_ffn_sw2)[0]
    return x

_drawn_inputs = setup_inputs


def setup_inputs(seed=0):
    import zlib

    import numpy as np

    out = dict(_drawn_inputs(seed))
    spreads = {'L0_gnn_b': (0.0, 0.1), 'L0_gnn_diffusion_weights': (0.25, 0.6), 'L0_ffn_bias': (0.0, 0.8)}
    factors = {'L0_ffn_router_w': 3.813,
     'L0_ffn_w_gate': 3.491,
     'L0_ffn_w_up': 3.464,
     'L0_ffn_w_down': 3.475,
     'L1_gnn_bias': 2.746,
     'L0_ffn_shared_w_gate': 3.203,
     'L0_ffn_shared_w_up': 3.122,
     'L0_ffn_shared_w_down': 3.119,
     'L1_ffn_gate_w': 8.375,
     'L1_ffn_w1': 2.953,
     'L1_ffn_w2': 2.911,
     'L1_ffn_w3': 2.91}
    for name, (base, spread) in spreads.items():
        noise = np.random.default_rng([zlib.crc32(name.encode()), seed]).standard_normal(out[name].shape)
        drawn = base * np.exp(spread * noise) if base else spread * noise
        out[name] = jnp.asarray(drawn.astype(out[name].dtype))
    for name, factor in factors.items():
        out[name] = (out[name] * factor).astype(out[name].dtype)
    return out
```

```python
from contextlib import ExitStack

import concourse.bass as bass
from concourse import mybir

ALU = mybir.AluOpType
ACT = mybir.ActivationFunctionType
F32 = mybir.dt.float32
F16 = mybir.dt.float16
BF16 = mybir.dt.bfloat16
I32 = mybir.dt.int32
U32 = mybir.dt.uint32
X = mybir.AxisListType.X

P = 128
N = 1024
D = 512
NT = N // P
KD = D // P
NE = 16384
EC = NE // P
STEPS = 3
E0 = 64
TOP = 6
CAP = N * TOP * 2 // E0
CB = CAP - P
SLOTS = E0 * CAP
F = 256
KF = F // P
GU = 2 * KD * F
WROW = GU + KF * D
SH = 2
E1 = 8
T1 = N // P + E1 - 1
EPS = 1e-5
FAR = float(1 << 20)


def build(nc, x, edges, w0, b0, dw, rwT, rbias, sgT, suT, sdT, we0, wc, wn, b1, gwT, we1, sw1T, sw2T, out):
    xn_dram = nc.dram_tensor("xn_dram", [N, D], F32, kind="Internal").ap()
    slot_token = nc.dram_tensor("slot_token", [SLOTS, 1], F32, kind="Internal").ap()
    slot_out = nc.dram_tensor("slot_out", [SLOTS, D], F32, kind="Internal").ap()
    sorted_in = nc.dram_tensor("sorted_in", [T1 * P, D], F32, kind="Internal").ap()
    sorted_out = nc.dram_tensor("sorted_out", [T1 * P, D], F32, kind="Internal").ap()

    with ExitStack() as ctx:
        def sb(name, shape, dt=F32):
            return ctx.enter_context(nc.sbuf_tensor(name, shape, dt))

        def sem(name):
            return ctx.enter_context(nc.semaphore(name))

        ps = ctx.enter_context(nc.psum_tensor("ps", [P, 8, 512], F32))

        xres = sb("xres", [P, NT, D])
        xn = sb("xn", [P, NT, D])
        xnT = sb("xnT", [P, KD, N])
        mT = sb("mT", [P, NT, N])
        ring = sb("ring", [P, 2, WROW])
        zone = sb("zone", [P, 20480])
        ident = sb("ident", [P, P])
        tri = sb("tri", [P, P], BF16)
        ones = sb("ones", [P, P], BF16)
        iota = sb("iota", [P, N], F16)
        segs = sb("segs", [P, NT * E0], BF16)
        segs8 = sb("segs8", [P, NT * E1], BF16)
        edge_i = sb("edge_i", [P, 2, EC], I32)
        edge_f = sb("edge_f", [P, 2, EC])
        b0b = sb("b0b", [P, D])
        b1b = sb("b1b", [P, D])
        dwb = sb("dwb", [P, STEPS + 1])
        rb = sb("rb", [P, E0])
        rw = sb("rw", [P, KD, E0])
        gw = sb("gw", [P, KD, E1])
        stats = sb("stats", [P, NT, 6])
        mv = sb("mv", [P, NT, 2])
        rstd = sb("rstd", [P, NT])
        rsum = sb("rsum", [P, NT])
        cnt = sb("cnt", [P, NT])
        wr = sb("wr", [P, STEPS, NT])
        red = sb("red", [P, 6, NT])
        top8 = sb("top8", [P, NT, 8])
        tokf = sb("tokf", [P, NT])
        ebase = sb("ebase", [P, E0])
        dk = sb("dk", [P, TOP, NT])
        dki = sb("dki", [P, TOP, NT], U32)
        gk = sb("gk", [P, TOP, NT])
        gki = sb("gki", [P, TOP, NT], U32)
        idxA = sb("idxA", [P, E0], U32)
        idxB = sb("idxB", [CB, E0], U32)
        colA = sb("colA", [P, 2], U32)
        colB = sb("colB", [CB, 2], U32)
        t1row = sb("t1row", [P, 4, 16])
        t1e = sb("t1e", [1, 16], I32)
        d1 = sb("d1", [P, NT])
        d1i = sb("d1i", [P, NT], U32)

        S = zone[:, 0:8192].rearrange("p (a n) -> p a n", a=NT)
        cur = zone[:, 8192:16384].rearrange("p (b i n) -> p b i n", b=2, i=NT)
        ohd = zone[:, 16384:17408].bitcast(BF16).rearrange("p (b n) -> p b n", b=2)
        ohs = zone[:, 17408:17920].bitcast(BF16).rearrange("p (b n) -> p b n", b=2)
        mrow = zone[:, 17920:19968].rearrange("p (b n) -> p b n", b=2)
        w0s = ring[:, 0, 0:KD * D].rearrange("p (k n) -> p k n", k=KD)
        sact = zone[:, 0:4096].rearrange("p (f n) -> p f n", f=4)
        sd = zone[:, 4096:6144].rearrange("p (k n) -> p k n", k=4)
        sg = zone[:, 6144:8192].rearrange("p (k n) -> p k n", k=KD)
        su = zone[:, 8192:10240].rearrange("p (k n) -> p k n", k=KD)
        xg = zone[:, 10240:12288].rearrange("p (b n) -> p b n", b=2)
        xT = zone[:, 12288:13824].rearrange("p (b n) -> p b n", b=2)
        sil = zone[:, 13824:14592].rearrange("p (b n) -> p b n", b=2)
        act = zone[:, 14592:15360].rearrange("p (b f n) -> p b f n", b=2, f=KF)
        ob = zone[:, 15360:17408].rearrange("p (b n) -> p b n", b=2)
        gat = zone[:, 17408:19456].rearrange("p (b n) -> p b n", b=4)
        utmp = zone[:, 19456:20480].rearrange("p (b n) -> p b n", b=2)
        def table(j):
            return zone[:, 15360 + 512 * j:15872 + 512 * j]
        def by_e(t):
            return t.rearrange("p (i e) -> p i e", e=E0)
        prob, sel, csel, dest, gate, tmp, rank_t = [table(j) for j in range(7)]
        selb = table(7)[:, 0:256].bitcast(BF16)
        tki = table(7)[0:E0, 256:256 + CAP]
        beta = zone[:, 0:4096].rearrange("p (i n) -> p i n", i=NT)
        wns = sg
        wcs = su
        s1w = zone[:, 4096:5120].rearrange("p (k n) -> p k n", k=KD)
        s2w = zone[:, 5120:6144].rearrange("p (k n) -> p k n", k=KF)
        gact = zone[:, 0:2048].rearrange("p (f n) -> p f n", f=KF)

        ld_x, ld_edge, ld_w0, ld_bc, ld_small = [sem(f"ld_{n}") for n in ("x", "edge", "w0", "bc", "small")]
        ld_shared, ld_c, ld_s1 = [sem(f"ld_{n}") for n in ("shared", "c", "s1")]
        const_ready = sem("const_ready")
        pool_step = sem("pool_step")
        zero_ready, zeroed = sem("zero_ready"), sem("zeroed")
        dve_step, edgef_ready = sem("dve_step"), sem("edgef_ready")
        xn_ready, tr_done, tr_evac = sem("xn_ready"), sem("tr_done"), sem("tr_evac")
        var_ready, std_ready = sem("var_ready"), sem("std_ready")
        h_done, h_evac = sem("h_done"), sem("h_evac")
        oh_ready, oh_used = sem("oh_ready"), sem("oh_used")
        m_done, m_evac_a, m_evac_v = sem("m_done"), sem("m_evac_a"), sem("m_evac_v")
        mt_done, mrow_ready, mrow_used, s_ready, rs_ready = [sem(n) for n in ("mt_done", "mrow_ready", "mrow_used", "s_ready", "rs_ready")]
        s_done, s_evac = sem("s_done"), sem("s_evac")
        zone_free = sem("zone_free")
        xn_stored = sem("xn_stored")
        lg_done, lgc_ready, ex_ready, sel_ready, rank_done = [sem(n) for n in ("lg_done", "lgc_ready", "ex_ready", "sel_ready", "rank_done")]
        sh_done, sh_sil, sh_u, sh_act, shd_done, shd_evac = [sem(n) for n in ("sh_done", "sh_sil", "sh_u", "sh_act", "shd_done", "shd_evac")]
        dki_ready, scattered, tki_loaded, tki_tr, idx_ready = [sem(n) for n in ("dki_ready", "scattered", "tki_loaded", "tki_tr", "idx_ready")]
        col_ready, gather_go = sem("col_ready"), sem("gather_go")
        xg_ready = [sem(f"xg_ready{u}") for u in range(2)]
        wgu_ready = [sem(f"wgu_ready{u}") for u in range(2)]
        wd_ready = [sem(f"wd_ready{u}") for u in range(2)]
        xt_done, xt_evac = sem("xt_done"), sem("xt_evac")
        gu_done, sil_ready, act_ready = sem("gu_done"), sem("sil_ready"), sem("act_ready")
        dn_done, oa_ready, obb_ready = sem("dn_done"), sem("oa_ready"), sem("obb_ready")
        o_stored = [sem(f"o_stored{u}") for u in range(2)]
        gat_ready = [sem(f"gat_ready{u}") for u in range(4)]
        gat_used = sem("gat_used")
        be_done, be_evac, al_done, al_evac, ga_done, ga_evac = [sem(n) for n in ("be_done", "be_evac", "al_done", "al_evac", "ga_done", "ga_evac")]
        lg1_done, sel1_ready, rank1_done, t1_ready, d1i_ready = [sem(n) for n in ("lg1_done", "sel1_ready", "rank1_done", "t1_ready", "d1i_ready")]
        s1_done, s1_act, s2_done, s2_evac = [sem(n) for n in ("s1_done", "s1_act", "s2_done", "s2_evac")]
        scattered1, x1_ready, w1_ready = sem("scattered1"), [sem(f"x1_ready{u}") for u in range(2)], [sem(f"w1_ready{u}") for u in range(2)]
        y1_evac, y1_stored = sem("y1_evac"), [sem(f"y1_stored{u}") for u in range(2)]
        x1t_done, x1t_evac, h1_done, g1_ready, a1_ready, a1t_done, a1t_evac, y1_done = [
            sem(n) for n in ("x1t_done", "x1t_evac", "h1_done", "g1_ready", "a1_ready", "a1t_done", "a1t_evac", "y1_done")]
        out_ready, out_done = sem("out_ready"), sem("out_done")

        rows = lambda t: t.rearrange("(i p) d -> p i d", p=P)
        xn_rows = rows(xn_dram)

        block = ctx.enter_context(nc.Block())

        @block.sync
        def _(sp):
            sp.dma_start(xres[:], rows(x)).then_inc(ld_x, 16)
            sp.dma_start(edge_i[:], edges.rearrange("p (t c) -> p t c", t=2)).then_inc(ld_edge, 16)
            sp.dma_start(w0s, w0.rearrange("(k p) n -> p k n", p=P)).then_inc(ld_w0, 16)
            sp.dma_start(rw[:], rwT.rearrange("(k p) n -> p k n", p=P)).then_inc(ld_small, 16)
            sp.dma_start(gw[:], gwT.rearrange("(k p) n -> p k n", p=P)).then_inc(ld_small, 16)
            sp.dma_start(b0b[:], b0.partition_broadcast(P)).then_inc(ld_bc, 16)
            sp.dma_start(b1b[:], b1.partition_broadcast(P)).then_inc(ld_bc, 16)
            sp.dma_start(dwb[:], dw.partition_broadcast(P)).then_inc(ld_bc, 16)
            sp.dma_start(rb[:], rbias.partition_broadcast(P)).then_inc(ld_bc, 16)
            sp.wait_ge(zero_ready, 1)
            sp.dma_start(slot_token.rearrange("(p c) o -> p (c o)", p=P), mrow[:, 0, 0:SLOTS // P]).then_inc(zeroed, 16)
            for t in range(T1):
                sp.dma_start(sorted_in[t * P:(t + 1) * P, :], mrow[:, 0, 0:D]).then_inc(zeroed, 16)
            sp.wait_ge(h_done, NT)
            for u in range(2):
                sp.dma_start(ring[:, u, 0:GU], we0[u, :, 0:GU]).then_inc(wgu_ready[u], 16)
                sp.dma_start(ring[:, u, GU:WROW], we0[u, :, GU:WROW]).then_inc(wd_ready[u], 16)
            sp.wait_ge(s_done, STEPS * NT)
            sp.wait_ge(s_evac, STEPS * NT)
            sp.dma_start(sg, sgT.rearrange("(k p) n -> p k n", p=P)).then_inc(ld_shared, 16)
            sp.dma_start(su, suT.rearrange("(k p) n -> p k n", p=P)).then_inc(ld_shared, 16)
            sp.dma_start(sd, sdT.rearrange("(k p) n -> p k n", p=P)).then_inc(ld_shared, 16)
            sp.wait_ge(xn_ready, 2 * NT)
            sp.dma_start(xn_rows, xn[:]).then_inc(xn_stored, 16)
            sp.wait_ge(scattered, 16 * TOP * NT)
            sp.wait_ge(sel_ready, 1)
            sp.wait_ge(rank_done, 1)
            sp.dma_start(tki, slot_token.rearrange("(e c) o -> e (c o)", e=E0)).then_inc(tki_loaded, 16)
            with sp.Fori(0, E0 // 2 - 1) as g:
                e = g * 2
                for u in range(2):
                    nxt = we0[bass.ds(e + u + 2, 1)].rearrange("o p n -> p (o n)")
                    sp.wait_ge(gu_done, e + u + 1)
                    sp.dma_start(ring[:, u, 0:GU], nxt[:, 0:GU]).then_inc(wgu_ready[u], 16)
                    sp.wait_ge(dn_done, e + u + 1)
                    sp.dma_start(ring[:, u, GU:WROW], nxt[:, GU:WROW]).then_inc(wd_ready[u], 16)
            sp.wait_ge(sh_done, 2 * 4)
            sp.dma_start(wns, wn.rearrange("(k p) n -> p k n", p=P)).then_inc(ld_c, 16)
            sp.dma_start(wcs, wc.rearrange("(k p) n -> p k n", p=P)).then_inc(ld_c, 16)
            sp.wait_ge(shd_done, NT)
            sp.dma_start(s1w, sw1T.rearrange("(k p) n -> p k n", p=P)).then_inc(ld_s1, 16)
            sp.dma_start(s2w, sw2T.rearrange("(k p) n -> p k n", p=P)).then_inc(ld_s1, 16)
            sp.wait_ge(dn_done, E0)
            sp.wait_ge(t1_ready, 1)
            sp.wait_ge(scattered1, 16 * NT)
            for t in range(T1):
                if t >= 2:
                    sp.wait_ge(y1_done, t - 1)
                ex = sp.value_load(t1e[0:1, t:t + 1], min_val=0, max_val=E1 - 1)
                sp.dma_start(ring[:, t % 2, :], we1[bass.ds(ex, 1)].rearrange("o p n -> p (o n)")).then_inc(w1_ready[t % 2], 16)
                sp.dma_start(xg[:, t % 2, 0:D], sorted_in[t * P:(t + 1) * P, :]).then_inc(x1_ready[t % 2], 16)
            for i in range(NT):
                sp.wait_ge(out_ready, i + 1)
                sp.dma_start(out[i * P:(i + 1) * P, :], xres[:, i, :]).then_inc(out_done, 16)
            sp.wait_ge(out_done, 16 * NT)

        @block.gpsimd
        def _(pool):
            steps = [0]

            def link(ins):
                steps[0] += 1
                ins.then_inc(pool_step, 1)
                pool.wait_ge(pool_step, steps[0])

            pool.memset(mrow[:, 0, :], 0.0).then_inc(zero_ready, 1)
            link(pool.iota(iota[:], pattern=[[1, N]], base=0, channel_multiplier=0, allow_small_or_imprecise_dtypes=True))
            pool.iota(tokf[:], pattern=[[P, NT]], base=0, channel_multiplier=1, allow_small_or_imprecise_dtypes=True)
            pool.iota(ebase[:], pattern=[[CAP, E0]], base=0, channel_multiplier=0, allow_small_or_imprecise_dtypes=True)
            pool.iota(t1row[:, 3, :], pattern=[[1, 16]], base=0, channel_multiplier=0, allow_small_or_imprecise_dtypes=True)
            pool.memset(ones[:], 1.0)
            pool.memset(tri[:], 1.0)
            pool.memset(segs[:], 1.0)
            pool.memset(segs8[:], 1.0)
            link(pool.memset(ident[:], 0.0))
            pool.affine_select(out=ident[:], in_=ident[:], compare_op=ALU.not_equal, fill=1.0, base=0, pattern=[[-1, P]], channel_multiplier=1)
            pool.affine_select(out=tri[:], in_=tri[:], compare_op=ALU.is_ge, fill=0.0, base=-1, pattern=[[1, P]], channel_multiplier=-1)
            pool.memset(segs[:].rearrange("p (i e) -> p i e", e=E0)[:, :, 0:1], 0.0)
            pool.memset(segs8[:].rearrange("p (i e) -> p i e", e=E1)[:, :, 0:1], 0.0).then_inc(const_ready, 1)

            def shared_mul(j):
                pool.wait_ge(sh_u, j + 1)
                f, h = j % 4, j // 4
                blk = sact[:, f, h * 512:(h + 1) * 512]
                pool.tensor_tensor(blk, blk, utmp[:, j % 2, :], ALU.mult).then_inc(sh_act, 1)

            for j in range(4):
                shared_mul(j)
            pool.wait_ge(zeroed, 16 * (T1 + 1))
            for k in range(TOP):
                pool.wait_ge(dki_ready, k + 1)
                for i in range(NT):
                    pool.indirect_dma_start(slot_token, bass.IndirectOffsetOnAxis(dki[:, k, i:i + 1], 0), tokf[:, i:i + 1], None,
                                            bounds_check=SLOTS - 1, oob_is_err=False).then_inc(scattered, 16)
                if k < 4:
                    shared_mul(4 + k)
            pool.wait_ge(xn_stored, 16)
            pool.wait_ge(idx_ready, 1)

            def gather(u, e):
                pool.tensor_copy(colA[:, u:u + 1], idxA[:, bass.ds(e, 1)]).then_inc(col_ready, 1)
                pool.tensor_copy(colB[:, u:u + 1], idxB[:, bass.ds(e, 1)]).then_inc(col_ready, 1)
                pool.wait_ge(col_ready, (e + 1) * 2)
                pool.sem_inc(gather_go, 1)
                pool.indirect_dma_start(xg[:, u, 0:D], None, xn_dram, bass.IndirectOffsetOnAxis(colA[:, u:u + 1], 0)).then_inc(xg_ready[u], 16)
                pool.indirect_dma_start(xg[0:CB, u, D:2 * D], None, xn_dram, bass.IndirectOffsetOnAxis(colB[:, u:u + 1], 0)).then_inc(xg_ready[u], 16)

            gather(0, 0)
            gather(1, 1)
            with pool.Fori(1, E0 // 2) as g:
                e = g * 2
                for u in range(2):
                    pool.wait_ge(xt_done, e + u - 1)
                    gather(u, e + u)

            for u in range(2):
                pool.wait_ge(o_stored[u], 32 * (E0 // 2))
            for j in range(NT * TOP):
                i, k = j // TOP, j % TOP
                if j >= 4:
                    pool.wait_ge(gat_used, j - 3)
                pool.indirect_dma_start(gat[:, j % 4, :], None, slot_out, bass.IndirectOffsetOnAxis(gki[:, k, i:i + 1], 0),
                                        bounds_check=SLOTS - 1, oob_is_err=False).then_inc(gat_ready[j % 4], 16)

            pool.wait_ge(d1i_ready, 1)
            for i in range(NT):
                pool.indirect_dma_start(sorted_in, bass.IndirectOffsetOnAxis(d1i[:, i:i + 1], 0), xn[:, i, :], None,
                                        bounds_check=T1 * P - 1, oob_is_err=False).then_inc(scattered1, 16)
            for u in range(2):
                pool.wait_ge(y1_stored[u], 16 * ((T1 + 1 - u) // 2))
            for i in range(NT):
                j = NT * TOP + i
                pool.wait_ge(gat_used, j - 3)
                pool.indirect_dma_start(gat[:, j % 4, :], None, sorted_out, bass.IndirectOffsetOnAxis(d1i[:, i:i + 1], 0),
                                        bounds_check=T1 * P - 1, oob_is_err=False).then_inc(gat_ready[j % 4], 16)

        @block.scalar
        def _(sc):
            def copy(o, i):
                return nc.scalar.activation(o, i, ACT.Copy)

            def root(ln):
                sc.wait_ge(var_ready, ln + 1)
                nc.scalar.activation(rstd[:], rstd[:], ACT.Sqrt).then_inc(std_ready, 1)

            def evac_transposes(ln):
                root(ln)
                for i in range(NT):
                    sc.wait_ge(tr_done, NT * ln + i + 1)
                    copy(xnT[:, :, i * P:(i + 1) * P], ps[:, i % 2, :].rearrange("p (k n) -> p k n", k=KD)).then_inc(tr_evac, 1)

            evac_transposes(0)
            for h in range(2):
                sc.wait_ge(m_done, h + 1)
                for b in range(0, NT, 2):
                    copy(mT[:, b, h * 512:(h + 1) * 512], ps[:, b, :]).then_inc(m_evac_a, 1)
            for a in range(NT):
                sc.wait_ge(mt_done, a + 1)
                if a >= 2:
                    sc.wait_ge(mrow_used, a - 1)
                else:
                    sc.wait_ge(zeroed, 16 * (T1 + 1))
                q = 2 * (a % 4)
                nc.scalar.activation(mrow[:, a % 2, :], ps[:, q:q + 2, :].rearrange("p a n -> p (a n)"), ACT.Copy,
                                     accum_out=cnt[:, a:a + 1]).then_inc(mrow_ready, 1)
            evac_transposes(1)

            def shared_evac(j):
                f, h = j % 4, j // 4
                sc.wait_ge(sh_done, j + 1)
                g = 4 + 2 * (j % 2)
                nc.scalar.activation(sact[:, f, h * 512:(h + 1) * 512], ps[:, g, :], ACT.Silu).then_inc(sh_sil, 1)
                if j >= 2:
                    sc.wait_ge(sh_act, j - 1)
                copy(utmp[:, j % 2, :], ps[:, g + 1, :]).then_inc(sh_u, 1)

            sc.wait_ge(lgc_ready, 1)
            nc.scalar.activation(tmp, tmp, ACT.Exp).then_inc(ex_ready, 1)
            for j in range(8):
                shared_evac(j)

            def expert(u, e):
                sc.wait_ge(gu_done, e + 1)
                nc.scalar.activation(sil[:, u, :], ps[:, 2 * u, 0:KF * CAP], ACT.Silu).then_inc(sil_ready, 1)

            def expert_out(u, e, later):
                sc.wait_ge(dn_done, e + 1)
                if later:
                    sc.wait_ge(o_stored[u], (e - u) * 16)
                copy(ob[:, u, 0:D], ps[:, 6, :]).then_inc(oa_ready, 1)
                sc.wait_ge(oa_ready, e + 1)
                nc.scalar.dma_start(slot_out[bass.ds(e * CAP, P), :], ob[:, u, 0:D]).then_inc(o_stored[u], 16)
                sc.wait_ge(obb_ready, e + 1)
                nc.scalar.dma_start(slot_out[bass.ds(e * CAP + P, CB), :], ob[0:CB, u, D:2 * D]).then_inc(o_stored[u], 16)

            expert(0, 0)
            expert(1, 1)
            expert_out(0, 0, False)
            expert(0, 2)
            expert_out(1, 1, False)
            with sc.Fori(1, E0 // 2 - 1) as g:
                e = g * 2
                for u in range(2):
                    expert(1 - u, e + u + 1)
                    expert_out(u, e + u, True)
            expert(1, E0 - 1)
            expert_out(0, E0 - 2, True)
            expert_out(1, E0 - 1, True)

            evac_transposes(2)
            for i in range(NT):
                sc.wait_ge(be_done, i + 1)
                copy(beta[:, i, :], ps[:, 2 + i % 2, :]).then_inc(be_evac, 1)
            evac_transposes(3)
            for j in range(4):
                f, h = j % 2, j // 2
                sc.wait_ge(s1_done, j + 1)
                nc.scalar.activation(gact[:, f, h * 512:(h + 1) * 512], ps[:, 4 + j % 2, :], ACT.Gelu).then_inc(s1_act, 1)
            for t in range(T1):
                u = t % 2
                sc.wait_ge(h1_done, t + 1)
                nc.scalar.activation(sil[:, u, 0:F], ps[:, 2, 0:F], ACT.Silu).then_inc(g1_ready, 1)
                sc.wait_ge(y1_done, t + 1)
                if t >= 2:
                    sc.wait_ge(y1_stored[u], 16 * (t // 2))
                copy(ob[:, u, 0:D], ps[:, 6, :]).then_inc(y1_evac, 1)
                sc.wait_ge(y1_evac, t + 1)
                nc.scalar.dma_start(sorted_out[t * P:(t + 1) * P, :], ob[:, u, 0:D]).then_inc(y1_stored[u], 16)

        @block.vector
        def _(ve):
            v = nc.vector
            steps = [0]

            def link(ins):
                steps[0] += 1
                ins.then_inc(dve_step, 1)
                ve.wait_ge(dve_step, steps[0])

            def layernorm(ln):
                for i in range(NT):
                    last = v.bn_stats(stats[:, i, :], xres[:, i, :])
                link(last)
                for i in range(NT):
                    last = v.bn_aggr(mv[:, i, :], stats[:, i, :])
                link(last)
                v.tensor_scalar(rstd[:], mv[:, :, 1], EPS, None, ALU.add).then_inc(var_ready, 1)
                ve.wait_ge(std_ready, ln + 1)
                link(v.reciprocal(rstd[:], rstd[:]))
                for i in range(NT):
                    v.tensor_scalar(xn[:, i, :], xres[:, i, :], mv[:, i, 0:1], rstd[:, i:i + 1],
                                    ALU.subtract, ALU.mult).then_inc(xn_ready, 1)

            ve.wait_ge(ld_edge, 16)
            v.tensor_copy(edge_f[:], edge_i[:]).then_inc(edgef_ready, 1)
            ve.wait_ge(ld_x, 16)
            layernorm(0)
            ve.wait_ge(ld_bc, 64)
            for i in range(NT):
                ve.wait_ge(h_done, i + 1)
                v.tensor_tensor(cur[:, 0, i, :], ps[:, 2 + i % 2, :], b0b[:], ALU.add).then_inc(h_evac, 1)
                ve.wait_ge(h_evac, i + 1)
                v.tensor_scalar(xn[:, i, :], cur[:, 0, i, :], dwb[:, 0:1], None, ALU.mult)
            ve.wait_ge(const_ready, 1)
            ve.wait_ge(edgef_ready, 1)
            def onehots(u, h, c):
                v.tensor_scalar(ohd[:, u, :], iota[:], edge_f[:, 1, bass.ds(c, 1)], None, ALU.is_equal)
                v.tensor_scalar(ohs[:, u, :], iota[:, h * 512:(h + 1) * 512], edge_f[:, 0, bass.ds(c, 1)], None,
                                ALU.is_equal).then_inc(oh_ready, 1)

            for h in range(2):
                onehots(0, h, 0)
                onehots(1, h, 1)
                with ve.Fori(1, EC // 2) as g:
                    for u in range(2):
                        ve.wait_ge(oh_used, g * 2 + (u - 1) + h * (EC - 1))
                        onehots(u, h, g * 2 + u)
                ve.wait_ge(m_done, h + 1)
                for b in range(1, NT, 2):
                    v.tensor_copy(mT[:, b, h * 512:(h + 1) * 512], ps[:, b, :]).then_inc(m_evac_v, 1)
            ve.wait_ge(m_evac_v, NT)
            for a in range(NT):
                ve.wait_ge(mrow_ready, a + 1)
                ve.wait_ge(m_evac_a, NT)
                link(v.tensor_tensor(mrow[:, a % 2, :], mrow[:, a % 2, :], mT[:, a, :], ALU.add))
                link(v.tensor_scalar(S[:, a, :], mrow[:, a % 2, :], 1.0, None, ALU.min))
                diag = S[:, a, a * P:(a + 1) * P]
                v.tensor_tensor(diag, diag, ident[:], ALU.add).then_inc(mrow_used, 1)
                ve.wait_ge(mrow_used, a + 1)
                last = v.tensor_reduce(rsum[:, a:a + 1], S[:, a, :], X, ALU.add)
            link(last)
            link(v.tensor_scalar(rsum[:], rsum[:], 1.0, None, ALU.max))
            link(v.reciprocal(rsum[:], rsum[:]))
            v.reciprocal(cnt[:], cnt[:])
            for t in range(STEPS):
                last = v.tensor_scalar(wr[:, t, :], rsum[:], dwb[:, t + 1:t + 2], None, ALU.mult)
            link(last)
            for t in range(STEPS):
                for m in range(NT):
                    ve.wait_ge(s_done, t * NT + m + 1)
                    if t < STEPS - 1:
                        v.tensor_scalar(cur[:, (t + 1) % 2, m, :], ps[:, m, :], rsum[:, m:m + 1], None, ALU.mult)
                    ins = v.scalar_tensor_tensor(xn[:, m, :], ps[:, m, :], wr[:, t, m:m + 1], xn[:, m, :], ALU.mult, ALU.add)
                    ins.then_inc(s_evac, 1)
            ve.wait_ge(s_evac, STEPS * NT)
            for i in range(NT):
                last = v.scalar_tensor_tensor(xres[:, i, :], xn[:, i, :], 0.0, xres[:, i, :], ALU.max, ALU.add)
            link(last)
            layernorm(1)

            def bc(t):
                return t.unsqueeze(2).broadcast_to([P, NT, E0])

            def seg_sum(o, t):
                return v.tensor_reduce(o, by_e(t), X, ALU.add)

            ve.wait_ge(lg_done, 1)
            link(v.tensor_tensor(by_e(tmp), ps[:, 2, :].rearrange("p (i e) -> p i e", e=E0),
                                 rb[:].unsqueeze(1).broadcast_to([P, NT, E0]), ALU.add))
            link(v.tensor_reduce(red[:, 0, :], by_e(tmp), X, ALU.max))
            v.tensor_tensor(by_e(tmp), by_e(tmp), bc(red[:, 0, :]), ALU.subtract).then_inc(lgc_ready, 1)
            ve.wait_ge(ex_ready, 1)
            link(seg_sum(red[:, 1, :], tmp))
            link(v.reciprocal(red[:, 1, :], red[:, 1, :]))
            link(v.tensor_tensor(by_e(prob), by_e(tmp), bc(red[:, 1, :]), ALU.mult))
            for i in range(NT):
                last = v.max(top8[:, i, :], prob[:, i * E0:(i + 1) * E0])
            link(last)
            sixth = bc(top8[:, :, TOP - 1])
            v.tensor_tensor(by_e(dest), by_e(prob), sixth, ALU.is_gt)
            link(v.tensor_tensor(by_e(tmp), by_e(prob), sixth, ALU.is_equal))
            link(seg_sum(red[:, 2, :], dest))
            v.tensor_scalar(red[:, 2, :], red[:, 2, :], -1.0, float(TOP), ALU.mult, ALU.add)
            link(v.tensor_tensor_scan(csel, segs[:], tmp, 0.0, ALU.mult, ALU.add))
            link(v.tensor_tensor(by_e(csel), by_e(csel), bc(red[:, 2, :]), ALU.is_le))
            link(v.tensor_tensor(tmp, tmp, csel, ALU.mult))
            link(v.tensor_tensor(sel, dest, tmp, ALU.add))
            v.tensor_copy(selb, sel).then_inc(sel_ready, 1)
            v.tensor_tensor_scan(csel, segs[:], sel, 0.0, ALU.mult, ALU.add)
            link(v.tensor_tensor(gate, prob, sel, ALU.mult))
            link(seg_sum(red[:, 3, :], gate))
            link(v.tensor_scalar(red[:, 3, :], red[:, 3, :], 1e-9, None, ALU.add))
            link(v.reciprocal(red[:, 3, :], red[:, 3, :]))
            link(v.tensor_tensor(by_e(gate), by_e(gate), bc(red[:, 3, :]), ALU.mult))
            ve.wait_ge(rank_done, 1)
            link(v.tensor_copy(rank_t, ps[:, 3, :]))
            link(v.tensor_scalar(tmp, rank_t, float(CAP), None, ALU.is_ge))
            v.tensor_tensor(by_e(dest), by_e(rank_t), ebase[:].unsqueeze(1).broadcast_to([P, NT, E0]), ALU.add)
            link(v.tensor_scalar(prob, tmp, -1.0, 1.0, ALU.mult, ALU.add))
            v.tensor_tensor(gate, gate, prob, ALU.mult)
            link(v.scalar_tensor_tensor(dest, tmp, FAR, dest, ALU.mult, ALU.add))
            for k in range(TOP):
                link(v.scalar_tensor_tensor(tmp, csel, float(k + 1), sel, ALU.is_equal, ALU.mult))
                v.tensor_tensor(prob, tmp, dest, ALU.mult)
                link(v.tensor_tensor(rank_t, tmp, gate, ALU.mult))
                link(seg_sum(dk[:, k, :], prob))
                seg_sum(gk[:, k, :], rank_t)
                v.tensor_copy(dki[:, k, :], dk[:, k, :]).then_inc(dki_ready, 1)
            link(v.tensor_scalar(prob[:, 0:TOP * NT], dk[:].rearrange("p k i -> p (k i)"), float(SLOTS), None, ALU.is_lt))
            link(v.tensor_tensor(prob[:, 0:TOP * NT], prob[:, 0:TOP * NT], dk[:].rearrange("p k i -> p (k i)"), ALU.mult))
            link(v.tensor_copy(gki[:].rearrange("p k i -> p (k i)"), prob[:, 0:TOP * NT]))
            for i in range(NT):
                ve.wait_ge(shd_done, i + 1)
                v.scalar_tensor_tensor(xres[:, i, :], ps[:, 4 + i % 4, :], 1.0 / SH, xres[:, i, :], ALU.mult, ALU.add).then_inc(shd_evac, 1)
            ve.wait_ge(tki_tr, 1)
            v.tensor_copy(idxA[:], ps[:, 2, 0:E0])
            v.tensor_copy(idxB[:], ps[0:CB, 2, E0:2 * E0]).then_inc(idx_ready, 1)

            def xt_evacuate(u, e):
                ve.wait_ge(xt_done, e + 1)
                v.tensor_copy(xT[:, u, :].rearrange("p (b n) -> p b n", b=2), ps[:, 4:6, 0:2 * CAP]).then_inc(xt_evac, 1)

            def multiply(u, e):
                ve.wait_ge(sil_ready, e + 1)
                v.tensor_tensor(act[:, u, :, :].rearrange("p f n -> p (f n)"), sil[:, u, :], ps[:, 2 * u + 1, 0:KF * CAP],
                                ALU.mult).then_inc(act_ready, 1)

            def second_out(u, e, later):
                ve.wait_ge(dn_done, e + 1)
                if later:
                    ve.wait_ge(o_stored[u], (e - u) * 16)
                v.tensor_copy(ob[0:CB, u, D:2 * D], ps[0:CB, 7, :]).then_inc(obb_ready, 1)

            xt_evacuate(0, 0)
            xt_evacuate(1, 1)
            multiply(0, 0)
            for e in range(2):
                multiply(1 - e, e + 1)
                xt_evacuate(e, e + 2)
                second_out(e, e, False)
            with ve.Fori(1, E0 // 2 - 1) as g:
                e = g * 2
                for u in range(2):
                    multiply(1 - u, e + u + 1)
                    xt_evacuate(u, e + u + 2)
                    second_out(u, e + u, True)
            multiply(1, E0 - 1)
            second_out(0, E0 - 2, True)
            second_out(1, E0 - 1, True)

            for j in range(NT * TOP):
                i, k = j // TOP, j % TOP
                ve.wait_ge(gat_ready[j % 4], 16 * (j // 4 + 1))
                if j >= 1:
                    ve.wait_ge(gat_used, j)
                v.scalar_tensor_tensor(xres[:, i, :], gat[:, j % 4, :], gk[:, k, i:i + 1], xres[:, i, :], ALU.mult, ALU.add).then_inc(gat_used, 1)
            ve.wait_ge(gat_used, NT * TOP)

            layernorm(2)
            for i in range(NT):
                ve.wait_ge(al_done, i + 1)
                v.tensor_tensor(xres[:, i, :], xres[:, i, :], ps[:, 4 + i % 2, :], ALU.add).then_inc(al_evac, 1)
            ve.wait_ge(al_evac, NT)
            for i in range(NT):
                last = v.tensor_tensor(xres[:, i, :], xres[:, i, :], b1b[:], ALU.add)
            link(last)
            for i in range(NT):
                ve.wait_ge(ga_done, i + 1)
                v.scalar_tensor_tensor(xres[:, i, :], ps[:, 6 + i % 2, :], cnt[:, i:i + 1], xres[:, i, :], ALU.mult, ALU.add).then_inc(ga_evac, 1)
            ve.wait_ge(ga_evac, NT)
            layernorm(3)

            W8 = NT * E1
            def t8(t):
                return t[:, 0:W8].rearrange("p (i e) -> p i e", e=E1)
            def bc8(t):
                return t.unsqueeze(2).broadcast_to([P, NT, E1])
            lg, one, cum, place = utmp[:, 0, 0:64], utmp[:, 0, 64:128], utmp[:, 0, 128:192], utmp[:, 0, 192:256]
            oneb = utmp[:, 0, 256:288].bitcast(BF16)
            ve.wait_ge(lg1_done, 1)
            link(v.tensor_copy(lg, ps[:, 2, 0:W8]))
            link(v.tensor_reduce(red[:, 0, :], t8(lg), X, ALU.max))
            link(v.tensor_tensor(t8(one), t8(lg), bc8(red[:, 0, :]), ALU.is_equal))
            link(v.tensor_tensor_scan(cum, segs8[:], one, 0.0, ALU.mult, ALU.add))
            link(v.scalar_tensor_tensor(one, cum, 1.0, one, ALU.is_equal, ALU.mult))
            v.tensor_copy(oneb, one).then_inc(sel1_ready, 1)
            ve.wait_ge(rank1_done, 1)
            r0, r1, r2, num = [t1row[:, j, :] for j in range(4)]
            link(v.tensor_copy(r0[:, 0:E1], ps[:, 3, W8:W8 + E1]))
            ge = utmp[:, 1, 0:64].rearrange("p (e t) -> p e t", t=8)
            link(v.tensor_scalar(r2[:, 0:8], num[:, 0:8], float(P), None, ALU.mult))
            link(v.tensor_tensor(ge, r0[:, 0:E1].unsqueeze(2).broadcast_to([P, E1, 8]), r2[:, 0:8].unsqueeze(1).broadcast_to([P, E1, 8]), ALU.is_gt))
            link(v.tensor_reduce(r0[:, 0:E1], ge, X, ALU.add))
            link(v.memset(r1[:, 0:E1], 1.0))
            link(v.tensor_tensor_scan(r2[:, 0:E1], r1[:, 0:E1], r0[:, 0:E1], 0.0, ALU.mult, ALU.add))
            link(v.tensor_tensor(r0[:, 0:E1], r2[:, 0:E1], r0[:, 0:E1], ALU.subtract))
            link(v.tensor_scalar(r0[:, 0:E1], r0[:, 0:E1], float(P), None, ALU.mult))
            link(v.tensor_tensor(t8(place), ps[:, 3, 0:W8].rearrange("p (i e) -> p i e", e=E1), r0[:, 0:E1].unsqueeze(1).broadcast_to([P, NT, E1]), ALU.add))
            link(v.tensor_tensor(place, place, one, ALU.mult))
            link(v.tensor_reduce(d1[:], t8(place), X, ALU.add))
            v.tensor_copy(d1i[:], d1[:]).then_inc(d1i_ready, 1)
            te = utmp[:, 1, 128:256].rearrange("p (t e) -> p t e", e=E1)
            link(v.tensor_tensor(te, r2[:, 0:E1].unsqueeze(1).broadcast_to([P, 16, E1]), num.unsqueeze(2).broadcast_to([P, 16, E1]), ALU.is_le))
            link(v.tensor_reduce(r1, te, X, ALU.add))
            link(v.tensor_scalar(r1, r1, float(E1 - 1), None, ALU.min))
            v.tensor_copy(t1e[:], r1[0:1, :]).then_inc(t1_ready, 1)
            for i in range(NT):
                ve.wait_ge(s2_done, i + 1)
                v.tensor_tensor(xres[:, i, :], xres[:, i, :], ps[:, 6 + i % 2, :], ALU.add).then_inc(s2_evac, 1)
            for t in range(T1):
                u = t % 2
                ve.wait_ge(x1t_done, t + 1)
                v.tensor_copy(xT[:, u, 0:D], ps[:, 4, :]).then_inc(x1t_evac, 1)
                ve.wait_ge(g1_ready, t + 1)
                v.tensor_tensor(act[:, u, :, :].rearrange("p f n -> p (f n)")[:, 0:F],
                                sil[:, u, 0:F], ps[:, 2, F:2 * F], ALU.mult).then_inc(a1_ready, 1)
                ve.wait_ge(a1t_done, t + 1)
                v.tensor_copy(xT[:, u, D:D + F], ps[:, 5, 0:F]).then_inc(a1t_evac, 1)
            ve.wait_ge(s2_evac, NT)
            for i in range(NT):
                j = NT * TOP + i
                ve.wait_ge(gat_ready[j % 4], 16 * (j // 4 + 1))
                v.tensor_tensor(xres[:, i, :], xres[:, i, :], gat[:, j % 4, :], ALU.add).then_inc(out_ready, 1)
                ve.wait_ge(out_ready, i + 1)
                v.tensor_copy(red[:, 5, 0:1], red[:, 0, 0:1]).then_inc(gat_used, 1)

        @block.tensor
        def _(pe):
            t_ = nc.tensor

            def mm(o, l, r, start, stop):
                return t_.matmul(o, l, r, start=start, stop=stop)

            def tokens(k, i):
                return xnT[:, k, i * P:(i + 1) * P]

            def transpose_rows(ln, i):
                pe.wait_ge(xn_ready, NT * ln + i + 1)
                if i >= 2:
                    pe.wait_ge(tr_evac, NT * ln + i - 1)
                for k in range(KD):
                    last = t_.transpose(ps[:, i % 2, k * P:(k + 1) * P], xn[:, i, k * P:(k + 1) * P], ident[:])
                last.then_inc(tr_done, 1)

            pe.wait_ge(const_ready, 1)
            for i in range(NT):
                transpose_rows(0, i)
            pe.wait_ge(ld_w0, 16)
            for i in range(NT):
                pe.wait_ge(tr_evac, i + 1)
                if i >= 2:
                    pe.wait_ge(h_evac, i - 1)
                for k in range(KD):
                    last = mm(ps[:, 2 + i % 2, :], tokens(k, i), w0s[:, k, :], k == 0, k == KD - 1)
                last.then_inc(h_done, 1)

            pe.wait_ge(h_evac, NT)

            def chunk(u, h, c, first, last_chunk):
                pe.wait_ge(oh_ready, c + h * EC + 1)
                for b in range(NT):
                    last = t_.matmul(ps[:, b, :], ohd[:, u, b * P:(b + 1) * P], ohs[:, u, :], start=first, stop=last_chunk)
                return last

            for h in range(2):
                if h == 1:
                    pe.wait_ge(m_evac_a, NT // 2)
                    pe.wait_ge(m_evac_v, NT // 2)
                chunk(0, h, 0, True, False).then_inc(oh_used, 1)
                chunk(1, h, 1, False, False).then_inc(oh_used, 1)
                with pe.Fori(1, EC // 2 - 1) as g:
                    c = g * 2
                    for u in range(2):
                        chunk(u, h, c + u, False, False).then_inc(oh_used, 1)
                chunk(0, h, EC - 2, False, False).then_inc(oh_used, 1)
                chunk(1, h, EC - 1, False, True).then_inc(m_done, 1)
            pe.wait_ge(m_evac_a, NT)
            pe.wait_ge(m_evac_v, NT)
            for a in range(NT):
                if a >= 4:
                    pe.wait_ge(mrow_ready, a - 3)
                for b in range(NT):
                    last = t_.transpose(ps[:, 2 * (a % 4) + b // 4, (b % 4) * P:(b % 4 + 1) * P], mT[:, b, a * P:(a + 1) * P], ident[:])
                last.then_inc(mt_done, 1)
            pe.wait_ge(mrow_used, NT)
            pe.wait_ge(mrow_ready, NT)
            for t in range(STEPS):
                if t >= 1:
                    pe.wait_ge(s_evac, t * NT)
                for m in range(NT):
                    for k in range(NT):
                        last = mm(ps[:, m, :], S[:, k, m * P:(m + 1) * P], cur[:, t % 2, k, :], k == 0, k == NT - 1)
                    last.then_inc(s_done, 1)
            pe.wait_ge(s_evac, STEPS * NT)

            pe.wait_ge(ld_small, 32)
            for i in range(NT):
                transpose_rows(1, i)
            for i in range(NT):
                pe.wait_ge(tr_evac, NT + i + 1)
                for k in range(KD):
                    last = mm(ps[:, 2, i * E0:(i + 1) * E0], tokens(k, i), rw[:, k, :], k == 0, k == KD - 1)
            last.then_inc(lg_done, 1)

            def shared(j):
                f, h = j % 4, j // 4
                if j >= 2:
                    pe.wait_ge(sh_u, j - 1)
                for w, g in ((sg, 4 + 2 * (j % 2)), (su, 5 + 2 * (j % 2))):
                    for k in range(KD):
                        last = mm(ps[:, g, :], w[:, k, f * P:(f + 1) * P], xnT[:, k, h * 512:(h + 1) * 512], k == 0, k == KD - 1)
                last.then_inc(sh_done, 1)

            pe.wait_ge(ld_shared, 48)
            for j in range(4):
                shared(j)
            pe.wait_ge(sel_ready, 1)
            selm = selb.rearrange("p (i e) -> p i e", e=E0)
            for i in range(NT):
                for j in range(i):
                    mm(ps[:, 3, i * E0:(i + 1) * E0], ones[:], selm[:, j, :], j == 0, False)
                last = mm(ps[:, 3, i * E0:(i + 1) * E0], tri[:], selm[:, i, :], i == 0, True)
            last.then_inc(rank_done, 1)
            for j in range(4, 8):
                shared(j)
            pe.wait_ge(sh_act, 8)
            pe.wait_ge(sh_u, 8)
            for i in range(NT):
                if i >= 4:
                    pe.wait_ge(shd_evac, i - 3)
                for k in range(4):
                    last = mm(ps[:, 4 + i % 4, :], sact[:, k, i * P:(i + 1) * P], sd[:, k, :], k == 0, k == 3)
                last.then_inc(shd_done, 1)
            pe.wait_ge(tki_loaded, 16)
            t_.transpose(ps[:, 2, 0:E0], tki[:, 0:P], ident[0:E0, 0:E0])
            t_.transpose(ps[0:CB, 2, E0:2 * E0], tki[:, P:CAP], ident[0:E0, 0:E0]).then_inc(tki_tr, 1)
            pe.wait_ge(shd_evac, NT)
            pe.wait_ge(idx_ready, 1)

            def turn(u, e, n, first):
                pe.wait_ge(xg_ready[u], n)
                if not first:
                    pe.wait_ge(xt_evac, e)
                for k in range(KD):
                    o = (k % 2) * CAP
                    t_.transpose(ps[:, 4 + k // 2, o:o + P], xg[:, u, k * P:(k + 1) * P], ident[:])
                    last = t_.transpose(ps[:, 4 + k // 2, o + P:o + CAP], xg[0:CB, u, D + k * P:D + (k + 1) * P], ident[0:CB, 0:CB])
                last.then_inc(xt_done, 1)

            def gate_up(u, e, n):
                pe.wait_ge(wgu_ready[u], n)
                pe.wait_ge(xt_evac, e + 1)
                for g in range(2):
                    for f in range(KF):
                        for k in range(KD):
                            last = mm(ps[:, 2 * u + g, f * CAP:(f + 1) * CAP],
                                      ring[:, u, (g * KD + k) * F + f * P:(g * KD + k) * F + (f + 1) * P],
                                      xT[:, u, k * CAP:(k + 1) * CAP], k == 0, k == KD - 1)
                last.then_inc(gu_done, 1)

            def down(u, e, n, first):
                pe.wait_ge(act_ready, e + 1)
                pe.wait_ge(wd_ready[u], n)
                if not first:
                    pe.wait_ge(oa_ready, e)
                    pe.wait_ge(obb_ready, e)
                for o, lo, hi in ((6, 0, P), (7, P, CAP)):
                    for f in range(KF):
                        last = mm(ps[0:hi - lo, o, :], act[:, u, f, lo:hi],
                                  ring[:, u, 2 * KD * F + f * D:2 * KD * F + (f + 1) * D], f == 0, f == KF - 1)
                last.then_inc(dn_done, 1)

            turn(0, 0, 32, True)
            turn(1, 1, 32, False)
            gate_up(0, 0, 16)
            gate_up(1, 1, 16)
            turn(0, 2, 64, False)
            down(0, 0, 16, True)
            gate_up(0, 2, 32)
            turn(1, 3, 64, False)
            down(1, 1, 16, False)
            with pe.Fori(1, E0 // 2 - 1) as g:
                e = g * 2
                for u in range(2):
                    gate_up(1 - u, e + u + 1, g * 16 + 16 * (u + 1) if u == 1 else g * 16 + 16)
                    turn(u, e + u + 2, g * 32 + 64, False)
                    down(u, e + u, g * 16 + 16, False)
            gate_up(1, E0 - 1, E0 * 8)
            down(0, E0 - 2, E0 * 8, False)
            down(1, E0 - 1, E0 * 8, False)

            pe.wait_ge(ld_c, 32)
            for i in range(NT):
                transpose_rows(2, i)
            for i in range(NT):
                pe.wait_ge(tr_evac, 2 * NT + i + 1)
                if i >= 2:
                    pe.wait_ge(be_evac, i - 1)
                for k in range(KD):
                    last = mm(ps[:, 2 + i % 2, :], tokens(k, i), wns[:, k, :], k == 0, k == KD - 1)
                last.then_inc(be_done, 1)
            for i in range(NT):
                if i >= 2:
                    pe.wait_ge(al_evac, i - 1)
                for k in range(KD):
                    last = mm(ps[:, 4 + i % 2, :], tokens(k, i), wcs[:, k, :], k == 0, k == KD - 1)
                last.then_inc(al_done, 1)
            pe.wait_ge(be_evac, NT)
            pe.wait_ge(obb_ready, E0)
            pe.wait_ge(oa_ready, E0)
            for i in range(NT):
                if i >= 2:
                    pe.wait_ge(ga_evac, i - 1)
                for b in range(NT):
                    last = mm(ps[:, 6 + i % 2, :], mT[:, b, i * P:(i + 1) * P], beta[:, b, :], b == 0, b == NT - 1)
                last.then_inc(ga_done, 1)

            for i in range(NT):
                transpose_rows(3, i)
            for i in range(NT):
                pe.wait_ge(tr_evac, 3 * NT + i + 1)
                for k in range(KD):
                    last = mm(ps[:, 2, i * E1:(i + 1) * E1], tokens(k, i), gw[:, k, :], k == 0, k == KD - 1)
            last.then_inc(lg1_done, 1)
            pe.wait_ge(ld_s1, 32)
            pe.wait_ge(al_evac, NT)
            for j in range(4):
                f, h = j % 2, j // 2
                if j >= 2:
                    pe.wait_ge(s1_act, j - 1)
                for k in range(KD):
                    last = mm(ps[:, 4 + j % 2, :], s1w[:, k, f * P:(f + 1) * P], xnT[:, k, h * 512:(h + 1) * 512], k == 0, k == KD - 1)
                last.then_inc(s1_done, 1)
            pe.wait_ge(sel1_ready, 1)
            onem = utmp[:, 0, 256:288].bitcast(BF16).rearrange("p (i e) -> p i e", e=E1)
            for i in range(NT):
                for j in range(i):
                    mm(ps[:, 3, i * E1:(i + 1) * E1], ones[:], onem[:, j, :], j == 0, False)
                mm(ps[:, 3, i * E1:(i + 1) * E1], tri[:], onem[:, i, :], i == 0, True)
            for j in range(NT):
                last = mm(ps[:, 3, NT * E1:NT * E1 + E1], ones[:], onem[:, j, :], j == 0, j == NT - 1)
            last.then_inc(rank1_done, 1)
            pe.wait_ge(s1_act, 4)
            pe.wait_ge(ga_evac, NT)
            for i in range(NT):
                if i >= 2:
                    pe.wait_ge(s2_evac, i - 1)
                for f in range(KF):
                    last = mm(ps[:, 6 + i % 2, :], gact[:, f, i * P:(i + 1) * P], s2w[:, f, :], f == 0, f == KF - 1)
                last.then_inc(s2_done, 1)
            pe.wait_ge(s2_evac, NT)
            for t in range(T1):
                u = t % 2
                w = ring[:, u, :]
                pe.wait_ge(x1_ready[u], 16 * (t // 2 + 1))
                if t >= 1:
                    pe.wait_ge(x1t_evac, t)
                for k in range(KD):
                    last = t_.transpose(ps[:, 4, k * P:(k + 1) * P], xg[:, u, k * P:(k + 1) * P], ident[:])
                last.then_inc(x1t_done, 1)
                pe.wait_ge(w1_ready[u], 16 * (t // 2 + 1))
                pe.wait_ge(x1t_evac, t + 1)
                if t >= 1:
                    pe.wait_ge(a1_ready, t)
                for k in range(KD):
                    last = mm(ps[:, 2, :], xT[:, u, k * P:(k + 1) * P], w[:, k * 2 * F:(k + 1) * 2 * F], k == 0, k == KD - 1)
                last.then_inc(h1_done, 1)
                pe.wait_ge(a1_ready, t + 1)
                if t >= 1:
                    pe.wait_ge(a1t_evac, t)
                for f in range(KF):
                    last = t_.transpose(ps[:, 5, f * P:(f + 1) * P], act[:, u, :, :].rearrange("p f n -> p (f n)")[:, f * P:(f + 1) * P], ident[:])
                last.then_inc(a1t_done, 1)
                pe.wait_ge(a1t_evac, t + 1)
                if t >= 1:
                    pe.wait_ge(y1_evac, t)
                for f in range(KF):
                    last = mm(ps[:, 6, :], xT[:, u, D + f * P:D + (f + 1) * P], w[:, 2 * KD * F + f * D:2 * KD * F + (f + 1) * D], f == 0, f == KF - 1)
                last.then_inc(y1_done, 1)


def kernel(**inputs):
    import numpy as np
    import concourse.bacc as bacc
    from concourse.bass_utils import run_bass_kernel_spmd

    a = {k: np.asarray(v) for k, v in inputs.items()}

    def chunked(w):
        e, k, m = w.shape
        return w.reshape(e, k // P, P, m).transpose(0, 2, 1, 3).reshape(e, P, -1)

    def turned(w):
        return w.transpose(0, 2, 1)

    arrays = {
        "x": a["x"],
        "edges": np.concatenate([a["src"].reshape(EC, P).T, a["dst"].reshape(EC, P).T], axis=1),
        "w0": a["L0_gnn_W"], "b0": a["L0_gnn_b"], "dw": a["L0_gnn_diffusion_weights"],
        "rwT": a["L0_ffn_router_w"].T, "rbias": a["L0_ffn_bias"],
        "sgT": a["L0_ffn_shared_w_gate"].reshape(SH * F, D).T,
        "suT": a["L0_ffn_shared_w_up"].reshape(SH * F, D).T,
        "sdT": turned(a["L0_ffn_shared_w_down"]).reshape(SH * F, D),
        "we0": np.concatenate([chunked(turned(a["L0_ffn_w_gate"])), chunked(turned(a["L0_ffn_w_up"])),
                               chunked(turned(a["L0_ffn_w_down"]))], axis=2),
        "wc": a["L1_gnn_wc"], "wn": a["L1_gnn_wn"], "b1": a["L1_gnn_bias"],
        "gwT": a["L1_ffn_gate_w"].T,
        "we1": np.concatenate([chunked(np.concatenate([turned(a["L1_ffn_w1"]), turned(a["L1_ffn_w3"])], axis=2)),
                               chunked(turned(a["L1_ffn_w2"]))], axis=2),
        "sw1T": a["L1_ffn_sw1"].T, "sw2T": a["L1_ffn_sw2"].T,
    }
    arrays = {f"in_{k}": np.ascontiguousarray(v) for k, v in arrays.items()}
    nc = bacc.Bacc("TRN2", target_bir_lowering=False, num_devices=1)
    args = [nc.dram_tensor(k, v.shape, mybir.dt.from_np(v.dtype), kind="ExternalInput").ap() for k, v in arrays.items()]
    args.append(nc.dram_tensor("out", (N, D), F32, kind="ExternalOutput").ap())
    build(nc, *args)
    r = run_bass_kernel_spmd(nc, [arrays], core_ids=[0])
    return r.results[0]["out"]
```

```python
from contextlib import ExitStack

import concourse.bass as bass
from concourse import mybir

ALU = mybir.AluOpType
ACT = mybir.ActivationFunctionType
F32 = mybir.dt.float32
F32R = mybir.dt.float32r
F16 = mybir.dt.float16
BF16 = mybir.dt.bfloat16
I32 = mybir.dt.int32
U32 = mybir.dt.uint32
X = mybir.AxisListType.X

P = 128
N = 1024
D = 512
NT = N // P
KD = D // P
NE = 16384
EC = NE // P
GROUP = 64
OHB = 16
HEAD = 5
RING = 8
STEPS = 3
OHS = NT + EC
E0 = 64
TOP = 6
CAP = N * TOP * 2 // E0
CB = CAP - P
SLOTS = E0 * CAP
F = 256
KF = F // P
GU = 2 * KD * F
WROW = GU + KF * D
SH = 2
E1 = 8
T1 = N // P + E1 - 1
EPS = 1e-5
FAR = float(1 << 20)


def build(nc, x, pairs, w0, b0, dw, rwT, rbias, sgT, suT, sdT, we0, wc, wn, b1, gwT, we1, sw1T, sw2T, out):
    xn_dram = nc.dram_tensor("xn_dram", [N, D], F32, kind="Internal").ap()
    slot_token = nc.dram_tensor("slot_token", [SLOTS, 1], F32, kind="Internal").ap()
    slot_out = nc.dram_tensor("slot_out", [SLOTS, D], F32, kind="Internal").ap()
    sorted_in = nc.dram_tensor("sorted_in", [T1 * P, D], F32, kind="Internal").ap()
    block_tot = nc.dram_tensor("block_tot", [NT, P], F32, kind="Internal").ap()
    moved = nc.dram_tensor("moved", [NE, 2], I32, kind="Internal").ap()
    sorted_out = nc.dram_tensor("sorted_out", [T1 * P, D], F32, kind="Internal").ap()

    with ExitStack() as ctx:
        def sb(name, shape, dt=F32):
            return ctx.enter_context(nc.sbuf_tensor(name, shape, dt))

        def sem(name):
            return ctx.enter_context(nc.semaphore(name))

        ps = ctx.enter_context(nc.psum_tensor("ps", [P, 8, 512], F32))

        xres = sb("xres", [P, NT, D])
        xn = sb("xn", [P, NT, D])
        with nc.sbuf_tensor("xnT", [P, KD, N], F32) as xnT:
            pass
        cur1_lo = sb("cur1_lo", [P, NT, D], F32R)
        with nc.sbuf_tensor("zone", [P, 20480], F32) as zone:
            pass
        S = sb("S", [P, NT, N], F32R)
        cur0_hi = sb("cur0_hi", [P, NT, D], F32R)
        cur0_lo = sb("cur0_lo", [P, NT, D], F32R)
        cur1_hi = sb("cur1_hi", [P, NT, D], F32R)
        cur = ((cur0_hi, cur0_lo), (cur1_hi, cur1_lo))
        mT = sb("mT", [P, NT, N], F32R)
        identr = sb("identr", [P, P], F32R)
        onesr = sb("onesr", [P, 2], F32R)
        ring = sb("ring", [P, 2, WROW])
        ident = sb("ident", [P, P])
        tri = sb("tri", [P, P], BF16)
        ones = sb("ones", [P, P], BF16)
        iota = sb("iota", [P, N], F16)
        segs = sb("segs", [P, NT * E0], BF16)
        segs8 = sb("segs8", [P, NT * E1], BF16)
        pair_i = sb("pair_i", [P, P, 2], I32)
        next_i = sb("next_i", [P, 2], I32)
        viol = sb("viol", [1, 1], I32)
        words = sb("words", [1, EC // RING], I32)
        b0b = sb("b0b", [P, D])
        b1b = sb("b1b", [P, D])
        dwb = sb("dwb", [P, STEPS + 1])
        rb = sb("rb", [P, E0])
        rw = sb("rw", [P, KD, E0])
        gw = sb("gw", [P, KD, E1])
        stats = sb("stats", [P, NT, 6])
        mv = sb("mv", [P, NT, 2])
        rstd = sb("rstd", [P, NT])
        rsum = sb("rsum", [P, NT])
        cnt = sb("cnt", [P, NT])
        wr = sb("wr", [P, STEPS, NT])
        red = sb("red", [P, 6, NT])
        top8 = sb("top8", [P, NT, 8])
        tokf = sb("tokf", [P, NT])
        ebase = sb("ebase", [P, E0])
        dk = sb("dk", [P, TOP, NT])
        dki = sb("dki", [P, TOP, NT], U32)
        gk = sb("gk", [P, TOP, NT])
        gki = sb("gki", [P, TOP, NT], U32)
        idxA = sb("idxA", [P, E0], U32)
        idxB = sb("idxB", [CB, E0], U32)
        fullw = sb("fullw", [1, E0 // RING], I32)
        colA = sb("colA", [P, 2], U32)
        colB = sb("colB", [CB, 2], U32)
        t1row = sb("t1row", [P, 4, 16])
        utmp_full = sb("utmp_full", [P, E0 + 8])
        t1e = sb("t1e", [1, 16], I32)
        d1 = sb("d1", [P, NT])
        d1i = sb("d1i", [P, NT], U32)

        ohd = zone[:, 0:8192].bitcast(BF16).rearrange("p (c n) -> p c n", c=EC)
        xnT_words = xnT[:].rearrange("p k n -> p (k n)")
        ohs = xnT_words.bitcast(BF16).rearrange("p (b n) -> p b n", b=OHB)
        ohx = zone[:, 19456:19968].bitcast(BF16).rearrange("p (b n) -> p b n", b=NT)
        pair_f = zone[:, 16384:16640].rearrange("p (t c) -> p t c", t=2)
        blk_i = zone[:, 16640:16768].bitcast(I32)
        blk = zone[:, 16768:16896]
        edge_f = zone[:, 16896:17152].rearrange("p (t c) -> p t c", t=2)
        dloc = zone[:, 17152:17280]
        lob = zone[:, 17280:17408]
        pick = zone[:, 17408:17536]
        diag = zone[:, 17536:17664]
        small = zone[:, 17664:17920]
        onesf = zone[:, 17920:18048]
        zerob = zone[:, 18048:18112].bitcast(BF16)
        edge_x = zone[:, 18112:18176].rearrange("p (t b) -> p t b", b=NT)
        zeros = zone[:, 18432:19456]
        g_mask = zone[:, 0:1024].rearrange("p (b j) -> p b j", b=NT)
        g_scan = zone[:, 1024:3072].rearrange("p (z b j) -> p z b j", z=2, b=NT)
        g_tot = zone[:, 3072:4096].rearrange("p (b q) -> p b q", b=NT)
        g_bef = zone[:, 4096:5120].rearrange("p (b q) -> p b q", b=NT)
        g_pos = zone[:, 5120:5248]
        g_posi = zone[:, 5248:5376].bitcast(U32)
        g_col = zone[:, 5376:5377].bitcast(U32)
        g_pair = zone[:, 5378:5380].bitcast(I32)
        g_sum = zone[:, 5380:5388]
        g_tmp = zone[:, 5504:5632]
        w0s = ring[:, 0, 0:KD * D].rearrange("p (k n) -> p k n", k=KD)
        sact = zone[:, 0:4096].rearrange("p (f n) -> p f n", f=4)
        sd = zone[:, 4096:6144].rearrange("p (k n) -> p k n", k=4)
        sg = zone[:, 6144:8192].rearrange("p (k n) -> p k n", k=KD)
        su = zone[:, 8192:10240].rearrange("p (k n) -> p k n", k=KD)
        xg = zone[:, 10240:12288].rearrange("p (b n) -> p b n", b=2)
        xT = zone[:, 12288:13824].rearrange("p (b n) -> p b n", b=2)
        sil = zone[:, 13824:14592].rearrange("p (b n) -> p b n", b=2)
        act = zone[:, 14592:15360].rearrange("p (b f n) -> p b f n", b=2, f=KF)
        ob = zone[:, 15360:17408].rearrange("p (b n) -> p b n", b=2)
        gat = zone[:, 17408:19456].rearrange("p (b n) -> p b n", b=4)
        utmp = zone[:, 19456:20480].rearrange("p (b n) -> p b n", b=2)
        def table(j):
            return zone[:, 15360 + 512 * j:15872 + 512 * j]
        def by_e(t):
            return t.rearrange("p (i e) -> p i e", e=E0)
        prob, sel, csel, dest, gate, tmp, rank_t = [table(j) for j in range(7)]
        selb = table(7)[:, 0:256].bitcast(BF16)
        tki = table(7)[0:E0, 256:256 + CAP]
        beta_hi = S[:, 0:NT // 2, :].rearrange("p a (b n) -> p (a b) n", n=D)
        beta_lo = cur0_lo
        wns = sg
        wcs = su
        s1w = zone[:, 4096:5120].rearrange("p (k n) -> p k n", k=KD)
        s2w = zone[:, 5120:6144].rearrange("p (k n) -> p k n", k=KF)
        gact = zone[:, 0:2048].rearrange("p (f n) -> p f n", f=KF)

        viol_ready, edges_final, lo_ready, lo_done, cols_done, cols_ready = [
            sem(n) for n in ("viol_ready", "edges_final", "lo_ready", "lo_done", "cols_done", "cols_ready")]
        vrow_ready, vsum_done, pairf_ready, words_ready, cnt_ready = [
            sem(n) for n in ("vrow_ready", "vsum_done", "pairf_ready", "words_ready", "cnt_ready")]
        g_dma, g_step, g_go = sem("g_dma"), sem("g_step"), sem("g_go")
        ld_x, ld_edge, ld_w0, ld_bc, ld_small = [sem(f"ld_{n}") for n in ("x", "edge", "w0", "bc", "small")]
        ld_shared, ld_c, ld_s1 = [sem(f"ld_{n}") for n in ("shared", "c", "s1")]
        const_ready = sem("const_ready")
        pool_step = sem("pool_step")
        zero_ready, zeroed = sem("zero_ready"), sem("zeroed")
        dve_step, edgef_ready = sem("dve_step"), sem("edgef_ready")
        xn_ready, tr_done, tr_evac = sem("xn_ready"), sem("tr_done"), sem("tr_evac")
        var_ready, std_ready = sem("var_ready"), sem("std_ready")
        vart_ready, stdt_ready = sem("vart_ready"), sem("stdt_ready")
        h_done, h_evac, h_hi, h_lo, h_term = [sem(n) for n in ("h_done", "h_evac", "h_hi", "h_lo", "h_term")]
        oh_ready, oh_used = sem("oh_ready"), sem("oh_used")
        m_done, m_evac_a, m_evac_v = sem("m_done"), sem("m_evac_a"), sem("m_evac_v")
        mt_done, adj_ready, s_ready = sem("mt_done"), sem("adj_ready"), sem("s_ready")
        cnt_done, ohd_ready = sem("cnt_done"), sem("ohd_ready")
        s_done, s_evac = sem("s_done"), sem("s_evac")
        zone_free = sem("zone_free")
        xn_stored = sem("xn_stored")
        lg_done, lgc_ready, ex_ready, sel_ready, rank_done = [sem(n) for n in ("lg_done", "lgc_ready", "ex_ready", "sel_ready", "rank_done")]
        sh_done, sh_sil, sh_act, shd_done, shd_evac = [sem(n) for n in ("sh_done", "sh_sil", "sh_act", "shd_done", "shd_evac")]
        dki_ready, scattered, tki_loaded, tki_tr, idx_ready = [sem(n) for n in ("dki_ready", "scattered", "tki_loaded", "tki_tr", "idx_ready")]
        full_ready = sem("full_ready")
        col_ready, gather_go = sem("col_ready"), sem("gather_go")
        xg_ready = [sem(f"xg_ready{u}") for u in range(2)]
        wgu_ready = [sem(f"wgu_ready{u}") for u in range(2)]
        wd_ready = [sem(f"wd_ready{u}") for u in range(2)]
        xt_done, xt_evac = sem("xt_done"), sem("xt_evac")
        gu_done, sil_ready, act_ready = sem("gu_done"), sem("sil_ready"), sem("act_ready")
        dn_done, oa_ready, obb_ready = sem("dn_done"), sem("oa_ready"), sem("obb_ready")
        o_stored = [sem(f"o_stored{u}") for u in range(2)]
        gat_ready = [sem(f"gat_ready{u}") for u in range(4)]
        gat_used = sem("gat_used")
        be_hi = sem("be_hi")
        be_done, be_evac, al_done, al_evac, ga_done, ga_evac = [sem(n) for n in ("be_done", "be_evac", "al_done", "al_evac", "ga_done", "ga_evac")]
        lg1_done, sel1_ready, rank1_done, t1_ready, d1i_ready = [sem(n) for n in ("lg1_done", "sel1_ready", "rank1_done", "t1_ready", "d1i_ready")]
        s1_done, s1_act, s2_done, s2_evac = [sem(n) for n in ("s1_done", "s1_act", "s2_done", "s2_evac")]
        scattered1, x1_ready = sem("scattered1"), [sem(f"x1_ready{u}") for u in range(2)]
        y1_stored = [sem(f"y1_stored{u}") for u in range(2)]
        out_ready, out_done = sem("out_ready"), sem("out_done")

        rows = lambda t: t.rearrange("(i p) d -> p i d", p=P)
        xn_rows = rows(xn_dram)

        def flags(eng, j):
            return eng.value_load(fullw[0:1, bass.ds(j, 1)], min_val=0, max_val=2 ** (RING + 2) - 1)

        H_BANKS = (2, 3, 4, 7)

        def bit(word, i):
            return (word // 2 ** i) % 2

        def by_size(eng, full, work):
            if full is None:
                work(P)
                return
            with eng.If(full > 0):
                work(CAP)
            with eng.Else():
                work(P)

        block = ctx.enter_context(nc.Block())

        @block.sync
        def _(sp):
            sp.dma_start(xres[:], rows(x)).then_inc(ld_x, 16)
            sp.dma_start(pair_i[:], pairs.rearrange("(c j) t -> c j t", j=P)).then_inc(ld_edge, 16)
            sp.dma_start(next_i[0:P - 1, :], pairs.rearrange("(c j) t -> c j t", j=P)[1:P, 0, :]).then_inc(ld_edge, 16)
            sp.dma_start(w0s, w0.rearrange("(k p) n -> p k n", p=P)).then_inc(ld_w0, 16)
            sp.dma_start(rw[:], rwT.rearrange("(k p) n -> p k n", p=P)).then_inc(ld_small, 16)
            sp.dma_start(gw[:], gwT.rearrange("(k p) n -> p k n", p=P)).then_inc(ld_small, 16)
            sp.dma_start(b0b[:], b0.partition_broadcast(P)).then_inc(ld_bc, 16)
            sp.dma_start(b1b[:], b1.partition_broadcast(P)).then_inc(ld_bc, 16)
            sp.dma_start(dwb[:], dw.partition_broadcast(P)).then_inc(ld_bc, 16)
            sp.dma_start(rb[:], rbias.partition_broadcast(P)).then_inc(ld_bc, 16)
            sp.wait_ge(zero_ready, 1)
            sp.dma_start(slot_token.rearrange("(p c) o -> p (c o)", p=P), zeros[:, 0:SLOTS // P]).then_inc(zeroed, 16)
            sp.dma_start(slot_out.rearrange("(e c) d -> c e d", c=CAP)[P:CAP], zeros[0:CB, 0:D].unsqueeze(1).broadcast_to([CB, E0, D])).then_inc(zeroed, 16)
            for t in range(T1):
                sp.dma_start(sorted_in[t * P:(t + 1) * P, :], zeros[:, 0:D]).then_inc(zeroed, 16)
            sp.wait_ge(h_done, NT)
            for u in range(2):
                sp.dma_start(ring[:, u, 0:GU], we0[u, :, 0:GU]).then_inc(wgu_ready[u], 16)
                sp.dma_start(ring[:, u, GU:WROW], we0[u, :, GU:WROW]).then_inc(wd_ready[u], 16)
            sp.wait_ge(s_done, STEPS * NT)
            sp.wait_ge(s_evac, STEPS * NT)
            sp.dma_start(sg, sgT.rearrange("(k p) n -> p k n", p=P)).then_inc(ld_shared, 16)
            sp.dma_start(su, suT.rearrange("(k p) n -> p k n", p=P)).then_inc(ld_shared, 16)
            sp.dma_start(sd, sdT.rearrange("(k p) n -> p k n", p=P)).then_inc(ld_shared, 16)
            sp.wait_ge(xn_ready, 2 * NT)
            sp.dma_start(xn_rows, xn[:]).then_inc(xn_stored, 16)
            sp.wait_ge(scattered, 16 * TOP * NT)
            sp.wait_ge(sel_ready, 1)
            sp.wait_ge(rank_done, 1)
            sp.dma_start(tki, slot_token.rearrange("(e c) o -> e (c o)", e=E0)).then_inc(tki_loaded, 16)
            with sp.Fori(0, E0 // 2 - 1) as g:
                e = g * 2
                for u in range(2):
                    nxt = we0[bass.ds(e + u + 2, 1)].rearrange("o p n -> p (o n)")
                    sp.wait_ge(gu_done, e + u + 1)
                    sp.dma_start(ring[:, u, 0:GU], nxt[:, 0:GU]).then_inc(wgu_ready[u], 16)
                    sp.wait_ge(dn_done, e + u + 1)
                    sp.dma_start(ring[:, u, GU:WROW], nxt[:, GU:WROW]).then_inc(wd_ready[u], 16)
            sp.wait_ge(sh_done, 2 * 4)
            sp.dma_start(wns, wn.rearrange("(k p) n -> p k n", p=P)).then_inc(ld_c, 16)
            sp.dma_start(wcs, wc.rearrange("(k p) n -> p k n", p=P)).then_inc(ld_c, 16)
            sp.wait_ge(shd_done, NT)
            sp.dma_start(s1w, sw1T.rearrange("(k p) n -> p k n", p=P)).then_inc(ld_s1, 16)
            sp.dma_start(s2w, sw2T.rearrange("(k p) n -> p k n", p=P)).then_inc(ld_s1, 16)
            sp.wait_ge(dn_done, E0)
            sp.wait_ge(t1_ready, 1)
            sp.wait_ge(scattered1, 16 * NT)
            for t in range(T1):
                u, e = t % 2, E0 + t
                ex = sp.value_load(t1e[0:1, t:t + 1], min_val=0, max_val=E1 - 1)
                own = we1[bass.ds(ex, 1)].rearrange("o p n -> p (o n)")
                if t >= 2:
                    sp.wait_ge(xt_done, e - 1)
                sp.dma_start(xg[:, u, 0:D], sorted_in[t * P:(t + 1) * P, :]).then_inc(x1_ready[u], 16)
                if t >= 2:
                    sp.wait_ge(gu_done, e - 1)
                sp.dma_start(ring[:, u, 0:GU], own[:, 0:GU]).then_inc(wgu_ready[u], 16)
                if t >= 2:
                    sp.wait_ge(dn_done, e - 1)
                sp.dma_start(ring[:, u, GU:WROW], own[:, GU:WROW]).then_inc(wd_ready[u], 16)
            for i in range(NT):
                sp.wait_ge(out_ready, i + 1)
                sp.dma_start(out[i * P:(i + 1) * P, :], xres[:, i, :]).then_inc(out_done, 16)
            sp.wait_ge(out_done, 16 * NT)

        @block.gpsimd
        def _(pool):
            steps = [0]

            def link(ins):
                steps[0] += 1
                ins.then_inc(pool_step, 1)
                pool.wait_ge(pool_step, steps[0])

            pool.memset(zeros, 0.0).then_inc(zero_ready, 1)
            link(pool.iota(iota[:], pattern=[[1, N]], base=0, channel_multiplier=0, allow_small_or_imprecise_dtypes=True))
            pool.iota(tokf[:], pattern=[[P, NT]], base=0, channel_multiplier=1, allow_small_or_imprecise_dtypes=True)
            pool.iota(ebase[:], pattern=[[CAP, E0]], base=0, channel_multiplier=0, allow_small_or_imprecise_dtypes=True)
            pool.iota(t1row[:, 3, :], pattern=[[1, 16]], base=0, channel_multiplier=0, allow_small_or_imprecise_dtypes=True)
            pool.memset(ones[:], 1.0)
            pool.memset(tri[:], 1.0)
            pool.memset(segs[:], 1.0)
            pool.memset(segs8[:], 1.0)
            link(pool.memset(ident[:], 0.0))
            pool.affine_select(out=ident[:], in_=ident[:], compare_op=ALU.not_equal, fill=1.0, base=0, pattern=[[-1, P]], channel_multiplier=1)
            pool.affine_select(out=tri[:], in_=tri[:], compare_op=ALU.is_ge, fill=0.0, base=-1, pattern=[[1, P]], channel_multiplier=-1)
            pool.memset(segs[:].rearrange("p (i e) -> p i e", e=E0)[:, :, 0:1], 0.0)
            pool.memset(segs8[:].rearrange("p (i e) -> p i e", e=E1)[:, :, 0:1], 0.0).then_inc(const_ready, 1)

            pool.wait_ge(viol_ready, 1)
            bad = pool.value_load(viol[0:1, 0:1], min_val=0, max_val=NE)
            with pool.If(bad > 0):
                gs = [0]
                gd = [0]

                def done(ins):
                    gs[0] += 1
                    ins.then_inc(g_step, 1)
                    pool.wait_ge(g_step, gs[0])

                def landed(ins):
                    gd[0] += 16
                    ins.then_inc(g_dma, 16)
                    pool.wait_ge(g_dma, gd[0])

                for b in range(NT):
                    done(pool.tensor_scalar(g_mask[:, b, :], blk, float(b), None, ALU.is_equal))
                done(pool.tensor_copy(g_scan[:, 0], g_mask))
                z, d = 0, 1
                while d < P:
                    done(pool.tensor_tensor(g_scan[:, 1 - z, :, d:P], g_scan[:, z, :, d:P], g_scan[:, z, :, 0:P - d], ALU.add))
                    done(pool.tensor_copy(g_scan[:, 1 - z, :, 0:d], g_scan[:, z, :, 0:d]))
                    z, d = 1 - z, 2 * d
                done(pool.tensor_copy(g_sum, g_scan[:, z, :, P - 1]))
                for b in range(NT):
                    landed(pool.dma_start(block_tot[b, :].rearrange("(q o) -> q o", o=1), g_sum[:, b:b + 1]))
                landed(pool.dma_start(g_tot, block_tot.rearrange("b q -> (b q)").partition_broadcast(P)))
                done(pool.affine_select(out=g_bef, in_=g_tot, compare_op=ALU.is_ge, fill=0.0, base=-1, pattern=[[0, NT], [-1, P]], channel_multiplier=1))
                d = P // 2
                while d:
                    for t in (g_tot, g_bef):
                        done(pool.tensor_tensor(t[:, :, 0:d], t[:, :, 0:d], t[:, :, d:2 * d], ALU.add))
                    d //= 2
                done(pool.memset(g_pos, 0.0))
                for b in range(NT):
                    done(pool.tensor_scalar(g_tmp, g_scan[:, z, b, :], g_bef[:, b, 0:1], -1.0, ALU.add, ALU.add))
                    for low in range(b):
                        done(pool.tensor_scalar(g_tmp, g_tmp, g_tot[:, low, 0:1], None, ALU.add))
                    done(pool.tensor_tensor(g_tmp, g_tmp, g_mask[:, b, :], ALU.mult))
                    done(pool.tensor_tensor(g_pos, g_pos, g_tmp, ALU.add))
                done(pool.tensor_copy(g_posi, g_pos))
                with pool.Fori(0, P) as j:
                    pool.tensor_copy(g_col, g_posi[:, bass.ds(j, 1)]).then_inc(g_step, 1)
                    pool.tensor_copy(g_pair, pair_i[:, bass.ds(j, 1), :].rearrange("p o t -> p (o t)")).then_inc(g_step, 1)
                    pool.wait_ge(g_step, j * 2 + (gs[0] + 2))
                    pool.sem_inc(g_go, 1)
                    pool.indirect_dma_start(moved, bass.IndirectOffsetOnAxis(g_col, 0), g_pair, None).then_inc(g_dma, 16)
                    pool.wait_ge(g_dma, j * 16 + (gd[0] + 16))
                    pool.sem_inc(g_go, 1)
                gd[0] += 16 * P
                landed(pool.dma_start(pair_i[:], moved.rearrange("(c j) t -> c j t", j=P)))
            pool.sem_inc(edges_final, 1)

            pool.wait_ge(words_ready, 1)
            for g in range(EC // RING):
                c = slice(g * RING, (g + 1) * RING)
                link(pool.tensor_tensor(ohd[:, c, :], iota[:, 0:P].unsqueeze(1).broadcast_to([P, RING, P]),
                                        dloc[:, c].unsqueeze(2).broadcast_to([P, RING, P]), ALU.subtract))
                pool.tensor_scalar(ohd[:, c, :], ohd[:, c, :], 0.0, None, ALU.is_equal).then_inc(ohd_ready, 1)

            pool.wait_ge(zeroed, 16 * (T1 + 2))
            for k in range(TOP):
                pool.wait_ge(dki_ready, k + 1)
                for i in range(NT):
                    pool.indirect_dma_start(slot_token, bass.IndirectOffsetOnAxis(dki[:, k, i:i + 1], 0), tokf[:, i:i + 1], None,
                                            bounds_check=SLOTS - 1, oob_is_err=False).then_inc(scattered, 16)
            pool.wait_ge(xn_stored, 16)
            pool.wait_ge(idx_ready, 1)

            def gather(u, e, full):
                pool.tensor_copy(colA[:, u:u + 1], idxA[:, bass.ds(e, 1)]).then_inc(col_ready, 1)
                pool.tensor_copy(colB[:, u:u + 1], idxB[:, bass.ds(e, 1)]).then_inc(col_ready, 1)
                pool.wait_ge(col_ready, (e + 1) * 2)
                pool.sem_inc(gather_go, 1)
                pool.indirect_dma_start(xg[:, u, 0:D], None, xn_dram, bass.IndirectOffsetOnAxis(colA[:, u:u + 1], 0)).then_inc(xg_ready[u], 16)

                def second(n):
                    if n > P:
                        pool.indirect_dma_start(xg[0:CB, u, D:2 * D], None, xn_dram,
                                                bass.IndirectOffsetOnAxis(colB[:, u:u + 1], 0)).then_inc(xg_ready[u], 16)
                    else:
                        pool.dma_start(xg[0:1, u, D:D + 16], xn_dram[0:1, 0:16]).then_inc(xg_ready[u], 16)

                by_size(pool, full, second)

            pool.wait_ge(full_ready, 1)
            word = flags(pool, 0)
            for i in range(RING):
                if i >= 2:
                    pool.wait_ge(xt_done, i - 1)
                gather(i % 2, i, bit(word, i))
            with pool.Fori(1, E0 // RING) as g:
                word = flags(pool, g)
                for i in range(RING):
                    pool.wait_ge(xt_done, g * RING + (i - 1))
                    gather(i % 2, g * RING + i, bit(word, i))

            for u in range(2):
                pool.wait_ge(o_stored[u], 32 * (E0 // 2))
            for j in range(NT * TOP):
                i, k = j // TOP, j % TOP
                if j >= 4:
                    pool.wait_ge(gat_used, j - 3)
                pool.indirect_dma_start(gat[:, j % 4, :], None, slot_out, bass.IndirectOffsetOnAxis(gki[:, k, i:i + 1], 0),
                                        bounds_check=SLOTS - 1, oob_is_err=False).then_inc(gat_ready[j % 4], 16)

            pool.wait_ge(d1i_ready, 1)
            for i in range(NT):
                pool.indirect_dma_start(sorted_in, bass.IndirectOffsetOnAxis(d1i[:, i:i + 1], 0), xn[:, i, :], None,
                                        bounds_check=T1 * P - 1, oob_is_err=False).then_inc(scattered1, 16)
            for u in range(2):
                pool.wait_ge(y1_stored[u], 16 * ((T1 + 1 - u) // 2))
            for i in range(NT):
                j = NT * TOP + i
                pool.wait_ge(gat_used, j - 3)
                pool.indirect_dma_start(gat[:, j % 4, :], None, sorted_out, bass.IndirectOffsetOnAxis(d1i[:, i:i + 1], 0),
                                        bounds_check=T1 * P - 1, oob_is_err=False).then_inc(gat_ready[j % 4], 16)

        @block.scalar
        def _(sc):
            def copy(o, i):
                return nc.scalar.activation(o, i, ACT.Copy)

            def evac_transposes(ln):
                if ln == 0:
                    sc.wait_ge(var_ready, 1)
                    nc.scalar.activation(rstd[:], rstd[:], ACT.Sqrt).then_inc(std_ready, 1)
                for i in range(NT):
                    if ln:
                        sc.wait_ge(vart_ready, NT * (ln - 1) + i + 1)
                        nc.scalar.activation(rstd[:, i:i + 1], rstd[:, i:i + 1], ACT.Sqrt).then_inc(stdt_ready, 1)
                    sc.wait_ge(tr_done, NT * ln + i + 1)
                    copy(xnT[:, :, i * P:(i + 1) * P], ps[:, i % 2, :].rearrange("p (k n) -> p k n", k=KD)).then_inc(tr_evac, 1)

            evac_transposes(0)
            sc.wait_ge(ld_bc, 64)
            for i in range(NT + 1):
                if i < NT:
                    sc.wait_ge(h_evac, i + 1)
                    copy(cur0_hi[:, i, :], xn[:, i, :]).then_inc(h_hi, 1)
                if i >= 1:
                    sc.wait_ge(h_lo, i)
                    nc.scalar.activation(xn[:, i - 1, :], xn[:, i - 1, :], ACT.Copy, scale=dwb[:, 0:1]).then_inc(h_term, 1)
            for h in range(2):
                sc.wait_ge(m_done, h + 1)
                for b in range(0, NT, 2):
                    copy(mT[:, b, h * 512:(h + 1) * 512], ps[:, b, :]).then_inc(m_evac_a, 1)
            for a in range(NT):
                sc.wait_ge(mt_done, a + 1)
                q = 2 * (a % 4)
                nc.scalar.activation(S[:, a, :], ps[:, q:q + 2, :].rearrange("p a n -> p (a n)"), ACT.Sign,
                                     accum_out=rsum[:, a:a + 1]).then_inc(adj_ready, 1)
            evac_transposes(1)

            def shared_evac(j):
                f, h = j % 4, j // 4
                sc.wait_ge(sh_done, j + 1)
                g = 4 + 2 * (j % 2)
                nc.scalar.activation(sact[:, f, h * 512:(h + 1) * 512], ps[:, g, :], ACT.Silu).then_inc(sh_sil, 1)

            sc.wait_ge(lgc_ready, 1)
            nc.scalar.activation(tmp, tmp, ACT.Exp).then_inc(ex_ready, 1)
            for j in range(8):
                shared_evac(j)

            def expert(u, e, full):
                def products(n):
                    sc.wait_ge(gu_done, e + 1)
                    nc.scalar.activation(sil[:, u, :].rearrange("p (f n) -> p f n", f=KF)[:, :, 0:n],
                                         ps[:, 2 * u, 0:KF * CAP].rearrange("p (f n) -> p f n", f=KF)[:, :, 0:n], ACT.Silu).then_inc(sil_ready, 1)

                by_size(sc, full, products)

            def expert_out(u, e, stored, full):
                sc.wait_ge(dn_done, e + 1)
                if stored is not None:
                    sc.wait_ge(o_stored[u], stored)
                copy(ob[:, u, 0:D], ps[:, 6, :]).then_inc(oa_ready, 1)
                sc.wait_ge(oa_ready, e + 1)
                nc.scalar.dma_start(slot_out[bass.ds(e * CAP, P), :], ob[:, u, 0:D]).then_inc(o_stored[u], 16)

                def second(n):
                    if n > P:
                        sc.wait_ge(obb_ready, e + 1)
                        nc.scalar.dma_start(slot_out[bass.ds(e * CAP + P, CB), :], ob[0:CB, u, D:2 * D]).then_inc(o_stored[u], 16)
                    else:
                        sc.sem_inc(o_stored[u], 16)

                by_size(sc, full, second)

            sc.wait_ge(full_ready, 1)
            word = flags(sc, 0)
            expert(0, 0, bit(word, 0))

            def step(i, e, stored, word, last=0):
                u = i % 2
                if last < 2:
                    expert(1 - u, e + 1, bit(word, i + 1))
                expert_out(u, e, stored, bit(word, i))

            for i in range(RING):
                step(i, i, 32 * (i // 2) or None, word)
            with sc.Fori(1, E0 // RING - 1) as g:
                word = flags(sc, g)
                for i in range(RING):
                    step(i, g * RING + i, g * 128 + 32 * (i // 2), word)
            word = flags(sc, E0 // RING - 1)
            for i in range(RING):
                e = E0 - RING + i
                step(i, e, 32 * (e // 2), word, last=max(0, i - RING + 3))

            for i in range(NT):
                sc.wait_ge(vart_ready, NT + i + 1)
                nc.scalar.activation(rstd[:, i:i + 1], rstd[:, i:i + 1], ACT.Sqrt).then_inc(stdt_ready, 1)
                sc.wait_ge(tr_done, NT * 2 + i + 1)
                copy(xnT[:, :, i * P:(i + 1) * P], ps[:, i % 2, :].rearrange("p (k n) -> p k n", k=KD)).then_inc(tr_evac, 1)
                sc.wait_ge(be_done, i + 1)
                copy(beta_hi[:, i, :], ps[:, 2 + i % 2, :]).then_inc(be_hi, 1)
            evac_transposes(3)
            for j in range(4):
                f, h = j % 2, j // 2
                sc.wait_ge(s1_done, j + 1)
                nc.scalar.activation(gact[:, f, h * 512:(h + 1) * 512], ps[:, 4 + j % 2, :], ACT.Gelu).then_inc(s1_act, 1)
            expert(0, E0, None)
            for t in range(T1):
                u, e = t % 2, E0 + t
                if t < T1 - 1:
                    expert(1 - u, e + 1, None)
                sc.wait_ge(dn_done, e + 1)
                if t >= 2:
                    sc.wait_ge(y1_stored[u], 16 * (t // 2))
                copy(ob[:, u, 0:D], ps[:, 6, :]).then_inc(oa_ready, 1)
                sc.wait_ge(oa_ready, e + 1)
                nc.scalar.dma_start(sorted_out[t * P:(t + 1) * P, :], ob[:, u, 0:D]).then_inc(y1_stored[u], 16)

        @block.vector
        def _(ve):
            v = nc.vector
            steps = [0, 0]

            def link(ins):
                steps[0] += 1
                ins.then_inc(dve_step, 1)
                ve.wait_ge(dve_step, steps[0])

            def layernorm(ln):
                for i in range(NT):
                    last = v.bn_stats(stats[:, i, :], xres[:, i, :])
                link(last)
                for i in range(NT):
                    last = v.bn_aggr(mv[:, i, :], stats[:, i, :])
                link(last)
                v.tensor_scalar(rstd[:], mv[:, :, 1], EPS, None, ALU.add).then_inc(var_ready, 1)
                ve.wait_ge(std_ready, ln + 1)
                link(v.reciprocal(rstd[:], rstd[:]))
                for i in range(NT):
                    v.tensor_scalar(xn[:, i, :], xres[:, i, :], mv[:, i, 0:1], rstd[:, i:i + 1],
                                    ALU.subtract, ALU.mult).then_inc(xn_ready, 1)

            def layernorm_tile(i):
                link(v.bn_stats(stats[:, i, :], xres[:, i, :]))
                link(v.bn_aggr(mv[:, i, :], stats[:, i, :]))
                steps[1] += 1
                v.tensor_scalar(rstd[:, i:i + 1], mv[:, i, 1:2], EPS, None, ALU.add).then_inc(vart_ready, 1)
                ve.wait_ge(stdt_ready, steps[1])
                link(v.reciprocal(rstd[:, i:i + 1], rstd[:, i:i + 1]))
                v.tensor_scalar(xn[:, i, :], xres[:, i, :], mv[:, i, 0:1], rstd[:, i:i + 1],
                                ALU.subtract, ALU.mult).then_inc(xn_ready, 1)

            def edges_to_float():
                v.tensor_copy(pair_f, pair_i[:].rearrange("c j t -> c t j"))
                link(v.tensor_scalar(blk_i, pair_i[:, :, 1], 7, None, ALU.logical_shift_right))
                link(v.tensor_copy(blk, blk_i))

            ve.wait_ge(ld_edge, 32)
            edges_to_float()
            nxt, n1, n2 = small[:, 0:1], small[:, 1:2], small[:, 2:3]
            link(v.memset(nxt, float(N)))
            link(v.tensor_copy(nxt[0:P - 1], next_i[0:P - 1, 1:2]))
            v.tensor_tensor(n1, pair_f[:, 1, P - 1:P], nxt, ALU.is_gt)
            link(v.tensor_tensor(pick[:, 0:P - 1], blk[:, 0:P - 1], blk[:, 1:P], ALU.is_gt))
            link(v.tensor_reduce(n2, pick[:, 0:P - 1], X, ALU.add))
            link(v.memset(onesf, 1.0))
            v.tensor_tensor(small[:, 3:4], n1, n2, ALU.add).then_inc(vrow_ready, 1)
            ve.wait_ge(vsum_done, 1)
            v.tensor_copy(viol[:], ps[0:1, 7, 0:1]).then_inc(viol_ready, 1)
            ve.wait_ge(ld_x, 16)
            layernorm(0)
            ve.wait_ge(const_ready, 1)
            ve.wait_ge(edges_final, 1)
            edges_to_float()
            v.tensor_scalar(diag, ident[:], blk[:, 0:1], None, ALU.mult)
            for b in range(1, NT):
                link(v.tensor_scalar(pick, blk, float(b), None, ALU.is_lt))
                link(v.tensor_reduce(small[:, 8 + b:9 + b], pick, X, ALU.add))
            v.memset(zerob, 0.0).then_inc(pairf_ready, 1)
            ve.wait_ge(cols_done, 1)
            v.tensor_copy(edge_f, ps[:, 5, 0:2 * P].rearrange("p (t c) -> p t c", t=2))
            v.tensor_copy(lob, ps[:, 6, 0:P])
            link(v.tensor_copy(small[:, 25:32], ps[:, 6, P:P + NT - 1]))
            link(v.scalar_tensor_tensor(dloc, lob, -float(P), edge_f[:, 1, :], ALU.mult, ALU.add))
            link(v.tensor_scalar(pick, lob, 1.0, None, ALU.mult))
            pk = pick.rearrange("p (w i) -> p w i", i=RING)
            for i in range(1, RING):
                last = v.tensor_scalar(pk[:, :, i], pk[:, :, i], float(8 ** i), None, ALU.mult)
            link(last)
            link(v.tensor_reduce(small[:, 32:48], pk, X, ALU.add))
            v.tensor_copy(words[:], small[0:1, 32:48]).then_inc(words_ready, 1)
            def evacuate_h(i):
                ve.wait_ge(h_done, i + 1)
                v.tensor_tensor(xn[:, i, :], ps[:, H_BANKS[i % 4], :], b0b[:], ALU.add).then_inc(h_evac, 1)
                if i >= 1:
                    split_h(i - 1)

            def split_h(i):
                ve.wait_ge(h_hi, i + 1)
                v.tensor_tensor(cur0_lo[:, i, :], xn[:, i, :], cur0_hi[:, i, :].bitcast(F32), ALU.subtract).then_inc(h_lo, 1)

            v.tensor_copy(identr[:], ident[:])
            v.tensor_copy(onesr[:], onesf[:, 0:2])
            ve.wait_ge(ld_bc, 64)
            for i in range(4):
                evacuate_h(i)
            link(v.tensor_copy(small[:, 49:56].bitcast(I32), small[:, 25:32]))
            link(v.tensor_scalar(small[:, 57:64].bitcast(I32), small[:, 49:56].bitcast(I32), 7, None, ALU.logical_shift_right))
            link(v.tensor_copy(small[:, 65:72], small[:, 57:64].bitcast(I32)))
            later = NT - 1
            on, prod = [mT[:, j, 0:later * P].rearrange("p (b c) -> p b c", c=P) for j in range(2)]
            link(v.tensor_tensor(on, iota[:, 0:P].unsqueeze(1).broadcast_to([P, later, P]),
                                 small[:, 65:72].unsqueeze(2).broadcast_to([P, later, P]), ALU.is_equal))
            for j, t in enumerate((edge_f[:, 0, :], edge_f[:, 1, :], lob)):
                link(v.tensor_tensor(prod, on.bitcast(F32), t.unsqueeze(1).broadcast_to([P, later, P]), ALU.mult))
                link(v.tensor_reduce(edge_x[:, j, 1:NT], prod.bitcast(F32), X, ALU.add))
            x_dst, x_own = edge_x[:, 1, 1:NT], edge_x[:, 2, 1:NT]
            v.tensor_tensor(x_own, x_own, iota[:, 1:NT], ALU.is_equal)
            link(v.scalar_tensor_tensor(x_dst, iota[:, 1:NT], -float(P), x_dst, ALU.mult, ALU.add))
            link(v.scalar_tensor_tensor(x_dst, x_own, float(8 * N), x_dst, ALU.mult, ALU.add))
            for i in range(4, NT):
                evacuate_h(i)
            split_h(NT - 1)

            def onehot_src(u, h, s_):
                v.tensor_scalar(ohs[:, u, :], iota[:, h * 512:(h + 1) * 512], s_, None, ALU.is_equal).then_inc(oh_ready, 1)

            for h in range(2):
                for b in range(1, NT):
                    if h:
                        ve.wait_ge(oh_used, OHS + HEAD)
                    else:
                        v.tensor_scalar(ohx[:, b, :], iota[:, 0:P], edge_x[:, 1, b:b + 1], None, ALU.is_equal)
                    onehot_src(b, h, edge_x[:, 0, b:b + 1])
                with ve.Fori(0, EC // OHB) as g:
                    for u in range(OHB):
                        if u % 4 == 0:
                            ve.wait_ge(oh_used, g * OHB + (u + 4 + NT - OHB + HEAD + h * OHS))
                        onehot_src((NT + u) % OHB, h, edge_f[:, 0, bass.ds(g * OHB + u, 1)])
                ve.wait_ge(m_done, h + 1)
                for b in range(1, NT, 2):
                    v.tensor_copy(mT[:, b, h * 512:(h + 1) * 512], ps[:, b, :]).then_inc(m_evac_v, 1)
            for a in range(NT):
                ve.wait_ge(adj_ready, a + 1)
                own = S[:, a, a * P:(a + 1) * P]
                v.tensor_tensor(own, own.bitcast(F32), ident[:], ALU.add).then_inc(s_ready, 1)
            link(v.tensor_scalar(rsum[:], rsum[:], 1.0, 1.0, ALU.add, ALU.max))
            link(v.reciprocal(rsum[:], rsum[:]))
            for t in range(STEPS):
                last = v.tensor_scalar(wr[:, t, :], rsum[:], dwb[:, t + 1:t + 2], None, ALU.mult)
            link(last)
            ve.wait_ge(h_term, NT)
            ve.wait_ge(zeroed, 16 * (T1 + 2))
            for t in range(STEPS):
                for m in range(NT):
                    ve.wait_ge(s_done, t * NT + m + 1)
                    if t < STEPS - 1:
                        hi, lo = cur[(t + 1) % 2]
                        link(v.tensor_scalar(hi[:, m, :], ps[:, m, :], rsum[:, m:m + 1], None, ALU.mult))
                        v.scalar_tensor_tensor(lo[:, m, :], ps[:, m, :], rsum[:, m:m + 1], hi[:, m, :].bitcast(F32), ALU.mult, ALU.subtract)
                    v.scalar_tensor_tensor(xn[:, m, :], ps[:, m, :], wr[:, t, m:m + 1], xn[:, m, :], ALU.mult, ALU.add).then_inc(s_evac, 1)
                    if t == STEPS - 1:
                        ve.wait_ge(s_evac, t * NT + m + 1)
                        link(v.scalar_tensor_tensor(xres[:, m, :], xn[:, m, :], 0.0, xres[:, m, :], ALU.max, ALU.add))
                        layernorm_tile(m)

            def bc(t):
                return t.unsqueeze(2).broadcast_to([P, NT, E0])

            def seg_sum(o, t):
                return v.tensor_reduce(o, by_e(t), X, ALU.add)

            ve.wait_ge(lg_done, 1)
            link(v.tensor_tensor(by_e(tmp), ps[:, 2, :].rearrange("p (i e) -> p i e", e=E0),
                                 rb[:].unsqueeze(1).broadcast_to([P, NT, E0]), ALU.add))
            link(v.tensor_reduce(red[:, 0, :], by_e(tmp), X, ALU.max))
            v.tensor_tensor(by_e(tmp), by_e(tmp), bc(red[:, 0, :]), ALU.subtract).then_inc(lgc_ready, 1)
            ve.wait_ge(ex_ready, 1)
            link(seg_sum(red[:, 1, :], tmp))
            link(v.reciprocal(red[:, 1, :], red[:, 1, :]))
            link(v.tensor_tensor(by_e(prob), by_e(tmp), bc(red[:, 1, :]), ALU.mult))
            for i in range(NT):
                last = v.max(top8[:, i, :], prob[:, i * E0:(i + 1) * E0])
            link(last)
            sixth = bc(top8[:, :, TOP - 1])
            v.tensor_tensor(by_e(dest), by_e(prob), sixth, ALU.is_gt)
            link(v.tensor_tensor(by_e(tmp), by_e(prob), sixth, ALU.is_equal))
            link(seg_sum(red[:, 2, :], dest))
            v.tensor_scalar(red[:, 2, :], red[:, 2, :], -1.0, float(TOP), ALU.mult, ALU.add)
            link(v.tensor_tensor_scan(csel, segs[:], tmp, 0.0, ALU.mult, ALU.add))
            link(v.tensor_tensor(by_e(csel), by_e(csel), bc(red[:, 2, :]), ALU.is_le))
            link(v.tensor_tensor(tmp, tmp, csel, ALU.mult))
            link(v.tensor_tensor(sel, dest, tmp, ALU.add))
            v.tensor_copy(selb, sel).then_inc(sel_ready, 1)
            v.tensor_tensor_scan(csel, segs[:], sel, 0.0, ALU.mult, ALU.add)
            link(v.tensor_tensor(gate, prob, sel, ALU.mult))
            link(seg_sum(red[:, 3, :], gate))
            link(v.tensor_scalar(red[:, 3, :], red[:, 3, :], 1e-9, None, ALU.add))
            link(v.reciprocal(red[:, 3, :], red[:, 3, :]))
            link(v.tensor_tensor(by_e(gate), by_e(gate), bc(red[:, 3, :]), ALU.mult))
            def shared_mul(j):
                ve.wait_ge(sh_sil, j + 1)
                blk = sact[:, j % 4, j // 4 * 512:(j // 4 + 1) * 512]
                v.tensor_tensor(blk, blk, ps[:, 5 + 2 * (j % 2), :], ALU.mult).then_inc(sh_act, 1)

            shared_mul(0)
            shared_mul(1)
            ve.wait_ge(rank_done, 1)
            link(v.tensor_copy(rank_t, ps[:, 3, :]))
            link(v.tensor_scalar(tmp, rank_t, float(CAP), None, ALU.is_ge))
            v.tensor_tensor(by_e(dest), by_e(rank_t), ebase[:].unsqueeze(1).broadcast_to([P, NT, E0]), ALU.add)
            link(v.tensor_scalar(prob, tmp, -1.0, 1.0, ALU.mult, ALU.add))
            v.tensor_tensor(gate, gate, prob, ALU.mult)
            link(v.scalar_tensor_tensor(dest, tmp, FAR, dest, ALU.mult, ALU.add))
            for k in range(TOP):
                link(v.scalar_tensor_tensor(tmp, csel, float(k + 1), sel, ALU.is_equal, ALU.mult))
                v.tensor_tensor(prob, tmp, dest, ALU.mult)
                link(v.tensor_tensor(rank_t, tmp, gate, ALU.mult))
                link(seg_sum(dk[:, k, :], prob))
                seg_sum(gk[:, k, :], rank_t)
                v.tensor_copy(dki[:, k, :], dk[:, k, :]).then_inc(dki_ready, 1)
            link(v.tensor_scalar(prob[:, 0:TOP * NT], dk[:].rearrange("p k i -> p (k i)"), float(SLOTS), None, ALU.is_lt))
            link(v.tensor_tensor(prob[:, 0:TOP * NT], prob[:, 0:TOP * NT], dk[:].rearrange("p k i -> p (k i)"), ALU.mult))
            link(v.tensor_copy(gki[:].rearrange("p k i -> p (k i)"), prob[:, 0:TOP * NT]))
            v.memset(t1row[:, 0:1, :], 0.0)
            link(v.memset(utmp_full[:, E0:E0 + 8], 0.0))
            link(v.tensor_scalar(utmp_full[:, 0:E0], ps[:, 2, 0:E0], float(P), None, ALU.is_gt))
            fw = t1row[:, 0, 0:E0 // RING]
            for i in range(RING + 2):
                src = utmp_full[:, i:i + E0 - RING + 1:RING]
                link(v.scalar_tensor_tensor(fw, src, float(2 ** i), fw, ALU.mult, ALU.add))
            v.tensor_copy(fullw[:], fw[0:1, :]).then_inc(full_ready, 1)
            ve.wait_ge(cnt_done, 1)
            v.tensor_copy(cnt[:], ps[:, 0, 0:2 * NT].rearrange("p (a o) -> p a o", o=2)[:, :, 0]).then_inc(cnt_ready, 1)
            for j in range(2, 8):
                shared_mul(j)
            for i in range(NT):
                ve.wait_ge(shd_done, i + 1)
                v.scalar_tensor_tensor(xres[:, i, :], ps[:, 4 + i % 4, :], 1.0 / SH, xres[:, i, :], ALU.mult, ALU.add).then_inc(shd_evac, 1)
                if i == NT // 2 - 1:
                    ve.wait_ge(tki_tr, 1)
                    v.tensor_copy(idxA[:], ps[:, 2, 0:E0])
                    v.tensor_copy(idxB[:], ps[0:CB, 2, E0:2 * E0]).then_inc(idx_ready, 1)

            def xt_evacuate(u, e, full):
                def rows_of(n):
                    ve.wait_ge(xt_done, e + 1)
                    v.tensor_copy(xT[:, u, :].rearrange("p (b k n) -> p b k n", b=2, k=2)[:, :, :, 0:n],
                                  ps[:, 4:6, 0:2 * CAP].rearrange("p b (k n) -> p b k n", k=2)[:, :, :, 0:n]).then_inc(xt_evac, 1)

                by_size(ve, full, rows_of)

            def multiply(u, e, full):
                def products(n):
                    ve.wait_ge(sil_ready, e + 1)
                    v.tensor_tensor(act[:, u, :, 0:n], sil[:, u, :].rearrange("p (f n) -> p f n", f=KF)[:, :, 0:n],
                                    ps[:, 2 * u + 1, 0:KF * CAP].rearrange("p (f n) -> p f n", f=KF)[:, :, 0:n], ALU.mult).then_inc(act_ready, 1)

                by_size(ve, full, products)

            def second_out(u, e, stored, full):
                def rows_of(n):
                    if n > P:
                        ve.wait_ge(dn_done, e + 1)
                        if stored is not None:
                            ve.wait_ge(o_stored[u], stored)
                        v.tensor_copy(ob[0:CB, u, D:2 * D], ps[0:CB, 7, :]).then_inc(obb_ready, 1)
                    else:
                        ve.sem_inc(obb_ready, 1)

                by_size(ve, full, rows_of)

            word = flags(ve, 0)
            xt_evacuate(0, 0, bit(word, 0))
            xt_evacuate(1, 1, bit(word, 1))
            multiply(0, 0, bit(word, 0))

            def step(i, e, stored, word, last=0):
                u = i % 2
                if last < 2:
                    multiply(1 - u, e + 1, bit(word, i + 1))
                if last < 1:
                    xt_evacuate(u, e + 2, bit(word, i + 2))
                second_out(u, e, stored, bit(word, i))

            for i in range(RING):
                step(i, i, 32 * (i // 2) or None, word)
            with ve.Fori(1, E0 // RING - 1) as g:
                word = flags(ve, g)
                for i in range(RING):
                    step(i, g * RING + i, g * 128 + 32 * (i // 2), word)
            word = flags(ve, E0 // RING - 1)
            for i in range(RING):
                e = E0 - RING + i
                step(i, e, 32 * (e // 2), word, last=max(0, i - RING + 3))

            ve.wait_ge(cnt_ready, 1)
            v.reciprocal(cnt[:], cnt[:])

            def add_alpha(i):
                ve.wait_ge(al_done, i + 1)
                v.tensor_tensor(xres[:, i, :], xres[:, i, :], ps[:, 4 + i % 2, :], ALU.add).then_inc(al_evac, 1)
                ve.wait_ge(al_evac, i + 1)
                link(v.tensor_tensor(xres[:, i, :], xres[:, i, :], b1b[:], ALU.add))

            def split_beta(i):
                ve.wait_ge(be_hi, i + 1)
                v.tensor_tensor(beta_lo[:, i, :], ps[:, 2 + i % 2, :], beta_hi[:, i, :].bitcast(F32), ALU.subtract).then_inc(be_evac, 1)

            for i in range(NT):
                for k in range(TOP):
                    j = i * TOP + k
                    ve.wait_ge(gat_ready[j % 4], 16 * (j // 4 + 1))
                    if k >= 1:
                        ve.wait_ge(gat_used, j)
                    v.scalar_tensor_tensor(xres[:, i, :], gat[:, j % 4, :], gk[:, k, i:i + 1], xres[:, i, :], ALU.mult, ALU.add).then_inc(gat_used, 1)
                ve.wait_ge(gat_used, (i + 1) * TOP)
                layernorm_tile(i)
                if i >= 1:
                    split_beta(i - 1)
                    add_alpha(i - 1)

            split_beta(NT - 1)
            add_alpha(NT - 1)
            for i in range(NT):
                ve.wait_ge(ga_done, i + 1)
                v.scalar_tensor_tensor(xres[:, i, :], ps[:, 6 + i % 2, :], cnt[:, i:i + 1], xres[:, i, :], ALU.mult, ALU.add).then_inc(ga_evac, 1)
                ve.wait_ge(ga_evac, i + 1)
                layernorm_tile(i)

            W8 = NT * E1
            def t8(t):
                return t[:, 0:W8].rearrange("p (i e) -> p i e", e=E1)
            def bc8(t):
                return t.unsqueeze(2).broadcast_to([P, NT, E1])
            lg, one, cum, place = utmp[:, 0, 0:64], utmp[:, 0, 64:128], utmp[:, 0, 128:192], utmp[:, 0, 192:256]
            oneb = utmp[:, 0, 256:288].bitcast(BF16)
            ve.wait_ge(lg1_done, 1)
            link(v.tensor_copy(lg, ps[:, 2, 0:W8]))
            link(v.tensor_reduce(red[:, 0, :], t8(lg), X, ALU.max))
            link(v.tensor_tensor(t8(one), t8(lg), bc8(red[:, 0, :]), ALU.is_equal))
            link(v.tensor_tensor_scan(cum, segs8[:], one, 0.0, ALU.mult, ALU.add))
            link(v.scalar_tensor_tensor(one, cum, 1.0, one, ALU.is_equal, ALU.mult))
            v.tensor_copy(oneb, one).then_inc(sel1_ready, 1)
            ve.wait_ge(rank1_done, 1)
            r0, r1, r2, num = [t1row[:, j, :] for j in range(4)]
            link(v.tensor_copy(r0[:, 0:E1], ps[:, 3, W8:W8 + E1]))
            ge = utmp[:, 1, 0:64].rearrange("p (e t) -> p e t", t=8)
            link(v.tensor_scalar(r2[:, 0:8], num[:, 0:8], float(P), None, ALU.mult))
            link(v.tensor_tensor(ge, r0[:, 0:E1].unsqueeze(2).broadcast_to([P, E1, 8]), r2[:, 0:8].unsqueeze(1).broadcast_to([P, E1, 8]), ALU.is_gt))
            link(v.tensor_reduce(r0[:, 0:E1], ge, X, ALU.add))
            link(v.memset(r1[:, 0:E1], 1.0))
            link(v.tensor_tensor_scan(r2[:, 0:E1], r1[:, 0:E1], r0[:, 0:E1], 0.0, ALU.mult, ALU.add))
            link(v.tensor_tensor(r0[:, 0:E1], r2[:, 0:E1], r0[:, 0:E1], ALU.subtract))
            link(v.tensor_scalar(r0[:, 0:E1], r0[:, 0:E1], float(P), None, ALU.mult))
            link(v.tensor_tensor(t8(place), ps[:, 3, 0:W8].rearrange("p (i e) -> p i e", e=E1), r0[:, 0:E1].unsqueeze(1).broadcast_to([P, NT, E1]), ALU.add))
            link(v.tensor_tensor(place, place, one, ALU.mult))
            link(v.tensor_reduce(d1[:], t8(place), X, ALU.add))
            v.tensor_copy(d1i[:], d1[:]).then_inc(d1i_ready, 1)
            te = utmp[:, 1, 128:256].rearrange("p (t e) -> p t e", e=E1)
            link(v.tensor_tensor(te, r2[:, 0:E1].unsqueeze(1).broadcast_to([P, 16, E1]), num.unsqueeze(2).broadcast_to([P, 16, E1]), ALU.is_le))
            link(v.tensor_reduce(r1, te, X, ALU.add))
            link(v.tensor_scalar(r1, r1, float(E1 - 1), None, ALU.min))
            v.tensor_copy(t1e[:], r1[0:1, :]).then_inc(t1_ready, 1)
            for i in range(NT):
                ve.wait_ge(s2_done, i + 1)
                v.tensor_tensor(xres[:, i, :], xres[:, i, :], ps[:, 6 + i % 2, :], ALU.add).then_inc(s2_evac, 1)
            xt_evacuate(0, E0, None)
            xt_evacuate(1, E0 + 1, None)
            multiply(0, E0, None)
            for t in range(T1):
                if t < T1 - 1:
                    multiply((t + 1) % 2, E0 + t + 1, None)
                if t < T1 - 2:
                    xt_evacuate(t % 2, E0 + t + 2, None)
            ve.wait_ge(s2_evac, NT)
            for i in range(NT):
                j = NT * TOP + i
                ve.wait_ge(gat_ready[j % 4], 16 * (j // 4 + 1))
                v.tensor_tensor(xres[:, i, :], xres[:, i, :], gat[:, j % 4, :], ALU.add).then_inc(out_ready, 1)
                ve.wait_ge(out_ready, i + 1)
                v.tensor_copy(red[:, 5, 0:1], red[:, 0, 0:1]).then_inc(gat_used, 1)

        @block.tensor
        def _(pe):
            t_ = nc.tensor

            def mm(o, l, r, start, stop):
                return t_.matmul(o, l, r, start=start, stop=stop)

            def tokens(k, i):
                return xnT[:, k, i * P:(i + 1) * P]

            def transpose_rows(ln, i):
                pe.wait_ge(xn_ready, NT * ln + i + 1)
                if i >= 2:
                    pe.wait_ge(tr_evac, NT * ln + i - 1)
                for k in range(KD):
                    last = t_.transpose(ps[:, i % 2, k * P:(k + 1) * P], xn[:, i, k * P:(k + 1) * P], ident[:])
                last.then_inc(tr_done, 1)

            pe.wait_ge(const_ready, 1)
            pe.wait_ge(vrow_ready, 1)
            mm(ps[:, 7, 0:1], onesf, small[:, 3:4], True, True).then_inc(vsum_done, 1)
            for i in range(NT):
                transpose_rows(0, i)
            pe.wait_ge(ld_w0, 16)
            pe.wait_ge(viol_ready, 1)
            for i in range(NT):
                pe.wait_ge(tr_evac, i + 1)
                if i >= 4:
                    pe.wait_ge(h_evac, i - 3)
                for k in range(KD):
                    last = mm(ps[:, H_BANKS[i % 4], :], tokens(k, i), w0s[:, k, :], k == 0, k == KD - 1)
                last.then_inc(h_done, 1)
                if i == 1:
                    pe.wait_ge(pairf_ready, 1)
                    for t in range(2):
                        t_.transpose(ps[:, 5, t * P:(t + 1) * P], pair_f[:, t, :], ident[:])
                    mm(ps[:, 6, 0:P], onesf, diag, True, True)
                    mm(ps[:, 6, P:P + NT - 1], onesf, small[:, 9:16], True, True).then_inc(cols_done, 1)

            pe.wait_ge(h_evac, NT)

            def outer(dst, src, out_, first):
                return t_.matmul(out_, dst, src, start=first, stop=False, skip_group_check=True).then_inc(oh_used, 1)

            pe.wait_ge(words_ready, 1)
            for h in range(2):
                if h == 1:
                    pe.wait_ge(m_evac_a, NT // 2)
                    pe.wait_ge(m_evac_v, NT // 2)
                base = h * (OHS - 1)
                t_.matmul(ps[:, 0, :], zerob, iota[:, 0:512], start=True, stop=False, skip_group_check=True).then_inc(oh_used, 1 if h else 1 + HEAD)
                for b in range(1, NT):
                    pe.wait_ge(oh_ready, base + b)
                    outer(ohx[:, b, :], ohs[:, b, :], ps[:, b, :], True)
                with pe.Fori(0, EC // GROUP) as g:
                    _, group_words = nc.values_load_multi_w_load_instructions(
                        words[0:1, bass.ds(g * (GROUP // RING), GROUP // RING)], engines=[mybir.EngineType.PE], min_val=0, max_val=8 ** RING - 1)
                    for u in range(GROUP):
                        if u % 4 == 0:
                            pe.wait_ge(oh_ready, g * GROUP + (base + NT + u + 3))
                            if h == 0 and u % RING == 0:
                                pe.wait_ge(ohd_ready, g * (GROUP // RING) + (u // RING + 1))
                        bank = (group_words[u // RING] // 8 ** (u % RING)) % 8
                        outer(ohd[:, bass.ds(g * GROUP + u, 1), :].rearrange("p o n -> p (o n)"), ohs[:, (NT + u) % OHB, :],
                              ps[:, bass.ds(bank, 1), :].rearrange("p o n -> p (o n)"), False)
                t_.matmul(ps[:, 0, 0:8], zerob, zerob[:, 0:8], start=False, stop=True, skip_group_check=True).then_inc(m_done, 1)
            pe.wait_ge(m_evac_a, NT)
            pe.wait_ge(m_evac_v, NT)
            for a in range(NT):
                if a >= 4:
                    pe.wait_ge(adj_ready, a - 3)

                def add(o, l, r, start, stop):
                    return t_.matmul(o, l, r, start=start, stop=stop, skip_group_check=True)

                q = 2 * (a % 4)
                for h in range(2):
                    add(ps[:, q + h, :], identr[:], mT[:, a, h * 512:(h + 1) * 512], True, False)
                    for b in range(4 * h, 4 * h + 4):
                        last = add(ps[:, q + h, (b % 4) * P:(b % 4 + 1) * P], mT[:, b, a * P:(a + 1) * P], identr[:], False, b % 4 == 3)
                last.then_inc(mt_done, 1)
            def router(i):
                pe.wait_ge(s_evac, (STEPS - 1) * NT + 3)
                pe.wait_ge(tr_evac, NT + i + 1)
                for k in range(KD):
                    last = mm(ps[:, 2, i * E0:(i + 1) * E0], tokens(k, i), rw[:, k, :], k == 0, k == KD - 1)
                return last

            pe.wait_ge(ld_small, 32)
            pe.wait_ge(s_ready, NT)
            pe.wait_ge(h_lo, NT)
            for t in range(STEPS):
                if t >= 1:
                    pe.wait_ge(s_evac, t * NT)
                for m in range(NT):
                    for k in range(NT):
                        for part in range(2):
                            last = mm(ps[:, m, :], S[:, k, m * P:(m + 1) * P], cur[t % 2][part][:, k, :], k + part == 0, k + part == NT)
                    last.then_inc(s_done, 1)
                    if t == STEPS - 1 and m >= 1:
                        transpose_rows(1, m - 1)
                    if t == STEPS - 1 and m >= 4:
                        router(m - 4)
            transpose_rows(1, NT - 1)
            for i in range(NT - 4, NT):
                last = router(i)
            last.then_inc(lg_done, 1)
            pe.wait_ge(s_evac, STEPS * NT)

            def shared(j):
                f, h = j % 4, j // 4
                if j >= 2:
                    pe.wait_ge(sh_act, j - 1)
                for w, g in ((sg, 4 + 2 * (j % 2)), (su, 5 + 2 * (j % 2))):
                    for k in range(KD):
                        last = mm(ps[:, g, :], w[:, k, f * P:(f + 1) * P], xnT[:, k, h * 512:(h + 1) * 512], k == 0, k == KD - 1)
                last.then_inc(sh_done, 1)

            pe.wait_ge(ld_shared, 48)
            for j in range(2):
                shared(j)
            pe.wait_ge(sel_ready, 1)
            selm = selb.rearrange("p (i e) -> p i e", e=E0)
            for i in range(NT):
                for j in range(i):
                    mm(ps[:, 3, i * E0:(i + 1) * E0], ones[:], selm[:, j, :], j == 0, False)
                mm(ps[:, 3, i * E0:(i + 1) * E0], tri[:], selm[:, i, :], i == 0, True)
            for i in range(NT):
                last = mm(ps[:, 2, 0:E0], ones[:], selm[:, i, :], i == 0, i == NT - 1)
            last.then_inc(rank_done, 1)
            for a in range(NT):
                for b in range(NT):
                    last = mm(ps[:, 0, 2 * a:2 * a + 2], mT[:, b, a * P:(a + 1) * P], onesr[:], b == 0, b == NT - 1)
            last.then_inc(cnt_done, 1)
            for j in range(2, 8):
                shared(j)
            pe.wait_ge(sh_act, 8)
            for i in range(NT):
                if i >= 4:
                    pe.wait_ge(shd_evac, i - 3)
                for k in range(4):
                    last = mm(ps[:, 4 + i % 4, :], sact[:, k, i * P:(i + 1) * P], sd[:, k, :], k == 0, k == 3)
                last.then_inc(shd_done, 1)
                if i == NT // 2 - 1:
                    pe.wait_ge(full_ready, 1)
                    pe.wait_ge(tki_loaded, 16)
                    t_.transpose(ps[:, 2, 0:E0], tki[:, 0:P], ident[0:E0, 0:E0])
                    t_.transpose(ps[0:CB, 2, E0:2 * E0], tki[:, P:CAP], ident[0:E0, 0:E0]).then_inc(tki_tr, 1)
            pe.wait_ge(cnt_ready, 1)
            pe.wait_ge(shd_evac, NT)
            pe.wait_ge(idx_ready, 1)

            def turn(u, e, n, first, full):
                pe.wait_ge((x1_ready if full is None else xg_ready)[u], n)
                if not first:
                    pe.wait_ge(xt_evac, e)
                def rows_of(n):
                    for k in range(KD):
                        o = (k % 2) * CAP
                        last = t_.transpose(ps[:, 4 + k // 2, o:o + P], xg[:, u, k * P:(k + 1) * P], ident[:])
                        if n > P:
                            last = t_.transpose(ps[:, 4 + k // 2, o + P:o + CAP], xg[0:CB, u, D + k * P:D + (k + 1) * P], ident[0:CB, 0:CB])
                    last.then_inc(xt_done, 1)

                by_size(pe, full, rows_of)

            def gate_up(u, e, n, full):
                pe.wait_ge(wgu_ready[u], n)
                pe.wait_ge(xt_evac, e + 1)
                def products(n):
                    for g in range(2):
                        for f in range(KF):
                            for k in range(KD):
                                last = mm(ps[:, 2 * u + g, f * CAP:f * CAP + n],
                                          ring[:, u, (g * KD + k) * F + f * P:(g * KD + k) * F + (f + 1) * P],
                                          xT[:, u, k * CAP:k * CAP + n], k == 0, k == KD - 1)
                    last.then_inc(gu_done, 1)

                by_size(pe, full, products)

            def down(u, e, n, first, full):
                pe.wait_ge(act_ready, e + 1)
                pe.wait_ge(wd_ready[u], n)
                if not first:
                    pe.wait_ge(oa_ready, e)
                    if full is not None:
                        pe.wait_ge(obb_ready, e)
                def products(n):
                    for o, lo, hi in ((6, 0, P), (7, P, CAP)):
                        if lo < n:
                            for f in range(KF):
                                last = mm(ps[0:hi - lo, o, :], act[:, u, f, lo:hi],
                                          ring[:, u, GU + f * D:GU + (f + 1) * D], f == 0, f == KF - 1)
                    last.then_inc(dn_done, 1)

                by_size(pe, full, products)

            pe.wait_ge(full_ready, 1)
            word = flags(pe, 0)
            turn(0, 0, 32, True, bit(word, 0))
            turn(1, 1, 32, False, bit(word, 1))
            gate_up(0, 0, 16, bit(word, 0))

            def step(i, e, gu_n, turn_n, down_n, word, first=False, last=0):
                u = i % 2
                if last < 2:
                    gate_up(1 - u, e + 1, gu_n, bit(word, i + 1))
                if last < 1:
                    turn(u, e + 2, turn_n, False, bit(word, i + 2))
                down(u, e, down_n, first, bit(word, i))

            for i in range(RING):
                step(i, i, 16 * ((i + 1) // 2 + 1), 32 * (i // 2 + 2), 16 * (i // 2 + 1), word, first=i == 0)
            with pe.Fori(1, E0 // RING - 1) as g:
                word = flags(pe, g)
                for i in range(RING):
                    step(i, g * RING + i, g * 64 + 16 * ((i + 1) // 2 + 1), g * 128 + 32 * (i // 2 + 2), g * 64 + 16 * (i // 2 + 1), word)
            word = flags(pe, E0 // RING - 1)
            for i in range(RING):
                e = E0 - RING + i
                step(i, e, 16 * ((e + 1) // 2 + 1), 32 * (e // 2 + 2), 16 * (e // 2 + 1), word, last=max(0, i - RING + 3))

            pe.wait_ge(ld_c, 32)
            pe.wait_ge(obb_ready, E0)
            pe.wait_ge(oa_ready, E0)
            for i in range(NT):
                transpose_rows(2, i)
                pe.wait_ge(tr_evac, 2 * NT + i + 1)
                if i >= 2:
                    pe.wait_ge(be_evac, i - 1)
                for k in range(KD):
                    last = mm(ps[:, 2 + i % 2, :], tokens(k, i), wns[:, k, :], k == 0, k == KD - 1)
                last.then_inc(be_done, 1)
                if i >= 2:
                    pe.wait_ge(al_evac, i - 1)
                for k in range(KD):
                    last = mm(ps[:, 4 + i % 2, :], tokens(k, i), wcs[:, k, :], k == 0, k == KD - 1)
                last.then_inc(al_done, 1)
            pe.wait_ge(be_evac, NT)
            for i in range(NT):
                if i >= 2:
                    pe.wait_ge(ga_evac, i - 1)
                for b in range(NT):
                    for part, beta in enumerate((beta_hi, beta_lo)):
                        last = mm(ps[:, 6 + i % 2, :], mT[:, b, i * P:(i + 1) * P], beta[:, b, :], b + part == 0, b + part == NT)
                last.then_inc(ga_done, 1)
                if i >= 1:
                    transpose_rows(3, i - 1)
            transpose_rows(3, NT - 1)

            for i in range(NT):
                pe.wait_ge(tr_evac, 3 * NT + i + 1)
                for k in range(KD):
                    last = mm(ps[:, 2, i * E1:(i + 1) * E1], tokens(k, i), gw[:, k, :], k == 0, k == KD - 1)
            last.then_inc(lg1_done, 1)
            pe.wait_ge(ld_s1, 32)
            pe.wait_ge(al_evac, NT)
            for j in range(4):
                f, h = j % 2, j // 2
                if j >= 2:
                    pe.wait_ge(s1_act, j - 1)
                for k in range(KD):
                    last = mm(ps[:, 4 + j % 2, :], s1w[:, k, f * P:(f + 1) * P], xnT[:, k, h * 512:(h + 1) * 512], k == 0, k == KD - 1)
                last.then_inc(s1_done, 1)
            pe.wait_ge(sel1_ready, 1)
            onem = utmp[:, 0, 256:288].bitcast(BF16).rearrange("p (i e) -> p i e", e=E1)
            for i in range(NT):
                for j in range(i):
                    mm(ps[:, 3, i * E1:(i + 1) * E1], ones[:], onem[:, j, :], j == 0, False)
                mm(ps[:, 3, i * E1:(i + 1) * E1], tri[:], onem[:, i, :], i == 0, True)
            for j in range(NT):
                last = mm(ps[:, 3, NT * E1:NT * E1 + E1], ones[:], onem[:, j, :], j == 0, j == NT - 1)
            last.then_inc(rank1_done, 1)
            pe.wait_ge(s1_act, 4)
            pe.wait_ge(ga_evac, NT)
            for i in range(NT):
                if i >= 2:
                    pe.wait_ge(s2_evac, i - 1)
                for f in range(KF):
                    last = mm(ps[:, 6 + i % 2, :], gact[:, f, i * P:(i + 1) * P], s2w[:, f, :], f == 0, f == KF - 1)
                last.then_inc(s2_done, 1)
            pe.wait_ge(s2_evac, NT)
            uses = E0 // 2
            turn(0, E0, 16, False, None)
            turn(1, E0 + 1, 16, False, None)
            gate_up(0, E0, 16 * (uses + 1), None)
            for t in range(T1):
                u, e = t % 2, E0 + t
                if t < T1 - 1:
                    gate_up(1 - u, e + 1, 16 * (uses + (t + 1) // 2 + 1), None)
                if t < T1 - 2:
                    turn(u, e + 2, 16 * (t // 2 + 2), False, None)
                down(u, e, 16 * (uses + t // 2 + 1), False, None)


def kernel(**inputs):
    import numpy as np
    import concourse.bacc as bacc
    from concourse.bass_utils import run_bass_kernel_spmd

    a = {k: np.asarray(v) for k, v in inputs.items()}

    def chunked(w):
        e, k, m = w.shape
        return w.reshape(e, k // P, P, m).transpose(0, 2, 1, 3).reshape(e, P, -1)

    def turned(w):
        return w.transpose(0, 2, 1)

    arrays = {
        "x": a["x"],
        "pairs": np.stack([a["src"], a["dst"]], axis=1),
        "w0": a["L0_gnn_W"], "b0": a["L0_gnn_b"], "dw": a["L0_gnn_diffusion_weights"],
        "rwT": a["L0_ffn_router_w"].T, "rbias": a["L0_ffn_bias"],
        "sgT": a["L0_ffn_shared_w_gate"].reshape(SH * F, D).T,
        "suT": a["L0_ffn_shared_w_up"].reshape(SH * F, D).T,
        "sdT": turned(a["L0_ffn_shared_w_down"]).reshape(SH * F, D),
        "we0": np.concatenate([chunked(turned(a["L0_ffn_w_gate"])), chunked(turned(a["L0_ffn_w_up"])),
                               chunked(turned(a["L0_ffn_w_down"]))], axis=2),
        "wc": a["L1_gnn_wc"], "wn": a["L1_gnn_wn"], "b1": a["L1_gnn_bias"],
        "gwT": a["L1_ffn_gate_w"].T,
        "we1": np.concatenate([chunked(turned(a["L1_ffn_w1"])), chunked(turned(a["L1_ffn_w3"])),
                               chunked(turned(a["L1_ffn_w2"]))], axis=2),
        "sw1T": a["L1_ffn_sw1"].T, "sw2T": a["L1_ffn_sw2"].T,
    }
    arrays = {f"in_{k}": np.ascontiguousarray(v) for k, v in arrays.items()}
    nc = bacc.Bacc("TRN2", target_bir_lowering=False, num_devices=1)
    args = [nc.dram_tensor(k, v.shape, mybir.dt.from_np(v.dtype), kind="ExternalInput").ap() for k, v in arrays.items()]
    args.append(nc.dram_tensor("out", (N, D), F32, kind="ExternalOutput").ap())
    build(nc, *args)
    r = run_bass_kernel_spmd(nc, [arrays], core_ids=[0])
    return r.results[0]["out"]
```

```python
from contextlib import ExitStack

import concourse.bass as bass
from concourse import mybir

ALU = mybir.AluOpType
ACT = mybir.ActivationFunctionType
F32 = mybir.dt.float32
F32R = mybir.dt.float32r
F16 = mybir.dt.float16
BF16 = mybir.dt.bfloat16
I32 = mybir.dt.int32
U32 = mybir.dt.uint32
X = mybir.AxisListType.X

P = 128
N = 1024
D = 512
NT = N // P
KD = D // P
NE = 16384
EC = NE // P
GROUP = 64
POOL_ROWS = 12
OHB = 16
HEAD = 5
RING = 8
STEPS = 3
OHS = NT + EC
E0 = 64
TOP = 6
CAP = N * TOP * 2 // E0
CB = CAP - P
FEW = P // 2
SLOTS = E0 * CAP
F = 256
KF = F // P
GU = 2 * KD * F
WROW = GU + KF * D
SH = 2
E1 = 8
T1 = N // P + E1 - 1
TS = N // P
ZEROED = 16 * (2 + T1 + T1 - TS)
EPS = 1e-5
FAR = float(1 << 20)


def build(nc, x, pairs, w0, b0, dw, rwT, rbias, sgT, suT, sdT, we0, wc, wn, b1, gwT, we1, sw1T, sw2T, out):
    xn_dram = nc.dram_tensor("xn_dram", [N, D], F32, kind="Internal").ap()
    slot_token = nc.dram_tensor("slot_token", [SLOTS, 1], F32, kind="Internal").ap()
    slot_out = nc.dram_tensor("slot_out", [SLOTS, D], F32, kind="Internal").ap()
    sorted_in = nc.dram_tensor("sorted_in", [T1 * P, D], F32, kind="Internal").ap()
    block_tot = nc.dram_tensor("block_tot", [NT, P], F32, kind="Internal").ap()
    moved = nc.dram_tensor("moved", [NE, 2], I32, kind="Internal").ap()
    sorted_out = nc.dram_tensor("sorted_out", [T1 * P, D], F32, kind="Internal").ap()

    with ExitStack() as ctx:
        def sb(name, shape, dt=F32):
            return ctx.enter_context(nc.sbuf_tensor(name, shape, dt))

        def sem(name):
            return ctx.enter_context(nc.semaphore(name))

        ps = ctx.enter_context(nc.psum_tensor("ps", [P, 8, 512], F32))

        xres = sb("xres", [P, NT, D])
        xn = sb("xn", [P, NT, D])
        with nc.sbuf_tensor("xnT", [P, KD, N], F32) as xnT:
            pass
        cur1_lo = sb("cur1_lo", [P, NT, D], F32R)
        with nc.sbuf_tensor("zone", [P, 20480], F32) as zone:
            pass
        S = sb("S", [P, NT, N], F32R)
        cur0_hi = sb("cur0_hi", [P, NT, D], F32R)
        cur0_lo = sb("cur0_lo", [P, NT, D], F32R)
        cur1_hi = sb("cur1_hi", [P, NT, D], F32R)
        cur = ((cur0_hi, cur0_lo), (cur1_hi, cur1_lo))
        with nc.sbuf_tensor("spare", [P, 2, WROW], F32) as spare:
            pass
        mT = sb("mT", [P, NT, N], F32R)
        identr = sb("identr", [P, P], F32R)
        onesr = sb("onesr", [P, 2], F32R)
        ring = sb("ring", [P, 2, WROW])
        ident = sb("ident", [P, P])
        tri = sb("tri", [P, P], BF16)
        ones = sb("ones", [P, P], BF16)
        iota = sb("iota", [P, N], F16)
        segs = sb("segs", [P, NT * E0], BF16)
        segs8 = sb("segs8", [P, NT * E1], BF16)
        pair_i = sb("pair_i", [P, P, 2], I32)
        next_i = sb("next_i", [P, 2], I32)
        viol = sb("viol", [1, 1], I32)
        words = sb("words", [1, EC // RING], I32)
        b0b = sb("b0b", [P, D])
        b1b = sb("b1b", [P, D])
        dwb = sb("dwb", [P, STEPS + 1])
        rb = sb("rb", [P, E0])
        rw = sb("rw", [P, KD, E0])
        gw = sb("gw", [P, KD, E1])
        stats = sb("stats", [P, NT, 6])
        mv = sb("mv", [P, NT, 2])
        rstd = sb("rstd", [P, NT])
        rsum = sb("rsum", [P, NT])
        cnt = sb("cnt", [P, NT])
        wr = sb("wr", [P, STEPS, NT])
        red = sb("red", [P, 6, NT])
        top8 = sb("top8", [P, NT, 8])
        tokf = sb("tokf", [P, NT])
        ebase = sb("ebase", [P, E0])
        dk = sb("dk", [P, TOP, NT])
        dki = sb("dki", [P, TOP, NT], U32)
        gk = sb("gk", [P, TOP, NT])
        gki = sb("gki", [P, TOP, NT], U32)
        idxA = sb("idxA", [P, E0], U32)
        idxB = sb("idxB", [CB, E0], U32)
        size_words = sb("size_words", [1, E0 // RING], I32)
        colA = sb("colA", [P, 2], U32)
        colB = sb("colB", [CB, 2], U32)
        t1row = sb("t1row", [P, 4, 16])
        sizes = sb("sizes", [P, E0 + 8])
        t1e = sb("t1e", [1, 16], I32)
        t1n = sb("t1n", [1, 1], I32)
        d1 = sb("d1", [P, NT])
        d1i = sb("d1i", [P, NT], U32)

        ohd = zone[:, 0:8192].bitcast(BF16).rearrange("p (c n) -> p c n", c=EC)
        xnT_words = xnT[:].rearrange("p k n -> p (k n)")
        ohs = xnT_words.bitcast(BF16).rearrange("p (b n) -> p b n", b=OHB)
        ohx = zone[:, 19456:19968].bitcast(BF16).rearrange("p (b n) -> p b n", b=NT)
        pair_f = zone[:, 16384:16640].rearrange("p (t c) -> p t c", t=2)
        blk_i = zone[:, 16640:16768].bitcast(I32)
        blk = zone[:, 16768:16896]
        edge_f = zone[:, 16896:17152].rearrange("p (t c) -> p t c", t=2)
        dloc = zone[:, 17152:17280]
        lob = zone[:, 17280:17408]
        pick = zone[:, 17408:17536]
        diag = zone[:, 17536:17664]
        small = zone[:, 17664:17920]
        onesf = zone[:, 17920:18048]
        zerob = zone[:, 18048:18112].bitcast(BF16)
        edge_x = zone[:, 18112:18176].rearrange("p (t b) -> p t b", b=NT)
        zeros = zone[:, 18432:19456]
        g_mask = zone[:, 0:1024].rearrange("p (b j) -> p b j", b=NT)
        g_scan = zone[:, 1024:3072].rearrange("p (z b j) -> p z b j", z=2, b=NT)
        g_tot = zone[:, 3072:4096].rearrange("p (b q) -> p b q", b=NT)
        g_bef = zone[:, 4096:5120].rearrange("p (b q) -> p b q", b=NT)
        g_pos = zone[:, 5120:5248]
        g_posi = zone[:, 5248:5376].bitcast(U32)
        g_col = zone[:, 5376:5377].bitcast(U32)
        g_pair = zone[:, 5378:5380].bitcast(I32)
        g_sum = zone[:, 5380:5388]
        g_tmp = zone[:, 5504:5632]
        w0s = ring[:, 0, 0:KD * D].rearrange("p (k n) -> p k n", k=KD)
        sact = zone[:, 0:4096].rearrange("p (f n) -> p f n", f=4)
        sd = zone[:, 4096:6144].rearrange("p (k n) -> p k n", k=4)
        sg = zone[:, 6144:8192].rearrange("p (k n) -> p k n", k=KD)
        su = zone[:, 8192:10240].rearrange("p (k n) -> p k n", k=KD)
        xg = zone[:, 10240:12288].rearrange("p (b n) -> p b n", b=2)
        xT = zone[:, 12288:13824].rearrange("p (b n) -> p b n", b=2)
        sil = zone[:, 13824:14592].rearrange("p (b n) -> p b n", b=2)
        act = zone[:, 14592:15360].rearrange("p (b f n) -> p b f n", b=2, f=KF)
        ob = zone[:, 15360:17408].rearrange("p (b n) -> p b n", b=2)
        gat = zone[:, 17408:19456].rearrange("p (b n) -> p b n", b=4)
        utmp = zone[:, 19456:20480].rearrange("p (b n) -> p b n", b=2)
        cnt_row = utmp[0:1].rearrange("p b n -> p (b n)")
        def table(j):
            return zone[:, 15360 + 512 * j:15872 + 512 * j]
        def by_e(t):
            return t.rearrange("p (i e) -> p i e", e=E0)
        prob, sel, csel, dest, gate, tmp, rank_t = [table(j) for j in range(7)]
        selb = table(7)[:, 0:256].bitcast(BF16)
        tki = table(7)[0:E0, 256:256 + CAP]
        beta_hi = S[:, 0:NT // 2, :].rearrange("p a (b n) -> p (a b) n", n=D)
        beta_lo = cur0_lo
        more = zone[:, 0:2 * WROW].rearrange("p (b n) -> p b n", b=2)
        wns = sg
        wcs = su
        s1w = zone[:, 4096:5120].rearrange("p (k n) -> p k n", k=KD)
        s2w = zone[:, 5120:6144].rearrange("p (k n) -> p k n", k=KF)
        gact = zone[:, 0:2048].rearrange("p (f n) -> p f n", f=KF)

        viol_ready, edges_final, cols_done = sem("viol_ready"), sem("edges_final"), sem("cols_done")
        vrow_ready, vsum_done, pairf_ready, words_ready, cnt_ready = [
            sem(n) for n in ("vrow_ready", "vsum_done", "pairf_ready", "words_ready", "cnt_ready")]
        g_dma, g_step, g_go = sem("g_dma"), sem("g_step"), sem("g_go")
        ld_x = [sem(f"ld_x{h}") for h in range(2)]
        ld_edge, ld_w0, ld_bc, ld_small = [sem(f"ld_{n}") for n in ("edge", "w0", "bc", "small")]
        ld_shared, ld_c, ld_s1 = [sem(f"ld_{n}") for n in ("shared", "c", "s1")]
        const_ready = sem("const_ready")
        pool_step = sem("pool_step")
        zero_ready, zeroed = sem("zero_ready"), sem("zeroed")
        dve_step = sem("dve_step")
        xn_ready, tr_done, tr_evac = sem("xn_ready"), sem("tr_done"), sem("tr_evac")
        var_ready, std_ready = sem("var_ready"), sem("std_ready")
        vart_ready, stdt_ready = sem("vart_ready"), sem("stdt_ready")
        h_done, h_evac, h_hi, h_lo, h_term = [sem(n) for n in ("h_done", "h_evac", "h_hi", "h_lo", "h_term")]
        oh_ready, oh_used = sem("oh_ready"), sem("oh_used")
        banks_free = sem("banks_free")
        m_done, m_evac_a, m_evac_v = sem("m_done"), sem("m_evac_a"), sem("m_evac_v")
        mt_done, adj_ready, s_ready = sem("mt_done"), sem("adj_ready"), sem("s_ready")
        ohd_ready, ohd_last = sem("ohd_ready"), sem("ohd_last")
        cntrow_done, cntrow_ready, cnt_done = sem("cntrow_done"), sem("cntrow_ready"), sem("cnt_done")
        s_done, s_evac = sem("s_done"), sem("s_evac")
        xn_stored = sem("xn_stored")
        lg_done, lgc_ready, ex_ready, sel_ready, rank_done = [sem(n) for n in ("lg_done", "lgc_ready", "ex_ready", "sel_ready", "rank_done")]
        sh_done, sh_sil, sh_act, shd_done, shd_evac = [sem(n) for n in ("sh_done", "sh_sil", "sh_act", "shd_done", "shd_evac")]
        dki_ready, scattered, tki_loaded, tki_tr, idx_ready = [sem(n) for n in ("dki_ready", "scattered", "tki_loaded", "tki_tr", "idx_ready")]
        sizes_ready = sem("sizes_ready")
        col_ready, gather_go = sem("col_ready"), sem("gather_go")
        xg_ready = [sem(f"xg_ready{u}") for u in range(2)]
        w_ready = [sem(f"w_ready{u}") for u in range(4)]
        xt_done, xt_evac = sem("xt_done"), sem("xt_evac")
        gu_done, sil_ready, act_ready = sem("gu_done"), sem("sil_ready"), sem("act_ready")
        dn_done, oa_ready, obb_ready = sem("dn_done"), sem("oa_ready"), sem("obb_ready")
        o_stored = [sem(f"o_stored{u}") for u in range(2)]
        gat_ready = [sem(f"gat_ready{u}") for u in range(8)]
        gat_used = sem("gat_used")
        be_hi, bias_added = sem("be_hi"), sem("bias_added")
        be_done, be_evac, al_done, al_evac, ga_done, ga_evac = [sem(n) for n in ("be_done", "be_evac", "al_done", "al_evac", "ga_done", "ga_evac")]
        lg1_done, sel1_ready, rank1_done, t1_ready, d1i_ready = [sem(n) for n in ("lg1_done", "sel1_ready", "rank1_done", "t1_ready", "d1i_ready")]
        s1_done, s1_act, s2_done, s2_evac = [sem(n) for n in ("s1_done", "s1_act", "s2_done", "s2_evac")]
        scattered1, x1_ready = sem("scattered1"), [sem(f"x1_ready{u}") for u in range(2)]
        y1_stored = [sem(f"y1_stored{u}") for u in range(2)]
        out_ready, out_done = sem("out_ready"), sem("out_done")

        rows = lambda t: t.rearrange("(i p) d -> p i d", p=P)
        xn_rows = rows(xn_dram)

        def size_word(eng, j):
            return eng.value_load(size_words[0:1, bass.ds(j, 1)], min_val=0, max_val=4 ** (RING + 2) - 1)

        H_BANKS = (2, 3, 4, 7)

        def weights(u, layer):
            return (ring, (spare, more)[layer == 0])[u // 2][:, u % 2, :]

        def gathered(j):
            return gat[:, j % 4, :] if j % 8 < 4 else xg[:, j % 4 // 2, j % 2 * D:(j % 2 + 1) * D]

        def size_of(word, i):
            return (word // 4 ** i) % 4

        def tiles_used(eng):
            return eng.value_load(t1n[0:1, 0:1], min_val=TS, max_val=T1)

        def if_used(eng, used, t, work):
            if t < TS:
                work()
                return
            with eng.If(used > t):
                work()

        def by_size(eng, size, work, few=True):
            if size is None:
                work(P)
                return
            with eng.If(size > 1):
                work(CAP)
            with eng.Else():
                if few:
                    with eng.If(size > 0):
                        work(P)
                    with eng.Else():
                        work(FEW)
                else:
                    work(P)

        block = ctx.enter_context(nc.Block())

        @block.sync
        def _(sp):
            for h in range(2):
                sp.dma_start(xres[:, h * 4:(h + 1) * 4, :], rows(x)[:, h * 4:(h + 1) * 4, :]).then_inc(ld_x[h], 16)
            sp.dma_start(pair_i[:], pairs.rearrange("(c j) t -> c j t", j=P)).then_inc(ld_edge, 16)
            sp.dma_start(next_i[0:P - 1, :], pairs.rearrange("(c j) t -> c j t", j=P)[1:P, 0, :]).then_inc(ld_edge, 16)
            sp.dma_start(w0s, w0.rearrange("(k p) n -> p k n", p=P)).then_inc(ld_w0, 16)
            sp.dma_start(rw[:], rwT.rearrange("(k p) n -> p k n", p=P)).then_inc(ld_small, 16)
            sp.dma_start(gw[:], gwT.rearrange("(k p) n -> p k n", p=P)).then_inc(ld_small, 16)
            sp.dma_start(b0b[:], b0.partition_broadcast(P)).then_inc(ld_bc, 16)
            sp.dma_start(b1b[:], b1.partition_broadcast(P)).then_inc(ld_bc, 16)
            sp.dma_start(dwb[:], dw.partition_broadcast(P)).then_inc(ld_bc, 16)
            sp.dma_start(rb[:], rbias.partition_broadcast(P)).then_inc(ld_bc, 16)
            sp.wait_ge(zero_ready, 1)
            sp.dma_start(slot_token.rearrange("(p c) o -> p (c o)", p=P), zeros[:, 0:SLOTS // P]).then_inc(zeroed, 16)
            sp.dma_start(slot_out.rearrange("(e c) d -> c e d", c=CAP)[FEW:CAP], zeros[0:CAP - FEW, 0:D].unsqueeze(1).broadcast_to([CAP - FEW, E0, D])).then_inc(zeroed, 16)
            for t in range(T1):
                sp.dma_start(sorted_in[t * P:(t + 1) * P, :], zeros[:, 0:D]).then_inc(zeroed, 16)
            for t in range(TS, T1):
                sp.dma_start(sorted_out[t * P:(t + 1) * P, :], zeros[:, 0:D]).then_inc(zeroed, 16)
            sp.wait_ge(h_done, NT)
            for u in range(2):
                sp.dma_start(weights(u, 0), we0[u]).then_inc(w_ready[u], 16)
            sp.wait_ge(s_done, STEPS * NT)
            sp.wait_ge(s_evac, STEPS * NT)
            sp.dma_start(sg, sgT.rearrange("(k p) n -> p k n", p=P)).then_inc(ld_shared, 16)
            sp.dma_start(su, suT.rearrange("(k p) n -> p k n", p=P)).then_inc(ld_shared, 16)
            sp.dma_start(sd, sdT.rearrange("(k p) n -> p k n", p=P)).then_inc(ld_shared, 16)
            sp.wait_ge(xn_ready, 2 * NT)
            sp.dma_start(xn_rows, xn[:]).then_inc(xn_stored, 16)
            sp.wait_ge(scattered, 16 * TOP * NT)
            sp.wait_ge(sel_ready, 1)
            sp.wait_ge(rank_done, 1)
            sp.dma_start(tki, slot_token.rearrange("(e c) o -> e (c o)", e=E0)).then_inc(tki_loaded, 16)
            sp.wait_ge(shd_done, NT)
            for u in range(2, 4):
                sp.dma_start(weights(u, 0), we0[u]).then_inc(w_ready[u], 16)
            with sp.Fori(0, E0 // 4 - 1) as g:
                for u in range(4):
                    sp.wait_ge(dn_done, g * 4 + (u + 1))
                    sp.dma_start(weights(u, 0), we0[bass.ds(g * 4 + (u + 4), 1)].rearrange("o p n -> p (o n)")).then_inc(w_ready[u], 16)
            sp.wait_ge(sh_done, 2 * 4)
            sp.dma_start(wns, wn.rearrange("(k p) n -> p k n", p=P)).then_inc(ld_c, 16)
            sp.dma_start(wcs, wc.rearrange("(k p) n -> p k n", p=P)).then_inc(ld_c, 16)
            sp.wait_ge(dn_done, E0)
            sp.dma_start(s1w, sw1T.rearrange("(k p) n -> p k n", p=P)).then_inc(ld_s1, 16)
            sp.dma_start(s2w, sw2T.rearrange("(k p) n -> p k n", p=P)).then_inc(ld_s1, 16)
            def tile_weights(t):
                ex = sp.value_load(t1e[0:1, t:t + 1], min_val=0, max_val=E1 - 1)
                if t >= 4:
                    sp.wait_ge(dn_done, E0 + t - 3)
                sp.dma_start(weights(t % 4, 1), we1[bass.ds(ex, 1)].rearrange("o p n -> p (o n)")).then_inc(w_ready[t % 4], 16)

            sp.wait_ge(ga_done, NT)
            sp.wait_ge(t1_ready, 1)
            for t in range(2):
                tile_weights(t)
            sp.wait_ge(scattered1, 16 * NT)
            used = tiles_used(sp)

            def tile_rows(t):
                if t >= 2:
                    sp.wait_ge(xt_done, E0 + t - 1)
                sp.dma_start(xg[:, t % 2, 0:D], sorted_in[t * P:(t + 1) * P, :]).then_inc(x1_ready[t % 2], 16)

            for t in range(T1):
                if_used(sp, used, t, lambda: tile_rows(t))
                for later in ((2, 3) if t == 1 else (t + 1,) if 3 <= t < T1 - 1 else ()):
                    if_used(sp, used, later, lambda: tile_weights(later))
            for i in range(NT):
                sp.wait_ge(out_ready, i + 1)
                sp.dma_start(out[i * P:(i + 1) * P, :], xres[:, i, :]).then_inc(out_done, 16)
            sp.wait_ge(out_done, 16 * NT)

        @block.gpsimd
        def _(pool):
            steps = [0]

            def link(ins):
                steps[0] += 1
                ins.then_inc(pool_step, 1)
                pool.wait_ge(pool_step, steps[0])

            pool.memset(zeros, 0.0).then_inc(zero_ready, 1)
            link(pool.iota(iota[:], pattern=[[1, N]], base=0, channel_multiplier=0, allow_small_or_imprecise_dtypes=True))
            pool.iota(tokf[:], pattern=[[P, NT]], base=0, channel_multiplier=1, allow_small_or_imprecise_dtypes=True)
            pool.iota(ebase[:], pattern=[[CAP, E0]], base=0, channel_multiplier=0, allow_small_or_imprecise_dtypes=True)
            pool.iota(t1row[:, 3, :], pattern=[[1, 16]], base=0, channel_multiplier=0, allow_small_or_imprecise_dtypes=True)
            pool.memset(ones[:], 1.0)
            pool.memset(tri[:], 1.0)
            pool.memset(segs[:], 1.0)
            pool.memset(segs8[:], 1.0)
            link(pool.memset(ident[:], 0.0))
            pool.affine_select(out=ident[:], in_=ident[:], compare_op=ALU.not_equal, fill=1.0, base=0, pattern=[[-1, P]], channel_multiplier=1)
            pool.affine_select(out=tri[:], in_=tri[:], compare_op=ALU.is_ge, fill=0.0, base=-1, pattern=[[1, P]], channel_multiplier=-1)
            pool.memset(segs[:].rearrange("p (i e) -> p i e", e=E0)[:, :, 0:1], 0.0)
            pool.memset(segs8[:].rearrange("p (i e) -> p i e", e=E1)[:, :, 0:1], 0.0).then_inc(const_ready, 1)

            pool.wait_ge(viol_ready, 1)
            bad = pool.value_load(viol[0:1, 0:1], min_val=0, max_val=NE)
            with pool.If(bad > 0):
                gs = [0]
                gd = [0]

                def done(ins):
                    gs[0] += 1
                    ins.then_inc(g_step, 1)
                    pool.wait_ge(g_step, gs[0])

                def landed(ins):
                    gd[0] += 16
                    ins.then_inc(g_dma, 16)
                    pool.wait_ge(g_dma, gd[0])

                for b in range(NT):
                    done(pool.tensor_scalar(g_mask[:, b, :], blk, float(b), None, ALU.is_equal))
                done(pool.tensor_copy(g_scan[:, 0], g_mask))
                z, d = 0, 1
                while d < P:
                    done(pool.tensor_tensor(g_scan[:, 1 - z, :, d:P], g_scan[:, z, :, d:P], g_scan[:, z, :, 0:P - d], ALU.add))
                    done(pool.tensor_copy(g_scan[:, 1 - z, :, 0:d], g_scan[:, z, :, 0:d]))
                    z, d = 1 - z, 2 * d
                done(pool.tensor_copy(g_sum, g_scan[:, z, :, P - 1]))
                for b in range(NT):
                    landed(pool.dma_start(block_tot[b, :].rearrange("(q o) -> q o", o=1), g_sum[:, b:b + 1]))
                landed(pool.dma_start(g_tot, block_tot.rearrange("b q -> (b q)").partition_broadcast(P)))
                done(pool.affine_select(out=g_bef, in_=g_tot, compare_op=ALU.is_ge, fill=0.0, base=-1, pattern=[[0, NT], [-1, P]], channel_multiplier=1))
                d = P // 2
                while d:
                    for t in (g_tot, g_bef):
                        done(pool.tensor_tensor(t[:, :, 0:d], t[:, :, 0:d], t[:, :, d:2 * d], ALU.add))
                    d //= 2
                done(pool.memset(g_pos, 0.0))
                for b in range(NT):
                    done(pool.tensor_scalar(g_tmp, g_scan[:, z, b, :], g_bef[:, b, 0:1], -1.0, ALU.add, ALU.add))
                    for low in range(b):
                        done(pool.tensor_scalar(g_tmp, g_tmp, g_tot[:, low, 0:1], None, ALU.add))
                    done(pool.tensor_tensor(g_tmp, g_tmp, g_mask[:, b, :], ALU.mult))
                    done(pool.tensor_tensor(g_pos, g_pos, g_tmp, ALU.add))
                done(pool.tensor_copy(g_posi, g_pos))
                with pool.Fori(0, P) as j:
                    pool.tensor_copy(g_col, g_posi[:, bass.ds(j, 1)]).then_inc(g_step, 1)
                    pool.tensor_copy(g_pair, pair_i[:, bass.ds(j, 1), :].rearrange("p o t -> p (o t)")).then_inc(g_step, 1)
                    pool.wait_ge(g_step, j * 2 + (gs[0] + 2))
                    pool.sem_inc(g_go, 1)
                    pool.indirect_dma_start(moved, bass.IndirectOffsetOnAxis(g_col, 0), g_pair, None).then_inc(g_dma, 16)
                    pool.wait_ge(g_dma, j * 16 + (gd[0] + 16))
                    pool.sem_inc(g_go, 1)
                gd[0] += 16 * P
                landed(pool.dma_start(pair_i[:], moved.rearrange("(c j) t -> c j t", j=P)))
            pool.sem_inc(edges_final, 1)

            pool.wait_ge(words_ready, 1)
            for g in range(POOL_ROWS):
                c = slice(g * RING, (g + 1) * RING)
                link(pool.tensor_tensor(ohd[:, c, :], iota[:, 0:P].unsqueeze(1).broadcast_to([P, RING, P]),
                                        dloc[:, c].unsqueeze(2).broadcast_to([P, RING, P]), ALU.subtract))
                pool.tensor_scalar(ohd[:, c, :], ohd[:, c, :], 0.0, None, ALU.is_equal).then_inc(ohd_ready, 1)

            pool.wait_ge(zeroed, ZEROED)
            for k in range(TOP):
                pool.wait_ge(dki_ready, k + 1)
                for i in range(NT):
                    pool.indirect_dma_start(slot_token, bass.IndirectOffsetOnAxis(dki[:, k, i:i + 1], 0), tokf[:, i:i + 1], None,
                                            bounds_check=SLOTS - 1, oob_is_err=False).then_inc(scattered, 16)
            pool.wait_ge(xn_stored, 16)
            pool.wait_ge(idx_ready, 1)

            def gather(u, e, size):
                pool.tensor_copy(colA[:, u:u + 1], idxA[:, bass.ds(e, 1)]).then_inc(col_ready, 1)
                pool.tensor_copy(colB[:, u:u + 1], idxB[:, bass.ds(e, 1)]).then_inc(col_ready, 1)
                pool.wait_ge(col_ready, (e + 1) * 2)
                pool.sem_inc(gather_go, 1)

                def rows_of(n):
                    first = min(n, P)
                    pool.indirect_dma_start(xg[0:first, u, 0:D], None, xn_dram,
                                            bass.IndirectOffsetOnAxis(colA[0:first, u:u + 1], 0)).then_inc(xg_ready[u], 16)
                    if n > P:
                        pool.indirect_dma_start(xg[0:CB, u, D:2 * D], None, xn_dram,
                                                bass.IndirectOffsetOnAxis(colB[:, u:u + 1], 0)).then_inc(xg_ready[u], 16)
                    else:
                        pool.dma_start(xg[0:1, u, D:D + 16], xn_dram[0:1, 0:16]).then_inc(xg_ready[u], 16)

                by_size(pool, size, rows_of)

            pool.wait_ge(sizes_ready, 1)
            word = size_word(pool, 0)
            for i in range(RING):
                if i >= 2:
                    pool.wait_ge(xt_done, i - 1)
                gather(i % 2, i, size_of(word, i))
            with pool.Fori(1, E0 // RING) as g:
                word = size_word(pool, g)
                for i in range(RING):
                    pool.wait_ge(xt_done, g * RING + (i - 1))
                    gather(i % 2, g * RING + i, size_of(word, i))

            for u in range(2):
                pool.wait_ge(o_stored[u], 32 * (E0 // 2))
            def add_bias(i):
                pool.wait_ge(al_evac, i + 1)
                pool.tensor_tensor(xres[:, i, :], xres[:, i, :], b1b[:], ALU.add).then_inc(bias_added, 1)

            for j in range(NT * TOP):
                i, k = j // TOP, j % TOP
                if k == 3 and i >= 3:
                    add_bias(i - 3)
                if j >= 8:
                    pool.wait_ge(gat_used, j - 7)
                pool.indirect_dma_start(gathered(j), None, slot_out, bass.IndirectOffsetOnAxis(gki[:, k, i:i + 1], 0),
                                        bounds_check=SLOTS - 1, oob_is_err=False).then_inc(gat_ready[j % 8], 16)

            for i in range(NT - 3, NT):
                add_bias(i)

            pool.wait_ge(d1i_ready, 1)
            for i in range(NT):
                pool.indirect_dma_start(sorted_in, bass.IndirectOffsetOnAxis(d1i[:, i:i + 1], 0), xn[:, i, :], None,
                                        bounds_check=T1 * P - 1, oob_is_err=False).then_inc(scattered1, 16)
            for u in range(2):
                pool.wait_ge(y1_stored[u], 16 * ((T1 + 1 - u) // 2))
            for i in range(NT):
                j = NT * TOP + i
                pool.wait_ge(gat_used, j - 7)
                pool.indirect_dma_start(gathered(j), None, sorted_out, bass.IndirectOffsetOnAxis(d1i[:, i:i + 1], 0),
                                        bounds_check=T1 * P - 1, oob_is_err=False).then_inc(gat_ready[j % 8], 16)

        @block.scalar
        def _(sc):
            def copy(o, i):
                return nc.scalar.activation(o, i, ACT.Copy)

            def evac_transposes(ln):
                if ln == 0:
                    sc.wait_ge(var_ready, 1)
                    nc.scalar.activation(rstd[:], rstd[:], ACT.Sqrt).then_inc(std_ready, 1)
                for i in range(NT):
                    if ln:
                        sc.wait_ge(vart_ready, NT * (ln - 1) + i + 1)
                        nc.scalar.activation(rstd[:, i:i + 1], rstd[:, i:i + 1], ACT.Sqrt).then_inc(stdt_ready, 1)
                    sc.wait_ge(tr_done, NT * ln + i + 1)
                    copy(xnT[:, :, i * P:(i + 1) * P], ps[:, i % 2, :].rearrange("p (k n) -> p k n", k=KD)).then_inc(tr_evac, 1)

            evac_transposes(0)
            sc.wait_ge(ld_bc, 64)
            for i in range(NT + 1):
                if i < NT:
                    sc.wait_ge(h_evac, i + 1)
                    copy(cur0_hi[:, i, :], xn[:, i, :]).then_inc(h_hi, 1)
                if i >= 1:
                    sc.wait_ge(h_lo, i)
                    nc.scalar.activation(xn[:, i - 1, :], xn[:, i - 1, :], ACT.Copy, scale=dwb[:, 0:1]).then_inc(h_term, 1)
            for h in range(2):
                sc.wait_ge(m_done, h + 1)
                for b in range(0, NT, 2):
                    copy(mT[:, b, h * 512:(h + 1) * 512], ps[:, b, :]).then_inc(m_evac_a, 1)
                sc.wait_ge(m_evac_a, (h + 1) * NT // 2)
                sc.sem_inc(banks_free, 1)
            for a in range(NT):
                sc.wait_ge(mt_done, a + 1)
                q = 2 * (a % 4)
                nc.scalar.activation(S[:, a, :], ps[:, q:q + 2, :].rearrange("p a n -> p (a n)"), ACT.Sign,
                                     accum_out=rsum[:, a:a + 1]).then_inc(adj_ready, 1)
            evac_transposes(1)

            def shared_evac(j):
                f, h = j % 4, j // 4
                sc.wait_ge(sh_done, j + 1)
                g = 4 + 2 * (j % 2)
                nc.scalar.activation(sact[:, f, h * 512:(h + 1) * 512], ps[:, g, :], ACT.Silu).then_inc(sh_sil, 1)

            sc.wait_ge(lgc_ready, 1)
            nc.scalar.activation(tmp, tmp, ACT.Exp).then_inc(ex_ready, 1)
            for j in range(8):
                if j == 2:
                    sc.wait_ge(cntrow_done, 1)
                    copy(cnt_row, ps[0:1, 0:2, :].rearrange("p h n -> p (h n)")).then_inc(cntrow_ready, 1)
                shared_evac(j)

            def expert(u, e, size):
                def products(n):
                    sc.wait_ge(gu_done, e + 1)
                    nc.scalar.activation(sil[:, u, :].rearrange("p (f n) -> p f n", f=KF)[:, :, 0:n],
                                         ps[:, 2 * u, 0:KF * CAP].rearrange("p (f n) -> p f n", f=KF)[:, :, 0:n], ACT.Silu).then_inc(sil_ready, 1)

                by_size(sc, size, products)

            def expert_out(u, e, stored, size):
                sc.wait_ge(dn_done, e + 1)
                if stored is not None:
                    sc.wait_ge(o_stored[u], stored)
                copy(ob[:, u, 0:D], ps[:, 6, :]).then_inc(oa_ready, 1)

                def store(n):
                    first = min(n, P)
                    sc.wait_ge(oa_ready, e + 1)
                    nc.scalar.dma_start(slot_out[bass.ds(e * CAP, first), :], ob[0:first, u, 0:D]).then_inc(o_stored[u], 16)
                    if n > P:
                        sc.wait_ge(obb_ready, e + 1)
                        nc.scalar.dma_start(slot_out[bass.ds(e * CAP + P, CB), :], ob[0:CB, u, D:2 * D]).then_inc(o_stored[u], 16)
                    else:
                        sc.sem_inc(o_stored[u], 16)

                by_size(sc, size, store)

            sc.wait_ge(sizes_ready, 1)
            word = size_word(sc, 0)
            expert(0, 0, size_of(word, 0))

            def step(i, e, stored, word, last=0):
                u = i % 2
                if last < 2:
                    expert(1 - u, e + 1, size_of(word, i + 1))
                expert_out(u, e, stored, size_of(word, i))

            for i in range(RING):
                step(i, i, 32 * (i // 2) or None, word)
            with sc.Fori(1, E0 // RING - 1) as g:
                word = size_word(sc, g)
                for i in range(RING):
                    step(i, g * RING + i, g * 128 + 32 * (i // 2), word)
            word = size_word(sc, E0 // RING - 1)
            for i in range(RING):
                e = E0 - RING + i
                step(i, e, 32 * (e // 2), word, last=max(0, i - RING + 3))

            for i in range(NT):
                sc.wait_ge(vart_ready, NT + i + 1)
                nc.scalar.activation(rstd[:, i:i + 1], rstd[:, i:i + 1], ACT.Sqrt).then_inc(stdt_ready, 1)
                sc.wait_ge(tr_done, NT * 2 + i + 1)
                copy(xnT[:, :, i * P:(i + 1) * P], ps[:, i % 2, :].rearrange("p (k n) -> p k n", k=KD)).then_inc(tr_evac, 1)
                sc.wait_ge(be_done, i + 1)
                copy(beta_hi[:, i, :], ps[:, 2 + i % 2, :]).then_inc(be_hi, 1)
            evac_transposes(3)
            for j in range(4):
                f, h = j % 2, j // 2
                sc.wait_ge(s1_done, j + 1)
                nc.scalar.activation(gact[:, f, h * 512:(h + 1) * 512], ps[:, 4 + j % 2, :], ACT.Gelu).then_inc(s1_act, 1)
            def tile_out(t):
                u, e = t % 2, E0 + t
                sc.wait_ge(dn_done, e + 1)
                if t >= 2:
                    sc.wait_ge(y1_stored[u], 16 * (t // 2))
                copy(ob[:, u, 0:D], ps[:, 6, :]).then_inc(oa_ready, 1)
                sc.wait_ge(oa_ready, e + 1)
                nc.scalar.dma_start(sorted_out[t * P:(t + 1) * P, :], ob[:, u, 0:D]).then_inc(y1_stored[u], 16)

            sc.wait_ge(t1_ready, 1)
            used = tiles_used(sc)
            expert(0, E0, None)
            for t in range(T1):
                if t < T1 - 1:
                    if_used(sc, used, t + 1, lambda: expert((t + 1) % 2, E0 + t + 1, None))
                if_used(sc, used, t, lambda: tile_out(t))
                if t >= TS:
                    with sc.If(used < t + 1):
                        sc.sem_inc(y1_stored[t % 2], 16)

        @block.vector
        def _(ve):
            v = nc.vector
            steps = [0, 0]

            def link(ins):
                steps[0] += 1
                ins.then_inc(dve_step, 1)
                ve.wait_ge(dve_step, steps[0])

            def layernorm_stats():
                for i in range(NT):
                    ve.wait_ge(ld_x[i // 4], 16)
                    last = v.bn_stats(stats[:, i, :], xres[:, i, :])
                link(last)
                for i in range(NT):
                    last = v.bn_aggr(mv[:, i, :], stats[:, i, :])
                link(last)
                v.tensor_scalar(rstd[:], mv[:, :, 1], EPS, None, ALU.add).then_inc(var_ready, 1)

            def normalise(tiles):
                for i in tiles:
                    v.tensor_scalar(xn[:, i, :], xres[:, i, :], mv[:, i, 0:1], rstd[:, i:i + 1],
                                    ALU.subtract, ALU.mult).then_inc(xn_ready, 1)

            def layernorm_tile(i):
                link(v.bn_stats(stats[:, i, :], xres[:, i, :]))
                link(v.bn_aggr(mv[:, i, :], stats[:, i, :]))
                steps[1] += 1
                v.tensor_scalar(rstd[:, i:i + 1], mv[:, i, 1:2], EPS, None, ALU.add).then_inc(vart_ready, 1)
                ve.wait_ge(stdt_ready, steps[1])
                link(v.reciprocal(rstd[:, i:i + 1], rstd[:, i:i + 1]))
                v.tensor_scalar(xn[:, i, :], xres[:, i, :], mv[:, i, 0:1], rstd[:, i:i + 1],
                                ALU.subtract, ALU.mult).then_inc(xn_ready, 1)

            def edges_to_float():
                v.tensor_copy(pair_f, pair_i[:].rearrange("c j t -> c t j"))
                link(v.tensor_scalar(blk_i, pair_i[:, :, 1], 7, None, ALU.logical_shift_right))
                link(v.tensor_copy(blk, blk_i))

            layernorm_stats()
            ve.wait_ge(ld_edge, 32)
            edges_to_float()
            nxt, n1, n2 = small[:, 0:1], small[:, 1:2], small[:, 2:3]
            link(v.memset(nxt, float(N)))
            link(v.tensor_copy(nxt[0:P - 1], next_i[0:P - 1, 1:2]))
            v.tensor_tensor(n1, pair_f[:, 1, P - 1:P], nxt, ALU.is_gt)
            link(v.tensor_tensor(pick[:, 0:P - 1], blk[:, 0:P - 1], blk[:, 1:P], ALU.is_gt))
            link(v.tensor_reduce(n2, pick[:, 0:P - 1], X, ALU.add))
            link(v.memset(onesf, 1.0))
            v.tensor_tensor(small[:, 3:4], n1, n2, ALU.add).then_inc(vrow_ready, 1)
            ve.wait_ge(std_ready, 1)
            link(v.reciprocal(rstd[:], rstd[:]))
            normalise(range(4))
            ve.wait_ge(vsum_done, 1)
            v.tensor_copy(viol[:], ps[0:1, 7, 0:1]).then_inc(viol_ready, 1)
            normalise(range(4, NT))
            ve.wait_ge(const_ready, 1)
            ve.wait_ge(edges_final, 1)
            edges_to_float()
            v.tensor_scalar(diag, ident[:], blk[:, 0:1], None, ALU.mult)
            for b in range(1, NT):
                link(v.tensor_scalar(pick, blk, float(b), None, ALU.is_lt))
                link(v.tensor_reduce(small[:, 8 + b:9 + b], pick, X, ALU.add))
            v.memset(zerob, 0.0).then_inc(pairf_ready, 1)
            ve.wait_ge(cols_done, 1)
            v.tensor_copy(edge_f, ps[:, 5, 0:2 * P].rearrange("p (t c) -> p t c", t=2))
            v.tensor_copy(lob, ps[:, 6, 0:P])
            link(v.tensor_copy(small[:, 25:32], ps[:, 6, P:P + NT - 1]))
            link(v.scalar_tensor_tensor(dloc, lob, -float(P), edge_f[:, 1, :], ALU.mult, ALU.add))
            link(v.tensor_scalar(pick, lob, 1.0, None, ALU.mult))
            pk = pick.rearrange("p (w i) -> p w i", i=RING)
            for i in range(1, RING):
                last = v.tensor_scalar(pk[:, :, i], pk[:, :, i], float(8 ** i), None, ALU.mult)
            link(last)
            link(v.tensor_reduce(small[:, 32:48], pk, X, ALU.add))
            v.tensor_copy(words[:], small[0:1, 32:48]).then_inc(words_ready, 1)
            def evacuate_h(i):
                ve.wait_ge(h_done, i + 1)
                v.tensor_tensor(xn[:, i, :], ps[:, H_BANKS[i % 4], :], b0b[:], ALU.add).then_inc(h_evac, 1)
                if i >= 1:
                    split_h(i - 1)

            def split_h(i):
                ve.wait_ge(h_hi, i + 1)
                v.tensor_tensor(cur0_lo[:, i, :], xn[:, i, :], cur0_hi[:, i, :].bitcast(F32), ALU.subtract).then_inc(h_lo, 1)

            v.tensor_copy(identr[:], ident[:])
            v.tensor_copy(onesr[:], onesf[:, 0:2])
            ve.wait_ge(ld_bc, 64)
            for i in range(4):
                evacuate_h(i)
            link(v.tensor_copy(small[:, 49:56].bitcast(I32), small[:, 25:32]))
            link(v.tensor_scalar(small[:, 57:64].bitcast(I32), small[:, 49:56].bitcast(I32), 7, None, ALU.logical_shift_right))
            link(v.tensor_copy(small[:, 65:72], small[:, 57:64].bitcast(I32)))
            later = NT - 1
            on, prod = [mT[:, j, 0:later * P].rearrange("p (b c) -> p b c", c=P) for j in range(2)]
            link(v.tensor_tensor(on, iota[:, 0:P].unsqueeze(1).broadcast_to([P, later, P]),
                                 small[:, 65:72].unsqueeze(2).broadcast_to([P, later, P]), ALU.is_equal))
            for j, t in enumerate((edge_f[:, 0, :], edge_f[:, 1, :], lob)):
                link(v.tensor_tensor(prod, on.bitcast(F32), t.unsqueeze(1).broadcast_to([P, later, P]), ALU.mult))
                link(v.tensor_reduce(edge_x[:, j, 1:NT], prod.bitcast(F32), X, ALU.add))
            x_dst, x_own = edge_x[:, 1, 1:NT], edge_x[:, 2, 1:NT]
            v.tensor_tensor(x_own, x_own, iota[:, 1:NT], ALU.is_equal)
            link(v.scalar_tensor_tensor(x_dst, iota[:, 1:NT], -float(P), x_dst, ALU.mult, ALU.add))
            link(v.scalar_tensor_tensor(x_dst, x_own, float(8 * N), x_dst, ALU.mult, ALU.add))
            for i in range(4, NT):
                evacuate_h(i)
            ve.wait_ge(h_evac, NT)
            ve.sem_inc(banks_free, 1)
            split_h(NT - 1)

            def onehot_src(u, h, s_):
                v.tensor_scalar(ohs[:, u, :], iota[:, h * 512:(h + 1) * 512], s_, None, ALU.is_equal).then_inc(oh_ready, 1)

            for h in range(2):
                for b in range(1, NT):
                    if h:
                        ve.wait_ge(oh_used, OHS + HEAD)
                    else:
                        v.tensor_scalar(ohx[:, b, :], iota[:, 0:P], edge_x[:, 1, b:b + 1], None, ALU.is_equal)
                    onehot_src(b, h, edge_x[:, 0, b:b + 1])
                for lo, hi in (((0, 4), (4, EC // OHB)) if h == 0 else ((0, EC // OHB),)):
                    with ve.Fori(lo, hi) as g:
                        for u in range(OHB):
                            if u % 4 == 0:
                                ve.wait_ge(oh_used, g * OHB + (u + 4 + NT - OHB + HEAD + h * (OHS + HEAD)))
                            onehot_src((NT + u) % OHB, h, edge_f[:, 0, bass.ds(g * OHB + u, 1)])
                    if h == 0 and lo == 0:
                        c = slice(POOL_ROWS * RING, EC)
                        v.tensor_tensor(ohd[:, c, :], iota[:, 0:P].unsqueeze(1).broadcast_to([P, EC - POOL_ROWS * RING, P]),
                                        dloc[:, c].unsqueeze(2).broadcast_to([P, EC - POOL_ROWS * RING, P]), ALU.is_equal).then_inc(ohd_last, 1)
                ve.wait_ge(m_done, h + 1)
                for b in range(1, NT, 2):
                    v.tensor_copy(mT[:, b, h * 512:(h + 1) * 512], ps[:, b, :]).then_inc(m_evac_v, 1)
                ve.wait_ge(m_evac_v, (h + 1) * NT // 2)
                ve.sem_inc(banks_free, 1)
            for a in range(NT):
                ve.wait_ge(adj_ready, a + 1)
                own = S[:, a, a * P:(a + 1) * P]
                v.tensor_tensor(own, own.bitcast(F32), ident[:], ALU.add).then_inc(s_ready, 1)
            link(v.tensor_scalar(rsum[:], rsum[:], 1.0, 1.0, ALU.add, ALU.max))
            link(v.reciprocal(rsum[:], rsum[:]))
            for t in range(STEPS):
                last = v.tensor_scalar(wr[:, t, :], rsum[:], dwb[:, t + 1:t + 2], None, ALU.mult)
            link(last)
            ve.wait_ge(h_term, NT)
            ve.wait_ge(zeroed, ZEROED)
            for t in range(STEPS):
                for m in range(NT):
                    ve.wait_ge(s_done, t * NT + m + 1)
                    if t < STEPS - 1:
                        hi, lo = cur[(t + 1) % 2]
                        link(v.tensor_scalar(hi[:, m, :], ps[:, m, :], rsum[:, m:m + 1], None, ALU.mult))
                        v.scalar_tensor_tensor(lo[:, m, :], ps[:, m, :], rsum[:, m:m + 1], hi[:, m, :].bitcast(F32), ALU.mult, ALU.subtract)
                    v.scalar_tensor_tensor(xn[:, m, :], ps[:, m, :], wr[:, t, m:m + 1], xn[:, m, :], ALU.mult, ALU.add).then_inc(s_evac, 1)
                    if t == STEPS - 1:
                        ve.wait_ge(s_evac, t * NT + m + 1)
                        link(v.scalar_tensor_tensor(xres[:, m, :], xn[:, m, :], 0.0, xres[:, m, :], ALU.max, ALU.add))
                        layernorm_tile(m)

            def bc(t):
                return t.unsqueeze(2).broadcast_to([P, NT, E0])

            def seg_sum(o, t):
                return v.tensor_reduce(o, by_e(t), X, ALU.add)

            ve.wait_ge(lg_done, 1)
            link(v.tensor_tensor(by_e(tmp), ps[:, 2, :].rearrange("p (i e) -> p i e", e=E0),
                                 rb[:].unsqueeze(1).broadcast_to([P, NT, E0]), ALU.add))
            link(v.tensor_reduce(red[:, 0, :], by_e(tmp), X, ALU.max))
            v.tensor_tensor(by_e(tmp), by_e(tmp), bc(red[:, 0, :]), ALU.subtract).then_inc(lgc_ready, 1)
            ve.wait_ge(ex_ready, 1)
            link(seg_sum(red[:, 1, :], tmp))
            link(v.reciprocal(red[:, 1, :], red[:, 1, :]))
            link(v.tensor_tensor(by_e(prob), by_e(tmp), bc(red[:, 1, :]), ALU.mult))
            for i in range(NT):
                last = v.max(top8[:, i, :], prob[:, i * E0:(i + 1) * E0])
            link(last)
            sixth = bc(top8[:, :, TOP - 1])
            v.tensor_tensor(by_e(dest), by_e(prob), sixth, ALU.is_gt)
            link(v.tensor_tensor(by_e(tmp), by_e(prob), sixth, ALU.is_equal))
            link(seg_sum(red[:, 2, :], dest))
            v.tensor_scalar(red[:, 2, :], red[:, 2, :], -1.0, float(TOP), ALU.mult, ALU.add)
            link(v.tensor_tensor_scan(csel, segs[:], tmp, 0.0, ALU.mult, ALU.add))
            link(v.tensor_tensor(by_e(csel), by_e(csel), bc(red[:, 2, :]), ALU.is_le))
            link(v.tensor_tensor(tmp, tmp, csel, ALU.mult))
            link(v.tensor_tensor(sel, dest, tmp, ALU.add))
            v.tensor_copy(selb, sel).then_inc(sel_ready, 1)
            v.tensor_tensor_scan(csel, segs[:], sel, 0.0, ALU.mult, ALU.add)
            link(v.tensor_tensor(gate, prob, sel, ALU.mult))
            link(seg_sum(red[:, 3, :], gate))
            link(v.tensor_scalar(red[:, 3, :], red[:, 3, :], 1e-9, None, ALU.add))
            link(v.reciprocal(red[:, 3, :], red[:, 3, :]))
            link(v.tensor_tensor(by_e(gate), by_e(gate), bc(red[:, 3, :]), ALU.mult))
            def shared_mul(j):
                ve.wait_ge(sh_sil, j + 1)
                blk = sact[:, j % 4, j // 4 * 512:(j // 4 + 1) * 512]
                v.tensor_tensor(blk, blk, ps[:, 5 + 2 * (j % 2), :], ALU.mult).then_inc(sh_act, 1)

            shared_mul(0)
            shared_mul(1)
            ve.wait_ge(rank_done, 1)
            link(v.tensor_copy(rank_t, ps[:, 3, :]))
            link(v.tensor_scalar(tmp, rank_t, float(CAP), None, ALU.is_ge))
            v.tensor_tensor(by_e(dest), by_e(rank_t), ebase[:].unsqueeze(1).broadcast_to([P, NT, E0]), ALU.add)
            link(v.tensor_scalar(prob, tmp, -1.0, 1.0, ALU.mult, ALU.add))
            v.tensor_tensor(gate, gate, prob, ALU.mult)
            link(v.scalar_tensor_tensor(dest, tmp, FAR, dest, ALU.mult, ALU.add))
            for k in range(TOP):
                link(v.scalar_tensor_tensor(tmp, csel, float(k + 1), sel, ALU.is_equal, ALU.mult))
                v.tensor_tensor(prob, tmp, dest, ALU.mult)
                link(v.tensor_tensor(rank_t, tmp, gate, ALU.mult))
                link(seg_sum(dk[:, k, :], prob))
                seg_sum(gk[:, k, :], rank_t)
                v.tensor_copy(dki[:, k, :], dk[:, k, :]).then_inc(dki_ready, 1)
                if k in (2, 4):
                    shared_mul(2 + k // 4)
            link(v.tensor_scalar(prob[:, 0:TOP * NT], dk[:].rearrange("p k i -> p (k i)"), float(SLOTS), None, ALU.is_lt))
            link(v.tensor_tensor(prob[:, 0:TOP * NT], prob[:, 0:TOP * NT], dk[:].rearrange("p k i -> p (k i)"), ALU.mult))
            link(v.tensor_copy(gki[:].rearrange("p k i -> p (k i)"), prob[:, 0:TOP * NT]))
            v.memset(t1row[:, 0:1, :], 0.0)
            link(v.memset(sizes[:, E0:E0 + 8], 0.0))
            link(v.tensor_scalar(sizes[:, 0:E0], ps[:, 2, 0:E0], float(P), None, ALU.is_gt))
            link(v.scalar_tensor_tensor(sizes[:, 0:E0], ps[:, 2, 0:E0], float(FEW), sizes[:, 0:E0], ALU.is_gt, ALU.add))
            fw = t1row[:, 0, 0:E0 // RING]
            for i in range(RING + 2):
                src = sizes[:, i:i + E0 - RING + 1:RING]
                link(v.scalar_tensor_tensor(fw, src, float(4 ** i), fw, ALU.mult, ALU.add))
            v.tensor_copy(size_words[:], fw[0:1, :]).then_inc(sizes_ready, 1)
            ve.wait_ge(cnt_done, 1)
            v.tensor_copy(cnt[:], ps[:, 0, 0:NT]).then_inc(cnt_ready, 1)
            for j in range(4, 8):
                shared_mul(j)
            for i in range(NT):
                ve.wait_ge(shd_done, i + 1)
                v.scalar_tensor_tensor(xres[:, i, :], ps[:, 4 + i % 4, :], 1.0 / SH, xres[:, i, :], ALU.mult, ALU.add).then_inc(shd_evac, 1)
                if i == NT // 2 - 1:
                    ve.wait_ge(tki_tr, 1)
                    v.tensor_copy(idxA[:], ps[:, 2, 0:E0])
                    v.tensor_copy(idxB[:], ps[0:CB, 2, E0:2 * E0]).then_inc(idx_ready, 1)

            def xt_evacuate(u, e, size):
                def rows_of(n):
                    ve.wait_ge(xt_done, e + 1)
                    v.tensor_copy(xT[:, u, :].rearrange("p (b k n) -> p b k n", b=2, k=2)[:, :, :, 0:n],
                                  ps[:, 4:6, 0:2 * CAP].rearrange("p b (k n) -> p b k n", k=2)[:, :, :, 0:n]).then_inc(xt_evac, 1)

                by_size(ve, size, rows_of)

            def multiply(u, e, size):
                def products(n):
                    ve.wait_ge(sil_ready, e + 1)
                    v.tensor_tensor(act[:, u, :, 0:n], sil[:, u, :].rearrange("p (f n) -> p f n", f=KF)[:, :, 0:n],
                                    ps[:, 2 * u + 1, 0:KF * CAP].rearrange("p (f n) -> p f n", f=KF)[:, :, 0:n], ALU.mult).then_inc(act_ready, 1)

                by_size(ve, size, products)

            def second_out(u, e, stored, size):
                def rows_of(n):
                    if n > P:
                        ve.wait_ge(dn_done, e + 1)
                        if stored is not None:
                            ve.wait_ge(o_stored[u], stored)
                        v.tensor_copy(ob[0:CB, u, D:2 * D], ps[0:CB, 7, :]).then_inc(obb_ready, 1)
                    else:
                        ve.sem_inc(obb_ready, 1)

                by_size(ve, size, rows_of, few=False)

            word = size_word(ve, 0)
            xt_evacuate(0, 0, size_of(word, 0))
            xt_evacuate(1, 1, size_of(word, 1))
            multiply(0, 0, size_of(word, 0))

            def step(i, e, stored, word, last=0):
                u = i % 2
                if last < 2:
                    multiply(1 - u, e + 1, size_of(word, i + 1))
                if last < 1:
                    xt_evacuate(u, e + 2, size_of(word, i + 2))
                second_out(u, e, stored, size_of(word, i))

            for i in range(RING):
                step(i, i, 32 * (i // 2) or None, word)
            with ve.Fori(1, E0 // RING - 1) as g:
                word = size_word(ve, g)
                for i in range(RING):
                    step(i, g * RING + i, g * 128 + 32 * (i // 2), word)
            word = size_word(ve, E0 // RING - 1)
            for i in range(RING):
                e = E0 - RING + i
                step(i, e, 32 * (e // 2), word, last=max(0, i - RING + 3))

            ve.wait_ge(cnt_ready, 1)
            v.reciprocal(cnt[:], cnt[:])

            def add_alpha(i):
                ve.wait_ge(al_done, i + 1)
                v.tensor_tensor(xres[:, i, :], xres[:, i, :], ps[:, 4 + i % 2, :], ALU.add).then_inc(al_evac, 1)

            def split_beta(i):
                ve.wait_ge(be_hi, i + 1)
                v.tensor_tensor(beta_lo[:, i, :], ps[:, 2 + i % 2, :], beta_hi[:, i, :].bitcast(F32), ALU.subtract).then_inc(be_evac, 1)

            for i in range(NT):
                for k in range(TOP):
                    j = i * TOP + k
                    ve.wait_ge(gat_ready[j % 8], 16 * (j // 8 + 1))
                    if k >= 1:
                        ve.wait_ge(gat_used, j)
                    v.scalar_tensor_tensor(xres[:, i, :], gathered(j), gk[:, k, i:i + 1], xres[:, i, :], ALU.mult, ALU.add).then_inc(gat_used, 1)
                ve.wait_ge(gat_used, (i + 1) * TOP)
                layernorm_tile(i)
                if i >= 1:
                    split_beta(i - 1)
                    add_alpha(i - 1)

            split_beta(NT - 1)
            add_alpha(NT - 1)
            for i in range(NT):
                ve.wait_ge(ga_done, i + 1)
                ve.wait_ge(bias_added, i + 1)
                v.scalar_tensor_tensor(xres[:, i, :], ps[:, 6 + i % 2, :], cnt[:, i:i + 1], xres[:, i, :], ALU.mult, ALU.add).then_inc(ga_evac, 1)
                ve.wait_ge(ga_evac, i + 1)
                layernorm_tile(i)

            W8 = NT * E1
            def t8(t):
                return t[:, 0:W8].rearrange("p (i e) -> p i e", e=E1)
            def bc8(t):
                return t.unsqueeze(2).broadcast_to([P, NT, E1])
            lg, one, cum, place = utmp[:, 0, 0:64], utmp[:, 0, 64:128], utmp[:, 0, 128:192], utmp[:, 0, 192:256]
            oneb = utmp[:, 0, 256:288].bitcast(BF16)
            ve.wait_ge(lg1_done, 1)
            link(v.tensor_copy(lg, ps[:, 2, 0:W8]))
            link(v.tensor_reduce(red[:, 0, :], t8(lg), X, ALU.max))
            link(v.tensor_tensor(t8(one), t8(lg), bc8(red[:, 0, :]), ALU.is_equal))
            link(v.tensor_tensor_scan(cum, segs8[:], one, 0.0, ALU.mult, ALU.add))
            link(v.scalar_tensor_tensor(one, cum, 1.0, one, ALU.is_equal, ALU.mult))
            v.tensor_copy(oneb, one).then_inc(sel1_ready, 1)
            ve.wait_ge(rank1_done, 1)
            r0, r1, r2, num = [t1row[:, j, :] for j in range(4)]
            link(v.tensor_copy(r0[:, 0:E1], ps[:, 3, W8:W8 + E1]))
            ge = utmp[:, 1, 0:64].rearrange("p (e t) -> p e t", t=8)
            link(v.tensor_scalar(r2[:, 0:8], num[:, 0:8], float(P), None, ALU.mult))
            link(v.tensor_tensor(ge, r0[:, 0:E1].unsqueeze(2).broadcast_to([P, E1, 8]), r2[:, 0:8].unsqueeze(1).broadcast_to([P, E1, 8]), ALU.is_gt))
            link(v.tensor_reduce(r0[:, 0:E1], ge, X, ALU.add))
            link(v.memset(r1[:, 0:E1], 1.0))
            link(v.tensor_tensor_scan(r2[:, 0:E1], r1[:, 0:E1], r0[:, 0:E1], 0.0, ALU.mult, ALU.add))
            link(v.tensor_tensor(r0[:, 0:E1], r2[:, 0:E1], r0[:, 0:E1], ALU.subtract))
            link(v.tensor_scalar(r0[:, 0:E1], r0[:, 0:E1], float(P), None, ALU.mult))
            link(v.tensor_tensor(t8(place), ps[:, 3, 0:W8].rearrange("p (i e) -> p i e", e=E1), r0[:, 0:E1].unsqueeze(1).broadcast_to([P, NT, E1]), ALU.add))
            link(v.tensor_tensor(place, place, one, ALU.mult))
            link(v.tensor_reduce(d1[:], t8(place), X, ALU.add))
            v.tensor_copy(d1i[:], d1[:]).then_inc(d1i_ready, 1)
            te = utmp[:, 1, 128:256].rearrange("p (t e) -> p t e", e=E1)
            link(v.tensor_tensor(te, r2[:, 0:E1].unsqueeze(1).broadcast_to([P, 16, E1]), num.unsqueeze(2).broadcast_to([P, 16, E1]), ALU.is_le))
            link(v.tensor_reduce(r1, te, X, ALU.add))
            link(v.tensor_scalar(r1, r1, float(E1 - 1), None, ALU.min))
            v.tensor_copy(t1n[:], r2[0:1, E1 - 1:E1])
            v.tensor_copy(t1e[:], r1[0:1, :]).then_inc(t1_ready, 1)
            for i in range(NT):
                ve.wait_ge(s2_done, i + 1)
                v.tensor_tensor(xres[:, i, :], xres[:, i, :], ps[:, 6 + i % 2, :], ALU.add).then_inc(s2_evac, 1)
            ve.wait_ge(t1_ready, 1)
            used = tiles_used(ve)
            xt_evacuate(0, E0, None)
            xt_evacuate(1, E0 + 1, None)
            multiply(0, E0, None)
            for t in range(T1):
                if t < T1 - 1:
                    if_used(ve, used, t + 1, lambda: multiply((t + 1) % 2, E0 + t + 1, None))
                if t < T1 - 2:
                    if_used(ve, used, t + 2, lambda: xt_evacuate(t % 2, E0 + t + 2, None))
            ve.wait_ge(s2_evac, NT)
            for i in range(NT):
                j = NT * TOP + i
                ve.wait_ge(gat_ready[j % 8], 16 * (j // 8 + 1))
                v.tensor_tensor(xres[:, i, :], xres[:, i, :], gathered(j), ALU.add).then_inc(out_ready, 1)
                ve.wait_ge(out_ready, i + 1)
                v.tensor_copy(red[:, 5, 0:1], red[:, 0, 0:1]).then_inc(gat_used, 1)

        @block.tensor
        def _(pe):
            t_ = nc.tensor

            def mm(o, l, r, start, stop):
                return t_.matmul(o, l, r, start=start, stop=stop)

            def tokens(k, i):
                return xnT[:, k, i * P:(i + 1) * P]

            def transpose_rows(ln, i):
                pe.wait_ge(xn_ready, NT * ln + i + 1)
                if i >= 2:
                    pe.wait_ge(tr_evac, NT * ln + i - 1)
                for k in range(KD):
                    last = t_.transpose(ps[:, i % 2, k * P:(k + 1) * P], xn[:, i, k * P:(k + 1) * P], ident[:])
                last.then_inc(tr_done, 1)

            pe.wait_ge(const_ready, 1)
            pe.wait_ge(vrow_ready, 1)
            mm(ps[:, 7, 0:1], onesf, small[:, 3:4], True, True).then_inc(vsum_done, 1)
            for i in range(NT):
                transpose_rows(0, i)
            pe.wait_ge(ld_w0, 16)
            pe.wait_ge(viol_ready, 1)
            for i in range(NT):
                pe.wait_ge(tr_evac, i + 1)
                if i >= 4:
                    pe.wait_ge(h_evac, i - 3)
                for k in range(KD):
                    last = mm(ps[:, H_BANKS[i % 4], :], tokens(k, i), w0s[:, k, :], k == 0, k == KD - 1)
                last.then_inc(h_done, 1)
                if i == 1:
                    pe.wait_ge(pairf_ready, 1)
                    for t in range(2):
                        t_.transpose(ps[:, 5, t * P:(t + 1) * P], pair_f[:, t, :], ident[:])
                    mm(ps[:, 6, 0:P], onesf, diag, True, True)
                    mm(ps[:, 6, P:P + NT - 1], onesf, small[:, 9:16], True, True).then_inc(cols_done, 1)

            def outer(dst, src, out_, first):
                return t_.matmul(out_, dst, src, start=first, stop=False, skip_group_check=True).then_inc(oh_used, 1)

            pe.wait_ge(words_ready, 1)
            with pe.Fori(0, 2) as h:
                pe.wait_ge(banks_free, h * 2 + 1)
                t_.matmul(ps[:, 0, :], zerob, iota[:, 0:512], start=True, stop=False, skip_group_check=True).then_inc(oh_used, 1 + HEAD)
                for b in range(1, NT):
                    pe.wait_ge(oh_ready, h * (OHS - 1) + b)
                    outer(ohx[:, b, :], ohs[:, b, :], ps[:, b, :], True)
                for c in range(EC):
                    if c % GROUP == 0:
                        _, group_words = nc.values_load_multi_w_load_instructions(
                            words[0:1, c // RING:(c + GROUP) // RING], engines=[mybir.EngineType.PE], min_val=0, max_val=8 ** RING - 1)
                    if c % 4 == 0:
                        pe.wait_ge(oh_ready, h * (OHS - 1) + (NT + c + 3))
                    if c % RING == 0:
                        if c // RING < POOL_ROWS:
                            pe.wait_ge(ohd_ready, c // RING + 1)
                        else:
                            pe.wait_ge(ohd_last, 1)
                    bank = (group_words[c % GROUP // RING] // 8 ** (c % RING)) % 8
                    outer(ohd[:, c, :], ohs[:, (NT + c) % OHB, :],
                          ps[:, bass.ds(bank, 1), :].rearrange("p o n -> p (o n)"), False)
                t_.matmul(ps[:, 0, 0:8], zerob, zerob[:, 0:8], start=False, stop=True, skip_group_check=True).then_inc(m_done, 1)
            pe.wait_ge(m_evac_a, NT)
            pe.wait_ge(m_evac_v, NT)
            for a in range(NT):
                if a >= 4:
                    pe.wait_ge(adj_ready, a - 3)

                def add(o, l, r, start, stop):
                    return t_.matmul(o, l, r, start=start, stop=stop, skip_group_check=True)

                q = 2 * (a % 4)
                for h in range(2):
                    add(ps[:, q + h, :], identr[:], mT[:, a, h * 512:(h + 1) * 512], True, False)
                    for b in range(4 * h, 4 * h + 4):
                        last = add(ps[:, q + h, (b % 4) * P:(b % 4 + 1) * P], mT[:, b, a * P:(a + 1) * P], identr[:], False, b % 4 == 3)
                last.then_inc(mt_done, 1)
            def router(i):
                pe.wait_ge(s_evac, (STEPS - 1) * NT + 3)
                pe.wait_ge(tr_evac, NT + i + 1)
                for k in range(KD):
                    last = mm(ps[:, 2, i * E0:(i + 1) * E0], tokens(k, i), rw[:, k, :], k == 0, k == KD - 1)
                return last

            pe.wait_ge(ld_small, 32)
            pe.wait_ge(s_ready, NT)
            pe.wait_ge(h_lo, NT)
            for t in range(STEPS):
                if t >= 1:
                    pe.wait_ge(s_evac, t * NT)
                for m in range(NT):
                    for k in range(NT):
                        for part in range(2):
                            last = mm(ps[:, m, :], S[:, k, m * P:(m + 1) * P], cur[t % 2][part][:, k, :], k + part == 0, k + part == NT)
                    last.then_inc(s_done, 1)
                    if t == STEPS - 1 and m >= 1:
                        transpose_rows(1, m - 1)
                    if t == STEPS - 1 and m >= 4:
                        router(m - 4)
            transpose_rows(1, NT - 1)
            for i in range(NT - 4, NT):
                last = router(i)
            last.then_inc(lg_done, 1)
            pe.wait_ge(s_evac, STEPS * NT)

            def shared(j):
                f, h = j % 4, j // 4
                if j >= 2:
                    pe.wait_ge(sh_act, j - 1)
                for w, g in ((sg, 4 + 2 * (j % 2)), (su, 5 + 2 * (j % 2))):
                    for k in range(KD):
                        last = mm(ps[:, g, :], w[:, k, f * P:(f + 1) * P], xnT[:, k, h * 512:(h + 1) * 512], k == 0, k == KD - 1)
                last.then_inc(sh_done, 1)

            pe.wait_ge(ld_shared, 48)
            for j in range(2):
                shared(j)
            pe.wait_ge(sel_ready, 1)
            selm = selb.rearrange("p (i e) -> p i e", e=E0)
            for i in range(NT):
                for j in range(i):
                    mm(ps[:, 3, i * E0:(i + 1) * E0], ones[:], selm[:, j, :], j == 0, False)
                mm(ps[:, 3, i * E0:(i + 1) * E0], tri[:], selm[:, i, :], i == 0, True)
            for i in range(NT):
                last = mm(ps[:, 2, 0:E0], ones[:], selm[:, i, :], i == 0, i == NT - 1)
            last.then_inc(rank_done, 1)
            for h in range(2):
                for b in range(NT):
                    last = mm(ps[0:2, h, :], onesr[:], mT[:, b, h * 512:(h + 1) * 512], b == 0, b == NT - 1)
            last.then_inc(cntrow_done, 1)
            shared(2)
            pe.wait_ge(cntrow_ready, 1)
            for a in range(NT):
                last = mm(ps[:, 0, a:a + 1], cnt_row[:, a * P:(a + 1) * P], ident[0:1, 0:1], True, True)
            last.then_inc(cnt_done, 1)
            for j in range(3, 8):
                shared(j)
            pe.wait_ge(sh_act, 8)
            for i in range(NT):
                if i >= 4:
                    pe.wait_ge(shd_evac, i - 3)
                for k in range(4):
                    last = mm(ps[:, 4 + i % 4, :], sact[:, k, i * P:(i + 1) * P], sd[:, k, :], k == 0, k == 3)
                last.then_inc(shd_done, 1)
                if i == NT // 2 - 1:
                    pe.wait_ge(sizes_ready, 1)
                    pe.wait_ge(tki_loaded, 16)
                    t_.transpose(ps[:, 2, 0:E0], tki[:, 0:P], ident[0:E0, 0:E0])
                    t_.transpose(ps[0:CB, 2, E0:2 * E0], tki[:, P:CAP], ident[0:E0, 0:E0]).then_inc(tki_tr, 1)
            pe.wait_ge(cnt_ready, 1)
            pe.wait_ge(shd_evac, NT)
            pe.wait_ge(idx_ready, 1)

            def turn(u, e, n, first, size):
                pe.wait_ge((x1_ready if size is None else xg_ready)[u], n)
                if not first:
                    pe.wait_ge(xt_evac, e)
                def rows_of(n):
                    for k in range(KD):
                        o = (k % 2) * CAP
                        first = min(n, P)
                        last = t_.transpose(ps[:, 4 + k // 2, o:o + first], xg[0:first, u, k * P:(k + 1) * P], ident[0:first, 0:first])
                        if n > P:
                            last = t_.transpose(ps[:, 4 + k // 2, o + P:o + CAP], xg[0:CB, u, D + k * P:D + (k + 1) * P], ident[0:CB, 0:CB])
                    last.then_inc(xt_done, 1)

                by_size(pe, size, rows_of)

            def gate_up(b, e, n, size):
                u, w = b % 2, weights(b, int(size is None))
                pe.wait_ge(w_ready[b], n)
                pe.wait_ge(xt_evac, e + 1)
                def products(n):
                    for g in range(2):
                        for f in range(KF):
                            for k in range(KD):
                                last = mm(ps[:, 2 * u + g, f * CAP:f * CAP + n],
                                          w[:, (g * KD + k) * F + f * P:(g * KD + k) * F + (f + 1) * P],
                                          xT[:, u, k * CAP:k * CAP + n], k == 0, k == KD - 1)
                    last.then_inc(gu_done, 1)

                by_size(pe, size, products)

            def down(b, e, first, size):
                u, w = b % 2, weights(b, int(size is None))
                pe.wait_ge(act_ready, e + 1)
                if not first:
                    pe.wait_ge(oa_ready, e)
                    if size is not None:
                        pe.wait_ge(obb_ready, e)
                def products(n):
                    for o, lo, hi in ((6, 0, min(n, P)), (7, P, CAP)):
                        if lo < n:
                            for f in range(KF):
                                last = mm(ps[0:hi - lo, o, :], act[:, u, f, lo:hi],
                                          w[:, GU + f * D:GU + (f + 1) * D], f == 0, f == KF - 1)
                    last.then_inc(dn_done, 1)

                by_size(pe, size, products)

            pe.wait_ge(sizes_ready, 1)
            word = size_word(pe, 0)
            turn(0, 0, 32, True, size_of(word, 0))
            turn(1, 1, 32, False, size_of(word, 1))
            gate_up(0, 0, 16, size_of(word, 0))

            def step(i, e, gu_n, turn_n, word, first=False, last=0):
                if last < 2:
                    gate_up((i + 1) % 4, e + 1, gu_n, size_of(word, i + 1))
                if last < 1:
                    turn(i % 2, e + 2, turn_n, False, size_of(word, i + 2))
                down(i % 4, e, first, size_of(word, i))

            for i in range(RING):
                step(i, i, 16 * ((i + 1) // 4 + 1), 32 * (i // 2 + 2), word, first=i == 0)
            with pe.Fori(1, E0 // RING - 1) as g:
                word = size_word(pe, g)
                for i in range(RING):
                    step(i, g * RING + i, g * (16 * RING // 4) + 16 * ((i + 1) // 4 + 1), g * 128 + 32 * (i // 2 + 2), word)
            word = size_word(pe, E0 // RING - 1)
            for i in range(RING):
                e = E0 - RING + i
                step(i, e, 16 * ((e + 1) // 4 + 1), 32 * (e // 2 + 2), word, last=max(0, i - RING + 3))

            pe.wait_ge(ld_c, 32)
            pe.wait_ge(obb_ready, E0)
            pe.wait_ge(oa_ready, E0)
            for i in range(NT):
                transpose_rows(2, i)
                pe.wait_ge(tr_evac, 2 * NT + i + 1)
                if i >= 2:
                    pe.wait_ge(be_evac, i - 1)
                for k in range(KD):
                    last = mm(ps[:, 2 + i % 2, :], tokens(k, i), wns[:, k, :], k == 0, k == KD - 1)
                last.then_inc(be_done, 1)
                if i >= 2:
                    pe.wait_ge(al_evac, i - 1)
                for k in range(KD):
                    last = mm(ps[:, 4 + i % 2, :], tokens(k, i), wcs[:, k, :], k == 0, k == KD - 1)
                last.then_inc(al_done, 1)
            pe.wait_ge(be_evac, NT)

            def router1(i):
                pe.wait_ge(tr_evac, 3 * NT + i + 1)
                for k in range(KD):
                    last = mm(ps[:, 2, i * E1:(i + 1) * E1], tokens(k, i), gw[:, k, :], k == 0, k == KD - 1)
                return last

            for i in range(NT):
                if i >= 2:
                    pe.wait_ge(ga_evac, i - 1)
                for b in range(NT):
                    for part, beta in enumerate((beta_hi, beta_lo)):
                        last = mm(ps[:, 6 + i % 2, :], mT[:, b, i * P:(i + 1) * P], beta[:, b, :], b + part == 0, b + part == NT)
                last.then_inc(ga_done, 1)
                if i >= 1:
                    transpose_rows(3, i - 1)
                if i >= 3:
                    router1(i - 3)
            transpose_rows(3, NT - 1)
            for i in range(NT - 3, NT):
                last = router1(i)
            last.then_inc(lg1_done, 1)

            pe.wait_ge(ld_s1, 32)
            pe.wait_ge(al_evac, NT)
            def shared1(j):
                f, h = j % 2, j // 2
                if j >= 2:
                    pe.wait_ge(s1_act, j - 1)
                for k in range(KD):
                    last = mm(ps[:, 4 + j % 2, :], s1w[:, k, f * P:(f + 1) * P], xnT[:, k, h * 512:(h + 1) * 512], k == 0, k == KD - 1)
                last.then_inc(s1_done, 1)

            shared1(0)
            pe.wait_ge(sel1_ready, 1)
            onem = utmp[:, 0, 256:288].bitcast(BF16).rearrange("p (i e) -> p i e", e=E1)
            for i in range(NT):
                for j in range(i):
                    mm(ps[:, 3, i * E1:(i + 1) * E1], ones[:], onem[:, j, :], j == 0, False)
                mm(ps[:, 3, i * E1:(i + 1) * E1], tri[:], onem[:, i, :], i == 0, True)
            for j in range(NT):
                last = mm(ps[:, 3, NT * E1:NT * E1 + E1], ones[:], onem[:, j, :], j == 0, j == NT - 1)
            last.then_inc(rank1_done, 1)
            for j in range(1, 4):
                shared1(j)
            pe.wait_ge(s1_act, 4)
            pe.wait_ge(ga_evac, NT)
            for i in range(NT):
                if i >= 2:
                    pe.wait_ge(s2_evac, i - 1)
                for f in range(KF):
                    last = mm(ps[:, 6 + i % 2, :], gact[:, f, i * P:(i + 1) * P], s2w[:, f, :], f == 0, f == KF - 1)
                last.then_inc(s2_done, 1)
            pe.wait_ge(s2_evac, NT)
            pe.wait_ge(t1_ready, 1)
            used = tiles_used(pe)
            turn(0, E0, 16, False, None)
            turn(1, E0 + 1, 16, False, None)
            gate_up(0, E0, 16 * (E0 // 4 + 1), None)
            for t in range(T1):
                e = E0 + t
                if t < T1 - 1:
                    if_used(pe, used, t + 1, lambda: gate_up((t + 1) % 4, e + 1, 16 * ((e + 1) // 4 + 1), None))
                if t < T1 - 2:
                    if_used(pe, used, t + 2, lambda: turn(t % 2, e + 2, 16 * (t // 2 + 2), False, None))
                if_used(pe, used, t, lambda: down(t % 4, e, False, None))


def kernel(**inputs):
    import numpy as np
    import concourse.bacc as bacc
    from concourse.bass_utils import run_bass_kernel_spmd

    a = {k: np.asarray(v) for k, v in inputs.items()}

    def chunked(w):
        e, k, m = w.shape
        return w.reshape(e, k // P, P, m).transpose(0, 2, 1, 3).reshape(e, P, -1)

    def turned(w):
        return w.transpose(0, 2, 1)

    arrays = {
        "x": a["x"],
        "pairs": np.stack([a["src"], a["dst"]], axis=1),
        "w0": a["L0_gnn_W"], "b0": a["L0_gnn_b"], "dw": a["L0_gnn_diffusion_weights"],
        "rwT": a["L0_ffn_router_w"].T, "rbias": a["L0_ffn_bias"],
        "sgT": a["L0_ffn_shared_w_gate"].reshape(SH * F, D).T,
        "suT": a["L0_ffn_shared_w_up"].reshape(SH * F, D).T,
        "sdT": turned(a["L0_ffn_shared_w_down"]).reshape(SH * F, D),
        "we0": np.concatenate([chunked(turned(a["L0_ffn_w_gate"])), chunked(turned(a["L0_ffn_w_up"])),
                               chunked(turned(a["L0_ffn_w_down"]))], axis=2),
        "wc": a["L1_gnn_wc"], "wn": a["L1_gnn_wn"], "b1": a["L1_gnn_bias"],
        "gwT": a["L1_ffn_gate_w"].T,
        "we1": np.concatenate([chunked(turned(a["L1_ffn_w1"])), chunked(turned(a["L1_ffn_w3"])),
                               chunked(turned(a["L1_ffn_w2"]))], axis=2),
        "sw1T": a["L1_ffn_sw1"].T, "sw2T": a["L1_ffn_sw2"].T,
    }
    arrays = {f"in_{k}": np.ascontiguousarray(v) for k, v in arrays.items()}
    nc = bacc.Bacc("TRN2", target_bir_lowering=False, num_devices=1)
    args = [nc.dram_tensor(k, v.shape, mybir.dt.from_np(v.dtype), kind="ExternalInput").ap() for k, v in arrays.items()]
    args.append(nc.dram_tensor("out", (N, D), F32, kind="ExternalOutput").ap())
    build(nc, *args)
    r = run_bass_kernel_spmd(nc, [arrays], core_ids=[0])
    return r.results[0]["out"]
```
